# Optimizing a Trainium2 kernel written in Bass

```python
import numpy as np
import jax
import jax.numpy as jnp

def _softmax(x, axis=-1):
    return jax.nn.softmax(x, axis=axis)

def _gelu(x):
    return jax.nn.gelu(x, approximate=True)

def _silu(x):
    return jax.nn.silu(x)

def _sigmoid(x):
    return jax.nn.sigmoid(x)

def _layernorm(x, axis=-1, eps=1e-05):
    m = jnp.mean(x, axis=axis, keepdims=True)
    v = jnp.var(x, axis=axis, keepdims=True)
    return (x - m) / jnp.sqrt(v + eps)

def _scatter_add(tgt, idx, src, axis=0):
    return tgt.at[idx].add(src)

def _segment_sum(src, seg, n):
    return jax.ops.segment_sum(src, seg, n)
kernel_name = 'mk_decoder_preln_d2_seqx_r8_3f9eea'

def setup_inputs(seed: int=0):
    np.random.seed(seed)
    _w = jnp.asarray

    def _rec_inputs():
        import jax
        import jax.numpy as jnp
        _rk = jax.random.key(seed)
        x = 7.22e-05 + 1 * jax.random.normal(jax.random.fold_in(_rk, 1), (1, 1024, 128), jnp.float32)
        _lenS = 1024 - jax.random.randint(jax.random.fold_in(_rk, 7), (1,), 0, max(1, 1024 // 4) + 1, jnp.int32)
        _lenS2 = 6404 - jax.random.randint(jax.random.fold_in(_rk, 8), (1,), 0, max(1, 6404 // 4) + 1, jnp.int32)
        _ctx_1024P = jax.random.normal(jax.random.fold_in(_rk, 11), (1, 16, 128), jnp.float32)
        _ctx_1024c = jax.random.dirichlet(jax.random.fold_in(_rk, 511), 0.3 * jnp.ones((16,), jnp.float32), (1, 6404))
        _ctx_1024t = jnp.einsum('bsk,bkd->bsd', _ctx_1024c, _ctx_1024P)
        _ctx_1024t = _ctx_1024t * jax.lax.rsqrt(jnp.mean(jnp.square(_ctx_1024t)) + 1e-12) * 0.953939
        ctx_1024 = 4.13588e-05 + 0.999923 * (_ctx_1024t + 0.3 * jax.random.normal(jax.random.fold_in(_rk, 611), (1, 6404, 128), jnp.float32))
        return (x, ctx_1024)
    x, ctx_1024 = _rec_inputs()

    def _L0_attn_setup():
        import jax, jax.numpy as jnp
        import numpy as np
        from math import sqrt
        DIM, RANK, NHEADS = (128, 64, 16)
        B, T = (2, 256)
        key = jax.random.key(seed)
        kx, kq, kk, kv = jax.random.split(key, 4)
        QK_a = sqrt(6.0 / (RANK + DIM))
        VO_a = sqrt(6.0 / (NHEADS * DIM + DIM))
        x = jax.random.normal(kx, (B, T, DIM), dtype=jnp.float32)
        Q = jax.random.uniform(kq, (NHEADS, RANK, DIM), jnp.float32, -QK_a, QK_a)
        K = jax.random.uniform(kk, (NHEADS, RANK, DIM), jnp.float32, -QK_a, QK_a)
        VO = jax.random.uniform(kv, (NHEADS, DIM, DIM), jnp.float32, -VO_a, VO_a)
        return {'x': x, 'Q': Q, 'K': K, 'VO': VO}
    _L0_attn_all = _L0_attn_setup()
    _L0_attn_in = {k: v for k, v in _L0_attn_all.items() if k in ('Q', 'K', 'VO')}
    del _L0_attn_all

    def _L0_xattn_setup():
        import jax, jax.numpy as jnp
        import numpy as np
        B, TQ, TK, DIM = (4, 256, 256, 128)
        key = jax.random.key(seed)
        k1, k2, k3, k4 = jax.random.split(key, 4)
        inputs = jax.random.normal(k1, (B, TQ, DIM), dtype=jnp.float32)
        context = jax.random.normal(k2, (B, TK, DIM), dtype=jnp.float32)
        scale = 1.0 / np.sqrt(DIM)
        Wg = jax.random.normal(k3, (DIM, DIM), dtype=jnp.float32) * scale
        bg = jnp.zeros((DIM,), dtype=jnp.float32)
        Wo = jax.random.normal(k4, (DIM, DIM), dtype=jnp.float32) * scale
        bo = jnp.zeros((DIM,), dtype=jnp.float32)
        return {'inputs': inputs, 'context': context, 'Wg': Wg, 'bg': bg, 'Wo': Wo, 'bo': bo}
    _L0_xattn_all = _L0_xattn_setup()
    _L0_xattn_in = {k: v for k, v in _L0_xattn_all.items() if k in ('Wg', 'bg', 'Wo', 'bo')}
    del _L0_xattn_all

    def _L0_ffn_setup():
        import jax, jax.numpy as jnp
        import numpy as np
        NUM_EXPERTS = 8
        TOP_K = 2
        B, T, D, F = (4, 256, 128, 352)
        key = jax.random.key(seed)
        ks = jax.random.split(key, 5)
        return {'x': jax.random.normal(ks[0], (B, T, D), dtype=jnp.float32), 'router_w': jax.random.normal(ks[1], (D, NUM_EXPERTS), dtype=jnp.float32) * 0.02, 'gate_proj': jax.random.normal(ks[2], (NUM_EXPERTS, D, F), dtype=jnp.float32) * 0.02, 'up_proj': jax.random.normal(ks[3], (NUM_EXPERTS, D, F), dtype=jnp.float32) * 0.02, 'down_proj': jax.random.normal(ks[4], (NUM_EXPERTS, F, D), dtype=jnp.float32) * 0.02}
    _L0_ffn_all = _L0_ffn_setup()
    _L0_ffn_in = {k: v for k, v in _L0_ffn_all.items() if k in ('router_w', 'gate_proj', 'up_proj', 'down_proj')}
    del _L0_ffn_all

    def _L1_attn_setup():
        import math
        import jax, jax.numpy as jnp
        import numpy as np
        B, L, D_MODEL = (2, 256, 128)
        N_HEAD, HEAD_DIM = (16, 64)
        ATT_SCALE = 1.0
        key = jax.random.key(seed)
        ks = jax.random.split(key, 6)
        HD = N_HEAD * HEAD_DIM

        def xavier(k, fan_in, fan_out):
            lim = math.sqrt(6.0 / (fan_in + fan_out))
            return jax.random.uniform(k, (fan_in, fan_out), jnp.float32, -lim, lim)
        return {'x': jax.random.normal(ks[0], (B, L, D_MODEL), jnp.float32), 'Wq': xavier(ks[1], D_MODEL, HD), 'bq': jnp.zeros((HD,), jnp.float32), 'Wk': xavier(ks[2], D_MODEL, HD), 'bk': jnp.zeros((HD,), jnp.float32), 'Wv': xavier(ks[3], D_MODEL, HD), 'bv': jnp.zeros((HD,), jnp.float32), 'Wo': xavier(ks[4], HD, D_MODEL), 'bo': jax.random.uniform(ks[5], (D_MODEL,), jnp.float32, -1.0 / math.sqrt(HD), 1.0 / math.sqrt(HD))}
    _L1_attn_all = _L1_attn_setup()
    _L1_attn_in = {k: v for k, v in _L1_attn_all.items() if k in ('Wq', 'bq', 'Wk', 'bk', 'Wv', 'bv', 'Wo', 'bo')}
    del _L1_attn_all

    def _L1_xattn_setup():
        import jax, jax.numpy as jnp
        import numpy as np
        B, S, E, H = (2, 256, 128, 16)
        D = E // H
        key = jax.random.key(seed)
        ks = jax.random.split(key, 7)
        return {'query': jax.random.normal(ks[0], (B, S, E), dtype=jnp.float32), 'key': jax.random.normal(ks[1], (B, S, E), dtype=jnp.float32), 'value': jax.random.normal(ks[2], (B, S, E), dtype=jnp.float32), 'Wq': jax.random.normal(ks[3], (E, E), dtype=jnp.float32) * E ** (-0.5), 'Wk': jax.random.normal(ks[4], (E, E), dtype=jnp.float32) * E ** (-0.5), 'Wv': jax.random.normal(ks[5], (E, E), dtype=jnp.float32) * E ** (-0.5), 'Wo': jax.random.normal(ks[6], (E, E), dtype=jnp.float32) * E ** (-0.5)}
    _L1_xattn_all = _L1_xattn_setup()
    _L1_xattn_in = {k: v for k, v in _L1_xattn_all.items() if k in ('Wq', 'Wk', 'Wv', 'Wo')}
    del _L1_xattn_all

    def _L1_ffn_setup():
        import jax, jax.numpy as jnp
        import numpy as np
        EPS = 1e-05

        def rmsnorm(x):
            var = jnp.mean(jnp.square(x), axis=-1, keepdims=True)
            return x * jax.lax.rsqrt(var + 1e-06)

        def activation_quant(x):
            scale = 127.0 / jnp.clip(jnp.max(jnp.abs(x), axis=-1, keepdims=True), EPS, None)
            return jnp.clip(jnp.round(x * scale), -128, 127) / scale

        def weight_quant(w):
            scale = 1.0 / jnp.clip(jnp.mean(jnp.abs(w)), EPS, None)
            return jnp.clip(jnp.round(w * scale), -1, 1) / scale

        def bitlinear(x, w, b):
            xn = rmsnorm(x)
            xq = xn + jax.lax.stop_gradient(activation_quant(xn) - xn)
            wq = w + jax.lax.stop_gradient(weight_quant(w) - w)
            return jnp.einsum('bsi,oi->bso', xq, wq) + b
        key = jax.random.key(seed)
        k1, k2, k3 = jax.random.split(key, 3)
        B, S, D, H = (4, 256, 128, 512)
        x = jax.random.normal(k1, (B, S, D), dtype=jnp.float32)
        w1 = jax.random.normal(k2, (H, D), dtype=jnp.float32) * D ** (-0.5)
        b1 = jnp.zeros((H,), dtype=jnp.float32)
        w2 = jax.random.normal(k3, (D, H), dtype=jnp.float32) * H ** (-0.5)
        b2 = jnp.zeros((D,), dtype=jnp.float32)
        return {'x': x, 'w1': w1, 'b1': b1, 'w2': w2, 'b2': b2}
    _L1_ffn_all = _L1_ffn_setup()
    _L1_ffn_in = {k: v for k, v in _L1_ffn_all.items() if k in ('w1', 'b1', 'w2', 'b2')}
    del _L1_ffn_all
    return {'x': x, 'ctx_1024': ctx_1024, 'L0_attn_Q': _L0_attn_in['Q'], 'L0_attn_K': _L0_attn_in['K'], 'L0_attn_VO': _L0_attn_in['VO'], 'L0_xattn_Wg': _L0_xattn_in['Wg'], 'L0_xattn_bg': _L0_xattn_in['bg'], 'L0_xattn_Wo': _L0_xattn_in['Wo'], 'L0_xattn_bo': _L0_xattn_in['bo'], 'L0_ffn_router_w': _L0_ffn_in['router_w'], 'L0_ffn_gate_proj': _L0_ffn_in['gate_proj'], 'L0_ffn_up_proj': _L0_ffn_in['up_proj'], 'L0_ffn_down_proj': _L0_ffn_in['down_proj'], 'L1_attn_Wq': _L1_attn_in['Wq'], 'L1_attn_bq': _L1_attn_in['bq'], 'L1_attn_Wk': _L1_attn_in['Wk'], 'L1_attn_bk': _L1_attn_in['bk'], 'L1_attn_Wv': _L1_attn_in['Wv'], 'L1_attn_bv': _L1_attn_in['bv'], 'L1_attn_Wo': _L1_attn_in['Wo'], 'L1_attn_bo': _L1_attn_in['bo'], 'L1_xattn_Wq': _L1_xattn_in['Wq'], 'L1_xattn_Wk': _L1_xattn_in['Wk'], 'L1_xattn_Wv': _L1_xattn_in['Wv'], 'L1_xattn_Wo': _L1_xattn_in['Wo'], 'L1_ffn_w1': _L1_ffn_in['w1'], 'L1_ffn_b1': _L1_ffn_in['b1'], 'L1_ffn_w2': _L1_ffn_in['w2'], 'L1_ffn_b2': _L1_ffn_in['b2']}

def reference(x, ctx_1024, L0_attn_Q, L0_attn_K, L0_attn_VO, L0_xattn_Wg, L0_xattn_bg, L0_xattn_Wo, L0_xattn_bo, L0_ffn_router_w, L0_ffn_gate_proj, L0_ffn_up_proj, L0_ffn_down_proj, L1_attn_Wq, L1_attn_bq, L1_attn_Wk, L1_attn_bk, L1_attn_Wv, L1_attn_bv, L1_attn_Wo, L1_attn_bo, L1_xattn_Wq, L1_xattn_Wk, L1_xattn_Wv, L1_xattn_Wo, L1_ffn_w1, L1_ffn_b1, L1_ffn_w2, L1_ffn_b2):
    import jax
    import jax.numpy as jnp

    def _L0_attn_ref(x, Q, K, VO):
        import jax, jax.numpy as jnp
        import numpy as np
        from math import sqrt
        DIM, RANK, NHEADS = (128, 64, 16)
        B, T = (2, 256)
        dim = x.shape[-1]
        xq = jnp.einsum('btd,hrd->bthr', x, Q)
        xk = jnp.einsum('bud,hrd->buhr', x, K)
        scores = jnp.einsum('bthr,buhr->bthu', xq, xk) / sqrt(dim)
        attn = jax.nn.softmax(scores, axis=3)
        return jnp.einsum('bthu,bud,hde->bte', attn, x, VO)

    def _L0_xattn_ref(inputs, context, Wg, bg, Wo, bo):
        import jax, jax.numpy as jnp
        import numpy as np
        B, TQ, TK, DIM = (4, 256, 256, 128)
        gate_signal = jnp.einsum('bkd,de->bke', context, Wg) + bg
        attn = jnp.einsum('bkd,bqd->bkq', gate_signal, inputs)
        attn = jax.nn.softmax(attn, axis=1)
        out = jnp.einsum('bkq,bkd->bqd', attn, context)
        return jnp.einsum('bqd,de->bqe', out, Wo) + bo

    def _L0_ffn_ref(x, router_w, gate_proj, up_proj, down_proj):
        import jax, jax.numpy as jnp
        import numpy as np
        NUM_EXPERTS = 8
        TOP_K = 2
        B, T, D, F = (4, 256, 128, 352)
        scores = jnp.einsum('btd,de->bte', x, router_w).astype(jnp.float32)
        probs = jax.nn.softmax(scores, axis=-1)
        routing_weights, routing_idx = jax.lax.top_k(probs, TOP_K)
        routing_weights = (routing_weights / jnp.sum(routing_weights, axis=-1, keepdims=True)).astype(x.dtype)
        one_hot = jax.nn.one_hot(routing_idx, NUM_EXPERTS, dtype=x.dtype)
        expert_w = jnp.einsum('btke,btk->bte', one_hot, routing_weights)
        dispatched = jnp.einsum('btd,btke->bted', x, one_hot)
        gate = jnp.einsum('bted,edf->btef', dispatched, gate_proj)
        up = jnp.einsum('bted,edf->btef', dispatched, up_proj)
        acts = jax.nn.silu(gate) * up
        expert_out = jnp.einsum('btef,efd->bted', acts, down_proj)
        return jnp.einsum('bted,bte->btd', expert_out, expert_w)

    def _L1_attn_ref(x, Wq, bq, Wk, bk, Wv, bv, Wo, bo):
        import math
        import jax, jax.numpy as jnp
        import numpy as np
        B, L, D_MODEL = (2, 256, 128)
        N_HEAD, HEAD_DIM = (16, 64)
        ATT_SCALE = 1.0
        b, l, _ = x.shape
        q = (x @ Wq + bq).reshape(b, l, N_HEAD, HEAD_DIM)
        k = (x @ Wk + bk).reshape(b, l, N_HEAD, HEAD_DIM)
        v = (x @ Wv + bv).reshape(b, l, N_HEAD, HEAD_DIM)
        scale = 1.0 / math.sqrt(HEAD_DIM ** ATT_SCALE)
        scores = jnp.einsum('blhd,bmhd->bhlm', q, k) * scale
        attn = jnp.einsum('bhlm,bmhd->blhd', scores, v)
        out = attn.reshape(b, l, N_HEAD * HEAD_DIM) @ Wo + bo
        return out

    def _L1_xattn_ref(query, key, value, Wq, Wk, Wv, Wo):
        import jax, jax.numpy as jnp
        import numpy as np
        B, S, E, H = (2, 256, 128, 16)
        D = E // H
        emb_dim = query.shape[-1]
        h = H
        d = emb_dim // h
        q = query @ Wq.T
        k = key @ Wk.T
        v = value @ Wv.T

        def split_heads(x):
            b, s, e = x.shape
            return x.reshape(b, s, h, d).transpose(0, 2, 1, 3)
        q = split_heads(q)
        k = split_heads(k)
        v = split_heads(v)
        scale = emb_dim ** (-0.5)
        scores = jnp.einsum('bhsd,bhtd->bhst', q * scale, k)
        weights = jax.nn.softmax(scores, axis=-1)
        heads = jnp.einsum('bhst,bhtd->bhsd', weights, v)
        b = heads.shape[0]
        out = heads.transpose(0, 2, 1, 3).reshape(b, -1, emb_dim)
        return out @ Wo.T

    def _L1_ffn_ref(x, w1, b1, w2, b2):
        import jax, jax.numpy as jnp
        import numpy as np
        EPS = 1e-05

        def rmsnorm(x):
            var = jnp.mean(jnp.square(x), axis=-1, keepdims=True)
            return x * jax.lax.rsqrt(var + 1e-06)

        def activation_quant(x):
            scale = 127.0 / jnp.clip(jnp.max(jnp.abs(x), axis=-1, keepdims=True), EPS, None)
            return jnp.clip(jnp.round(x * scale), -128, 127) / scale

        def weight_quant(w):
            scale = 1.0 / jnp.clip(jnp.mean(jnp.abs(w)), EPS, None)
            return jnp.clip(jnp.round(w * scale), -1, 1) / scale

        def bitlinear(x, w, b):
            xn = rmsnorm(x)
            xq = xn + jax.lax.stop_gradient(activation_quant(xn) - xn)
            wq = w + jax.lax.stop_gradient(weight_quant(w) - w)
            return jnp.einsum('bsi,oi->bso', xq, wq) + b
        h = bitlinear(x, w1, b1)
        h = jax.nn.gelu(h, approximate=False)
        return bitlinear(h, w2, b2)
    x = x + _L0_attn_ref(_layernorm(x, axis=-1), L0_attn_Q, L0_attn_K, L0_attn_VO)
    x = x + _L0_xattn_ref(_layernorm(x, axis=-1), ctx_1024, L0_xattn_Wg, L0_xattn_bg, L0_xattn_Wo, L0_xattn_bo)
    x = x + _L0_ffn_ref(_layernorm(x, axis=-1), L0_ffn_router_w, L0_ffn_gate_proj, L0_ffn_up_proj, L0_ffn_down_proj)
    x = x + _L1_attn_ref(_layernorm(x, axis=-1), L1_attn_Wq, L1_attn_bq, L1_attn_Wk, L1_attn_bk, L1_attn_Wv, L1_attn_bv, L1_attn_Wo, L1_attn_bo)
    x = x + _L1_xattn_ref(_layernorm(x, axis=-1), ctx_1024, ctx_1024, L1_xattn_Wq, L1_xattn_Wk, L1_xattn_Wv, L1_xattn_Wo)
    x = x + _L1_ffn_ref(_layernorm(x, axis=-1), L1_ffn_w1, L1_ffn_b1, L1_ffn_w2, L1_ffn_b2)
    return x

_drawn_inputs = setup_inputs


def setup_inputs(seed=0):
    import zlib

    import numpy as np

    out = dict(_drawn_inputs(seed))
    spreads = {'L0_xattn_bg': (0.0, 2.0),
     'L0_xattn_bo': (0.0, 0.1),
     'L1_attn_bq': (0.0, 0.1),
     'L1_attn_bk': (0.0, 0.1),
     'L1_attn_bv': (0.0, 0.1),
     'L1_ffn_b1': (0.0, 2.0),
     'L1_ffn_b2': (0.0, 0.8)}
    factors = {'L0_ffn_router_w': 8.0,
     'L0_ffn_gate_proj': 8.0,
     'L0_ffn_up_proj': 8.0,
     'L0_ffn_down_proj': 8.0,
     'L1_attn_bo': 24.986,
     'L1_xattn_Wq': 8.0,
     'L1_xattn_Wk': 8.0,
     'L1_xattn_Wv': 3.322,
     'L1_xattn_Wo': 3.772,
     'L1_ffn_w1': 7.672}
    for name, (base, spread) in spreads.items():
        noise = np.random.default_rng([zlib.crc32(name.encode()), seed]).standard_normal(out[name].shape)
        drawn = base * np.exp(spread * noise) if base else spread * noise
        out[name] = jnp.asarray(drawn.astype(out[name].dtype))
    for name, factor in factors.items():
        out[name] = (out[name] * factor).astype(out[name].dtype)
    return out
```

```python
from contextlib import ExitStack

import concourse.bass as bass
from concourse import mybir

F32 = mybir.dt.float32
F32R = mybir.dt.float32r
BF16 = mybir.dt.bfloat16
U32 = mybir.dt.uint32
ALU = mybir.AluOpType
ACT = mybir.ActivationFunctionType
AX = mybir.AxisListType.X

P = 128
BANK = 512
T = 1024
D = 128
TT = T // P
S = 6404
KT = -(-S // P)
HEADS = 16
LN_EPS = 1e-5


class Phase:

    def __init__(self, nc, sems, prefix):
        self.nc, self.sems, self.prefix = nc, sems, prefix
        self.stack = ExitStack()

    def __enter__(self):
        self.stack.__enter__()
        return self

    def __exit__(self, *exc):
        return self.stack.__exit__(*exc)

    def sb(self, name, shape, dtype=F32):
        return self.stack.enter_context(self.nc.sbuf_tensor(f"{self.prefix}_{name}", shape, dtype))

    def ps(self, name, shape):
        return self.stack.enter_context(self.nc.psum_tensor(f"{self.prefix}_{name}", shape, F32))

    def sem(self, name):
        return self.sems.enter_context(self.nc.semaphore(f"{self.prefix}_{name}"))

    def block(self):
        return self.nc.Block()


class Chain:

    def __init__(self, engine, sem, count=0):
        self.engine, self.sem, self.count = engine, sem, count

    def __call__(self, instruction):
        self.count += 1
        instruction.then_inc(self.sem, 1)
        self.engine.wait_ge(self.sem, self.count)


NORM_SEMS = ("chain", "var_ready", "std_ready", "normed_ready", "turned_ready")
NORM_STEPS = 10


def layernorm(nc, norm_sems, n, x_res, ident, xn_t, xn_tok=None):
    chain_sem, var_ready, std_ready, normed_ready, turned_ready = norm_sems
    with Phase(nc, None, f"norm{n}") as ph:
        centred = ph.sb("centred", [P, TT, D])
        squares = ph.sb("squares", [P, TT, D])
        normed = xn_tok if xn_tok is not None else ph.sb("normed", [P, TT, D])
        total = ph.sb("total", [P, TT])
        mean = ph.sb("mean", [P, TT])
        sum_sq = ph.sb("sum_sq", [P, TT])
        var = ph.sb("var", [P, TT])
        std = ph.sb("std", [P, TT])
        rstd = ph.sb("rstd", [P, TT])
        newton = ph.sb("newton", [P, TT])
        newton2 = ph.sb("newton2", [P, TT])
        newton3 = ph.sb("newton3", [P, TT])
        rstd2 = ph.sb("rstd2", [P, TT])
        turned = [ph.ps(f"turned{b}", [P, BANK]) for b in range(2)]

        def wide(stat):
            return stat[:, :].unsqueeze(2).to_broadcast([P, TT, D])

        with ph.block() as block:

            @block.vector
            def _(dve):
                step = Chain(dve, chain_sem, n * NORM_STEPS)
                step(nc.vector.tensor_reduce(total[:, :], x_res[:, :, :], AX, ALU.add))
                step(nc.vector.tensor_scalar(mean[:, :], total[:, :], 1.0 / D, None, ALU.mult))
                step(nc.vector.tensor_tensor(centred[:, :, :], x_res[:, :, :], wide(mean), ALU.subtract))
                step(nc.vector.tensor_tensor(squares[:, :, :], centred[:, :, :], centred[:, :, :], ALU.mult))
                step(nc.vector.tensor_reduce(sum_sq[:, :], squares[:, :, :], AX, ALU.add))
                nc.vector.tensor_scalar(var[:, :], sum_sq[:, :], 1.0 / D, LN_EPS, ALU.mult, ALU.add)\
                    .then_inc(var_ready, 1)
                dve.wait_ge(std_ready, n + 1)
                step(nc.vector.reciprocal(rstd[:, :], std[:, :]))
                step(nc.vector.tensor_tensor(newton[:, :], rstd[:, :], rstd[:, :], ALU.mult))
                step(nc.vector.tensor_tensor(newton2[:, :], newton[:, :], var[:, :], ALU.mult))
                step(nc.vector.tensor_scalar(newton3[:, :], newton2[:, :], -0.5, 1.5, ALU.mult, ALU.add))
                step(nc.vector.tensor_tensor(rstd2[:, :], rstd[:, :], newton3[:, :], ALU.mult))
                nc.vector.tensor_tensor(normed[:, :, :], centred[:, :, :], wide(rstd2), ALU.mult)\
                    .then_inc(normed_ready, 1)
                dve.wait_ge(turned_ready, n * 2 + 1)
                assert step.count == (n + 1) * NORM_STEPS
                nc.vector.tensor_copy(xn_t[:, 0:BANK], turned[0][:, :])

            @block.scalar
            def _(act):
                act.wait_ge(var_ready, n + 1)
                nc.scalar.activation(std[:, :], var[:, :], ACT.Sqrt).then_inc(std_ready, 1)
                act.wait_ge(turned_ready, n * 2 + 2)
                nc.scalar.activation(xn_t[:, BANK:T], turned[1][:, :], ACT.Copy)

            @block.tensor
            def _(pe):
                pe.wait_ge(normed_ready, n + 1)
                for i in range(TT):
                    turn = nc.tensor.transpose(turned[i // 4][:, i % 4 * P:(i % 4 + 1) * P],
                                               normed[:, i, :], ident[:, :])
                    if i % 4 == 3:
                        turn.then_inc(turned_ready, 1)


def self_attention_0(nc, sems, x_res, xn_t, ident, masks, w_heads):
    scale = float(D) ** -0.5
    with Phase(nc, sems, "sa0") as ph:
        w = [ph.sb(f"w{b}", [P, 3 * P]) for b in range(2)]
        q_round = ph.sb("q_round", [P, BANK], F32R)
        q_stack = [ph.sb(f"q_stack{b}", [P, T], F32R) for b in range(2)]
        k_hi = [ph.sb(f"k_hi{b}", [P, T], F32R) for b in range(2)]
        k_lo = [ph.sb(f"k_lo{b}", [P, T], F32R) for b in range(2)]
        values = [ph.sb(f"values{b}", [P, TT, D]) for b in range(2)]
        probs = [ph.sb(f"probs{b}", [P, T]) for b in range(2)]
        probs_t = ph.sb("probs_t", [P, T])
        neg_max = [ph.sb(f"neg_max{b}", [P, 1]) for b in range(2)]
        den = [ph.sb(f"den{b}", [P, 1]) for b in range(2)]
        inv_den = [ph.sb(f"inv_den{b}", [P, 1]) for b in range(2)]
        ps_scores = [ph.ps(f"ps_scores{b}", [P, T]) for b in range(2)]
        ps_turn = [ph.ps(f"ps_turn{b}", [P, BANK]) for b in range(2)]
        ps_out = ph.ps("ps_out", [P, D])
        ps_prep = ph.ps("ps_prep", [P, BANK])
        w_loaded = [ph.sem(f"w_loaded{b}") for b in range(2)]
        prep_ready = ph.sem("prep_ready")
        prep_rounded = ph.sem("prep_rounded")
        prep_done = ph.sem("prep_done")
        scores_ready = ph.sem("scores_ready")
        max_ready = ph.sem("max_ready")
        exp_done = ph.sem("exp_done")
        turned = [ph.sem(f"turned{b}") for b in range(2)]
        probs_t_ready = [ph.sem(f"probs_t_ready{b}") for b in range(2)]
        inv_ready = ph.sem("inv_ready")
        pv_done = ph.sem("pv_done")
        out_added = ph.sem("out_added")

        PIECES = 6
        PAIRS = HEADS // 2

        def rounds(u):
            return u % TT, u // TT

        with ph.block() as block:

            @block.sync
            def _(sp):
                for h in range(2):
                    sp.dma_start(w[h][:, :], w_heads[h]).then_inc(w_loaded[h], 16)
                with sp.Fori(1, PAIRS) as i:
                    for b in range(2):
                        sp.wait_ge(prep_done, i * (2 * PIECES) + PIECES * (b - 1))
                        sp.dma_start(w[b][:, :], w_heads[bass.ds(i * 2 + b, 1)].rearrange("a d n -> (a d) n"))\
                            .then_inc(w_loaded[b], 16)

            @block.tensor
            def _(pe):
                def piece(k, slot, count):
                    pe.wait_ge(prep_done, count + k)
                    if k < 4:
                        half = k % 2 * BANK
                        nc.tensor.matmul(ps_prep[:, :], w[slot][:, k // 2 * P:(k // 2 + 1) * P],
                                         xn_t[:, half:half + BANK], start=True, stop=True)\
                            .then_inc(prep_ready, 1)
                    else:
                        for j in range(4):
                            ut = (k - 4) * 4 + j
                            last = nc.tensor.matmul(ps_prep[:, j * P:(j + 1) * P], xn_t[:, ut * P:(ut + 1) * P],
                                                    w[slot][:, 2 * P:3 * P], start=True, stop=True)
                        last.then_inc(prep_ready, 1)

                def scores(n, u, first=False):
                    q, slot = rounds(u % (2 * TT))
                    if not first:
                        pe.wait_ge(exp_done, n - 1)
                    buf = ps_scores[u % 2]
                    for half in range(2):
                        cut = slice(half * BANK, (half + 1) * BANK)
                        for m, keys in enumerate((k_hi, k_lo)):
                            last = nc.tensor.matmul(buf[:, cut], q_stack[slot][:, q * P:(q + 1) * P],
                                                    keys[slot][:, cut], start=(m == 0), stop=(m == 1))
                    last.then_inc(scores_ready, 1)

                def turn(n, u):
                    pe.wait_ge(exp_done, n + 1)
                    for j in range(TT):
                        if j % 4 == 0:
                            pe.wait_ge(probs_t_ready[j // 4], n)
                        last = nc.tensor.transpose(ps_turn[j // 4][:, j % 4 * P:(j % 4 + 1) * P],
                                                   probs[u % 2][:, j * P:(j + 1) * P], ident[:, :])
                        if j % 4 == 3:
                            last.then_inc(turned[j // 4], 1)

                def times_values(n, u):
                    slot = u // TT
                    pe.wait_ge(out_added, n)
                    for j in range(TT):
                        if j % 4 == 0:
                            pe.wait_ge(probs_t_ready[j // 4], n + 1)
                        last = nc.tensor.matmul(ps_out[:, :], probs_t[:, j * P:(j + 1) * P], values[slot][:, j, :],
                                                start=(j == 0), stop=(j == TT - 1))
                    last.then_inc(pv_done, 1)

                def pair(i, final):
                    for u in range(2 * TT):
                        n = i * (2 * TT) + u
                        turn(n, u)
                        if not (final and u + 2 >= 2 * TT):
                            if u in (TT - 2, 2 * TT - 2):
                                pe.wait_ge(prep_done, i * (2 * PIECES) + PIECES * (u // TT + 1) + 4)
                            scores(n + 2, u + 2)
                        if u % TT < PIECES and not (final and u >= TT):
                            if u == 0:
                                pe.wait_ge(w_loaded[1], i * 16 + 16)
                            if u == TT:
                                pe.wait_ge(w_loaded[0], i * 16 + 32)
                            piece(u % TT, 1 - u // TT, i * (2 * PIECES) + PIECES * (u // TT + 1))
                        times_values(n, u)

                pe.wait_ge(w_loaded[0], 16)
                for k in range(PIECES):
                    if k == 0:
                        nc.tensor.matmul(ps_prep[:, :], w[0][:, 0:P], xn_t[:, 0:BANK], start=True, stop=True)\
                            .then_inc(prep_ready, 1)
                    else:
                        piece(k, 0, 0)
                pe.wait_ge(prep_done, 4)
                scores(0, 0, first=True)
                scores(1, 1, first=True)
                pe.wait_ge(prep_done, PIECES)
                with pe.Fori(0, PAIRS - 1) as i:
                    pair(i, False)
                pair(PAIRS - 1, True)

            @block.scalar
            def _(act):
                def exp(n, u):
                    act.wait_ge(max_ready, n + 1)
                    nc.scalar.activation(probs[u % 2][:, :], ps_scores[u % 2][:, :], ACT.Exp,
                                         bias=neg_max[u % 2][:, :], accum_out=den[u % 2][:, :])\
                        .then_inc(exp_done, 1)

                def round_piece(k, slot, count):
                    act.wait_ge(prep_ready, count + k + 1)
                    half = slice(k % 2 * BANK, (k % 2 + 1) * BANK)
                    if k < 2:
                        nc.scalar.activation(q_round[:, :], ps_prep[:, :], ACT.Copy).then_inc(prep_rounded, 1)
                    else:
                        nc.scalar.activation(k_hi[slot][:, half], ps_prep[:, :], ACT.Copy, scale=scale)\
                            .then_inc(prep_rounded, 1)

                def pair(i, final):
                    for u in range(2 * TT):
                        n = i * (2 * TT) + u
                        act.wait_ge(turned[1], n + 1)
                        nc.scalar.activation(probs_t[:, BANK:T], ps_turn[1][:, :], ACT.Copy)\
                            .then_inc(probs_t_ready[1], 1)
                        if u % TT < 4 and not (final and u >= TT):
                            round_piece(u % TT, 1 - u // TT, i * (2 * PIECES) + PIECES * (u // TT + 1))
                        if not (final and u + 2 >= 2 * TT):
                            exp(n + 2, u + 2)

                for k in range(4):
                    round_piece(k, 0, 0)
                exp(0, 0)
                exp(1, 1)
                with act.Fori(0, PAIRS - 1) as i:
                    pair(i, False)
                pair(PAIRS - 1, True)

            @block.vector
            def _(dve):
                def top(n, u):
                    dve.wait_ge(scores_ready, n + 1)
                    nc.vector.tensor_reduce(neg_max[u % 2][:, :], ps_scores[u % 2][:, :], AX, ALU.max, negate=True)\
                        .then_inc(max_ready, 1)

                def rest_piece(k, slot, rounded, ready):
                    half = slice(k % 2 * BANK, (k % 2 + 1) * BANK)
                    if k < 4:
                        dve.wait_ge(prep_rounded, rounded + k + 1)
                    else:
                        dve.wait_ge(prep_ready, ready + k + 1)
                    if k < 2:
                        out = nc.vector.scalar_tensor_tensor(
                            q_stack[slot][:, half], q_round[:, :].bitcast(F32), masks[:, 0:1], ps_prep[:, :],
                            ALU.mult, ALU.add)
                    elif k < 4:
                        out = nc.vector.scalar_tensor_tensor(
                            k_lo[slot][:, half], ps_prep[:, :], scale, k_hi[slot][:, half].bitcast(F32),
                            ALU.mult, ALU.subtract)
                    else:
                        ut = (k - 4) * 4
                        out = nc.vector.tensor_copy(values[slot][:, ut:ut + 4, :],
                                                    ps_prep[:, :].rearrange("p (a d) -> p a d", a=4))
                    out.then_inc(prep_done, 1)

                def pair(i, final):
                    for u in range(2 * TT):
                        n = i * (2 * TT) + u
                        dve.wait_ge(turned[0], n + 1)
                        nc.vector.tensor_copy(probs_t[:, 0:BANK], ps_turn[0][:, :]).then_inc(probs_t_ready[0], 1)
                        nc.vector.reciprocal(inv_den[u % 2][:, :], den[u % 2][:, :]).then_inc(inv_ready, 1)
                        if not (final and u + 2 >= 2 * TT):
                            top(n + 2, u + 2)
                        if u % TT < PIECES and not (final and u >= TT):
                            rest_piece(u % TT, 1 - u // TT, i * 8 + 4 * (u // TT + 1),
                                       i * (2 * PIECES) + PIECES * (u // TT + 1))
                        dve.wait_ge(pv_done, n + 1)
                        dve.wait_ge(inv_ready, n + 1)
                        nc.vector.scalar_tensor_tensor(x_res[:, u % TT, :], ps_out[:, :], inv_den[u % 2][:, :],
                                                       x_res[:, u % TT, :], ALU.mult, ALU.add)\
                            .then_inc(out_added, 1)

                for k in range(PIECES):
                    rest_piece(k, 0, 0, 0)
                top(0, 0)
                top(1, 1)
                with dve.Fori(0, PAIRS - 1) as i:
                    pair(i, False)
                pair(PAIRS - 1, True)


def cross_attention_0(nc, sems, x_res, xn_t, ident, ones, ctx_t, ctx_tok, ctx_loaded, ctx_tok_loaded, ins):
    CHUNKS = -(-S // BANK)
    TAIL = S - (CHUNKS - 1) * BANK
    TAIL_TILES = -(-TAIL // P)
    with Phase(nc, sems, "ca0") as ph:
        w_gate = ph.sb("w_gate", [P, D])
        b_gate = ph.sb("b_gate", [P, 1])
        w_out = ph.sb("w_out", [P, D])
        b_out = ph.sb("b_out", [1, D])
        gate_hi = ph.sb("gate_hi", [P, S], F32R)
        gate_lo = ph.sb("gate_lo", [P, S], F32R)
        xn_hi = ph.sb("xn_hi", [P, T], F32R)
        xn_lo = ph.sb("xn_lo", [P, T], F32R)
        q_hi = ph.sb("q_hi", [P, P], F32R)
        q_lo = ph.sb("q_lo", [P, P], F32R)
        scores = ph.sb("scores", [P, S])
        probs = [ph.sb(f"probs{b}", [P, BANK]) for b in range(2)]
        probs_tail = ph.sb("probs_tail", [P, TAIL_TILES * P])
        probs_t = [ph.sb(f"probs_t{b}", [P, BANK]) for b in range(2)]
        chunk_max = ph.sb("chunk_max", [P, CHUNKS])
        chunk_den = ph.sb("chunk_den", [P, CHUNKS])
        neg_max = ph.sb("neg_max", [P, 1])
        den = ph.sb("den", [P, 1])
        inv_den = ph.sb("inv_den", [P, 1])
        attended = ph.sb("attended", [P, TT, D])
        attended_t = ph.sb("attended_t", [P, T])
        ps_scores = [ph.ps(f"ps_scores{b}", [P, BANK]) for b in range(2)]
        ps_turn = [ph.ps(f"ps_turn{b}", [P, BANK]) for b in range(2)]
        ps_out = ph.ps("ps_out", [P, D])
        ps_proj = [ph.ps(f"ps_proj{b}", [P, BANK]) for b in range(2)]
        loaded = ph.sem("loaded")
        gate_ready = ph.sem("gate_ready")
        gate_rounded = ph.sem("gate_rounded")
        gate_done = ph.sem("gate_done")
        split_hi = ph.sem("split_hi")
        split_done = ph.sem("split_done")
        tail_cleared = ph.sem("tail_cleared")
        q_ready = ph.sem("q_ready")
        scores_ready = ph.sem("scores_ready")
        scores_kept = ph.sem("scores_kept")
        chunk_max_ready = ph.sem("chunk_max_ready")
        max_ready = ph.sem("max_ready")
        exp_done = ph.sem("exp_done")
        turned = ph.sem("turned")
        probs_t_ready = ph.sem("probs_t_ready")
        pv_done = ph.sem("pv_done")
        den_ready = ph.sem("den_ready")
        inv_ready = ph.sem("inv_ready")
        attended_ready = ph.sem("attended_ready")
        out_turned = ph.sem("out_turned")
        attended_t_ready = [ph.sem(f"attended_t_ready{b}") for b in range(2)]
        projected = ph.sem("projected")

        def width(c):
            return BANK if c < CHUNKS - 1 else TAIL

        def prob_tile(c):
            return probs[c % 2] if c < CHUNKS - 1 else probs_tail

        def tiles(c):
            return 4 if c < CHUNKS - 1 else TAIL_TILES

        with ph.block() as block:

            @block.sync
            def _(sp):
                sp.dma_start(w_gate[:, :], ins["w_gate"]).then_inc(loaded, 16)
                sp.dma_start(b_gate[:, :], ins["b_gate"]).then_inc(loaded, 16)
                sp.dma_start(w_out[:, :], ins["w_ca0_out"]).then_inc(loaded, 16)
                sp.dma_start(b_out[:, :], ins["b_ca0_out"]).then_inc(loaded, 16)

            @block.tensor
            def _(pe):
                def gate(n, b, at, w):
                    nc.tensor.matmul(ps_scores[b][:, 0:w], w_gate[:, :], ctx_t[:, at], start=True, stop=True)\
                        .then_inc(gate_ready, 1)

                def score(t, c, first=False):
                    if c == 0:
                        pe.wait_ge(q_ready, t + 1)
                    if c != 1 and not (first and c < 2):
                        pe.wait_ge(scores_kept, t * CHUNKS + (c - 1 if c else 0))
                    w, at = width(c), slice(c * BANK, c * BANK + width(c))
                    for m, (q, g) in enumerate(((q_hi, gate_hi), (q_hi, gate_lo), (q_lo, gate_hi))):
                        last = nc.tensor.matmul(ps_scores[c % 2][:, 0:w], q[:, :], g[:, at],
                                                start=(m == 0), stop=(m == 2))
                    last.then_inc(scores_ready, 1)

                def turn(t, c):
                    pe.wait_ge(exp_done, t * CHUNKS + c + 1)
                    if c != 1:
                        pe.wait_ge(probs_t_ready, t * CHUNKS + (c - 1 if c else 0))
                    for j in range(tiles(c)):
                        last = nc.tensor.transpose(ps_turn[c % 2][:, j * P:(j + 1) * P],
                                                   prob_tile(c)[:, j * P:(j + 1) * P], ident[:, :])
                    last.then_inc(turned, 1)

                def times_context(t, c):
                    pe.wait_ge(probs_t_ready, t * CHUNKS + c + 1)
                    if c == 0:
                        pe.wait_ge(attended_ready, t)
                    for j in range(tiles(c)):
                        last = nc.tensor.matmul(ps_out[:, :], probs_t[c % 2][:, j * P:(j + 1) * P],
                                                ctx_tok[:, c * 4 + j, :], start=(c == 0 and j == 0),
                                                stop=(c == CHUNKS - 1 and j == TAIL_TILES - 1))
                    if c == CHUNKS - 1:
                        last.then_inc(pv_done, 1)

                pe.wait_ge(loaded, 64)
                pe.wait_ge(ctx_loaded, 16)
                pe.wait_ge(ctx_tok_loaded, 32)
                gate(0, 0, slice(0, BANK), BANK)
                gate(1, 1, slice(BANK, 2 * BANK), BANK)
                with pe.Fori(1, CHUNKS // 2) as i:
                    for b in range(2):
                        pe.wait_ge(gate_done, i * 2 + (b - 1))
                        gate(i * 2 + b, b, bass.ds(i * (2 * BANK) + b * BANK, BANK), BANK)
                pe.wait_ge(gate_done, CHUNKS - 2)
                gate(CHUNKS - 1, 0, slice((CHUNKS - 1) * BANK, S), TAIL)
                pe.wait_ge(gate_done, CHUNKS)
                for c in range(CHUNKS):
                    score(0, c, first=True)
                with pe.Fori(0, TT - 1) as t:
                    for c in range(CHUNKS):
                        turn(t, c)
                        score(t + 1, c)
                        times_context(t, c)
                for c in range(CHUNKS):
                    turn(TT - 1, c)
                    times_context(TT - 1, c)
                pe.wait_ge(attended_ready, TT)
                for i in range(TT):
                    last = nc.tensor.transpose(ps_turn[i // 4][:, i % 4 * P:(i % 4 + 1) * P],
                                               attended[:, i, :], ident[:, :])
                    if i % 4 == 3:
                        last.then_inc(out_turned, 1)
                for half in range(2):
                    pe.wait_ge(attended_t_ready[half], 1)
                    for j in range(4):
                        i = half * 4 + j
                        nc.tensor.matmul(ps_proj[half][:, j * P:(j + 1) * P], attended_t[:, i * P:(i + 1) * P],
                                         w_out[:, :], start=True, stop=False)
                        last = nc.tensor.matmul(ps_proj[half][:, j * P:(j + 1) * P], ones[0:1, :],
                                                b_out[:, :], start=False, stop=True)
                    last.then_inc(projected, 1)

            @block.scalar
            def _(act):
                def round_gate(n, b, at, w):
                    act.wait_ge(gate_ready, n + 1)
                    nc.scalar.activation(gate_hi[:, at], ps_scores[b][:, 0:w], ACT.Identity, bias=b_gate[:, :])\
                        .then_inc(gate_rounded, 1)

                def keep(t, c, first=False):
                    act.wait_ge(scores_ready, t * CHUNKS + c + 1)
                    if not first:
                        act.wait_ge(exp_done, t * CHUNKS + (c + 1 - CHUNKS))
                    w, at = width(c), slice(c * BANK, c * BANK + width(c))
                    nc.scalar.activation(scores[:, at], ps_scores[c % 2][:, 0:w], ACT.Copy).then_inc(scores_kept, 1)

                def exp(t, c, first=False):
                    if c == 0:
                        act.wait_ge(max_ready, t + 1)
                    if c != 1 and not (first and c < 2):
                        act.wait_ge(turned, t * CHUNKS + (c - 1 if c else 0))
                    w, at = width(c), slice(c * BANK, c * BANK + width(c))
                    nc.scalar.activation(prob_tile(c)[:, 0:w], scores[:, at], ACT.Exp, bias=neg_max[:, :],
                                         accum_out=chunk_den[:, c:c + 1]).then_inc(exp_done, 1)

                nc.scalar.activation(xn_hi[:, :], xn_t[:, :], ACT.Copy).then_inc(split_hi, 1)
                act.wait_ge(loaded, 64)
                with act.Fori(0, CHUNKS // 2) as i:
                    for b in range(2):
                        round_gate(i * 2 + b, b, bass.ds(i * (2 * BANK) + b * BANK, BANK), BANK)
                round_gate(CHUNKS - 1, 0, slice((CHUNKS - 1) * BANK, S), TAIL)
                act.wait_ge(tail_cleared, 1)
                for c in range(CHUNKS):
                    keep(0, c, first=True)
                exp(0, 0, first=True)
                for c in range(CHUNKS):
                    if c + 1 < CHUNKS:
                        exp(0, c + 1, first=True)
                    keep(1, c)
                with act.Fori(1, TT - 1) as t:
                    exp(t, 0)
                    for c in range(CHUNKS):
                        if c + 1 < CHUNKS:
                            exp(t, c + 1)
                        keep(t + 1, c)
                for c in range(CHUNKS):
                    exp(TT - 1, c)
                act.wait_ge(out_turned, 2)
                nc.scalar.activation(attended_t[:, BANK:T], ps_turn[1][:, :], ACT.Copy).then_inc(attended_t_ready[1], 1)

            @block.vector
            def _(dve):
                def rest_gate(n, b, at, w):
                    dve.wait_ge(gate_rounded, n + 1)
                    nc.vector.scalar_tensor_tensor(gate_lo[:, at], ps_scores[b][:, 0:w], b_gate[:, :],
                                                   gate_hi[:, at].bitcast(F32), ALU.add, ALU.subtract)\
                        .then_inc(gate_done, 1)

                def top(t, c):
                    w, at = width(c), slice(c * BANK, c * BANK + width(c))
                    dve.wait_ge(scores_kept, t * CHUNKS + c + 1)
                    nc.vector.tensor_reduce(chunk_max[:, c:c + 1], scores[:, at], AX, ALU.max)\
                        .then_inc(chunk_max_ready, 1)

                def top_of_all(t):
                    dve.wait_ge(chunk_max_ready, t * CHUNKS + CHUNKS)
                    nc.vector.tensor_reduce(neg_max[:, :], chunk_max[:, :], AX, ALU.max, negate=True)\
                        .then_inc(max_ready, 1)

                def query(t, first=False):
                    if not first:
                        dve.wait_ge(scores_ready, t * CHUNKS)
                    at = slice(0, P) if first else bass.ds(t * P, P)
                    nc.vector.tensor_copy(q_hi[:, :], xn_hi[:, at].bitcast(F32))
                    nc.vector.tensor_copy(q_lo[:, :], xn_lo[:, at].bitcast(F32)).then_inc(q_ready, 1)

                def copy_turned(t, c):
                    dve.wait_ge(turned, t * CHUNKS + c + 1)
                    w = tiles(c) * P
                    nc.vector.tensor_copy(probs_t[c % 2][:, 0:w], ps_turn[c % 2][:, 0:w]).then_inc(probs_t_ready, 1)

                def invert(t):
                    dve.wait_ge(exp_done, t * CHUNKS + CHUNKS)
                    nc.vector.tensor_reduce(den[:, :], chunk_den[:, :], AX, ALU.add).then_inc(den_ready, 1)
                    dve.wait_ge(den_ready, t + 1)
                    nc.vector.reciprocal(inv_den[:, :], den[:, :]).then_inc(inv_ready, 1)

                def normalise(t, at):
                    dve.wait_ge(pv_done, t + 1)
                    dve.wait_ge(inv_ready, t + 1)
                    nc.vector.tensor_scalar(attended[:, at, :], ps_out[:, :].unsqueeze(1), inv_den[:, :], None, ALU.mult)\
                        .then_inc(attended_ready, 1)

                dve.wait_ge(split_hi, 1)
                nc.vector.tensor_tensor(xn_lo[:, :], xn_t[:, :], xn_hi[:, :].bitcast(F32), ALU.subtract)\
                    .then_inc(split_done, 1)
                nc.vector.memset(probs_tail[:, :], 0.0).then_inc(tail_cleared, 1)
                dve.wait_ge(loaded, 64)
                with dve.Fori(0, CHUNKS // 2) as i:
                    for b in range(2):
                        rest_gate(i * 2 + b, b, bass.ds(i * (2 * BANK) + b * BANK, BANK), BANK)
                rest_gate(CHUNKS - 1, 0, slice((CHUNKS - 1) * BANK, S), TAIL)
                dve.wait_ge(split_done, 1)
                query(0, first=True)
                for c in range(CHUNKS):
                    top(0, c)
                top_of_all(0)
                query(1)

                def tile(t, at):
                    for c in range(CHUNKS):
                        copy_turned(t, c)
                        top(t + 1, c)
                    invert(t)
                    top_of_all(t + 1)
                    normalise(t, at)

                with dve.Fori(0, TT - 2) as t:
                    tile(t, bass.ds(t, 1))
                    query(t + 2)
                tile(TT - 2, slice(TT - 2, TT - 1))
                for c in range(CHUNKS):
                    copy_turned(TT - 1, c)
                invert(TT - 1)
                normalise(TT - 1, slice(TT - 1, TT))
                dve.wait_ge(out_turned, 1)
                nc.vector.tensor_copy(attended_t[:, 0:BANK], ps_turn[0][:, :]).then_inc(attended_t_ready[0], 1)
                for half in range(2):
                    dve.wait_ge(projected, half + 1)
                    cut = slice(half * 4, half * 4 + 4)
                    nc.vector.tensor_tensor(x_res[:, cut, :], x_res[:, cut, :],
                                            ps_proj[half][:, :].rearrange("p (a d) -> p a d", a=4), ALU.add)


def experts(nc, sems, x_res, xn_t, consts, ins):
    E, F = 8, 352
    FT = [(0, P), (P, P), (2 * P, F - 2 * P)]
    UNITS = 2 * len(FT)
    with Phase(nc, sems, "moe") as ph:
        router = ph.sb("router", [P, E])
        w_in = [ph.sb(f"w_in{b}", [P, 2 * F]) for b in range(2)]
        w_down = [ph.sb(f"w_down{b}", [P, len(FT), D]) for b in range(2)]
        logit_max = ph.sb("logit_max", [P, TT])
        shifted = ph.sb("shifted", [P, TT, E])
        expd = ph.sb("expd", [P, TT, E])
        den = ph.sb("den", [P, TT])
        inv_den = ph.sb("inv_den", [P, TT])
        probs = ph.sb("probs", [P, TT, E])
        best = ph.sb("best", [P, TT, 8])
        best_at = ph.sb("best_at", [P, TT, 8], U32)
        best_at_f = ph.sb("best_at_f", [P, TT, 8])
        pair_sum = ph.sb("pair_sum", [P, TT])
        pair_inv = ph.sb("pair_inv", [P, TT])
        chosen_w = ph.sb("chosen_w", [P, TT, 2])
        hit = [ph.sb(f"hit{k}", [P, TT, E]) for k in range(2)]
        hit_w = [ph.sb(f"hit_w{k}", [P, TT, E]) for k in range(2)]
        expert_w = ph.sb("expert_w", [P, TT, E])
        silu = [ph.sb(f"silu{n}", [P, BANK]) for n in range(2)]
        acts = [[ph.sb(f"acts{b}_{f}", [P, T]) for f in range(len(FT))] for b in range(2)]
        ps_gate = [ph.ps(f"ps_gate{n}", [P, BANK]) for n in range(2)]
        ps_up = [ph.ps(f"ps_up{n}", [P, BANK]) for n in range(2)]
        ps_down = [ph.ps(f"ps_down{n}", [P, BANK]) for n in range(2)]
        ps_router = ph.ps("ps_router", [P, TT * E])
        chain_sem = ph.sem("chain")
        router_loaded = ph.sem("router_loaded")
        in_loaded = [ph.sem(f"in_loaded{b}") for b in range(2)]
        down_loaded = [ph.sem(f"down_loaded{b}") for b in range(2)]
        logits_ready = ph.sem("logits_ready")
        shifted_ready = ph.sem("shifted_ready")
        exp_done = ph.sem("exp_done")
        gate_ready = ph.sem("gate_ready")
        up_ready = ph.sem("up_ready")
        silu_done = ph.sem("silu_done")
        acts_done = ph.sem("acts_done")
        down_ready = ph.sem("down_ready")
        down_added = ph.sem("down_added")

        def wide(stat, n):
            return stat.unsqueeze(2).to_broadcast([P, TT, n])

        with ph.block() as block:

            @block.sync
            def _(sp):
                sp.dma_start(router[:, :], ins["router"]).then_inc(router_loaded, 16)

                def load(e, b):
                    at = slice(e, e + 1) if isinstance(e, int) else bass.ds(e, 1)
                    sp.dma_start(w_in[b][:, :], ins["w_moe_in"][at].rearrange("a d f -> (a d) f"))\
                        .then_inc(in_loaded[b], 16)

                def load_down(e, b):
                    at = slice(e, e + 1) if isinstance(e, int) else bass.ds(e, 1)
                    sp.dma_start(w_down[b][:, :, :], ins["w_moe_down"][at].rearrange("a f k d -> (a f) k d"))\
                        .then_inc(down_loaded[b], 16)

                for e in range(2):
                    load(e, e)
                    load_down(e, e)
                with sp.Fori(1, E // 2) as i:
                    for b in range(2):
                        sp.wait_ge(up_ready, i * (2 * UNITS) + UNITS * (b - 1))
                        load(i * 2 + b, b)
                        sp.wait_ge(down_ready, i * 4 + 2 * (b - 1))
                        load_down(i * 2 + b, b)

            @block.tensor
            def _(pe):
                def expert_in(e, b):
                    for f, (start, rows) in enumerate(FT):
                        for n in range(2):
                            count = e * UNITS + 2 * f + n
                            first = isinstance(e, int) and count < 2
                            cols = xn_t[:, n * BANK:(n + 1) * BANK]
                            if not first:
                                pe.wait_ge(silu_done, count - 1)
                            nc.tensor.matmul(ps_gate[n][0:rows, :], w_in[b][:, start:start + rows], cols,
                                             start=True, stop=True).then_inc(gate_ready, 1)
                            if not first:
                                pe.wait_ge(acts_done, count - 1)
                            nc.tensor.matmul(ps_up[n][0:rows, :], w_in[b][:, F + start:F + start + rows], cols,
                                             start=True, stop=True).then_inc(up_ready, 1)

                def expert_out(e, b):
                    pe.wait_ge(acts_done, e * UNITS + UNITS)
                    for half in range(2):
                        if not (isinstance(e, int) and e == 0):
                            pe.wait_ge(down_added, e * 2 + half - 1)
                        for j in range(4):
                            i = half * 4 + j
                            for f, (_, rows) in enumerate(FT):
                                last = nc.tensor.matmul(ps_down[half][:, j * P:(j + 1) * P],
                                                        acts[b][f][0:rows, i * P:(i + 1) * P],
                                                        w_down[b][0:rows, f, :], start=(f == 0), stop=(f == 2))
                        last.then_inc(down_ready, 1)

                pe.wait_ge(router_loaded, 16)
                for i in range(TT):
                    last = nc.tensor.matmul(ps_router[:, i * E:(i + 1) * E], xn_t[:, i * P:(i + 1) * P],
                                            router[:, :], start=True, stop=True)
                last.then_inc(logits_ready, 1)
                pe.wait_ge(in_loaded[0], 16)
                expert_in(0, 0)
                pe.wait_ge(in_loaded[1], 16)
                expert_in(1, 1)
                pe.wait_ge(down_loaded[0], 16)
                expert_out(0, 0)
                with pe.Fori(1, E // 2) as i:
                    for b in range(2):
                        pe.wait_ge(in_loaded[b], i * 16 + 16)
                        expert_in(i * 2 + b, b)
                        pe.wait_ge(down_loaded[1 - b], i * 16 + 16 * b)
                        expert_out(i * 2 + (b - 1), 1 - b)
                pe.wait_ge(down_loaded[1], E // 2 * 16)
                expert_out(E - 1, 1)

            @block.scalar
            def _(act):
                act.wait_ge(shifted_ready, 1)
                nc.scalar.activation(expd[:, :, :], shifted[:, :, :], ACT.Exp).then_inc(exp_done, 1)

                def gates(e):
                    for f, (_, rows) in enumerate(FT):
                        for n in range(2):
                            count = e * UNITS + 2 * f + n
                            act.wait_ge(gate_ready, count + 1)
                            if not (isinstance(e, int) and count < 2):
                                act.wait_ge(acts_done, count - 1)
                            nc.scalar.activation(silu[n][0:rows, :], ps_gate[n][0:rows, :], ACT.Silu)\
                                .then_inc(silu_done, 1)

                gates(0)
                with act.Fori(1, E) as e:
                    gates(e)

            @block.vector
            def _(dve):
                step = Chain(dve, chain_sem)
                logits = ps_router[:, :].rearrange("p (i e) -> p i e", e=E)
                dve.wait_ge(logits_ready, 1)
                step(nc.vector.tensor_reduce(logit_max[:, :], logits, AX, ALU.max))
                nc.vector.tensor_tensor(shifted[:, :, :], logits, wide(logit_max[:, :], E), ALU.subtract)\
                    .then_inc(shifted_ready, 1)
                dve.wait_ge(exp_done, 1)
                step(nc.vector.tensor_reduce(den[:, :], expd[:, :, :], AX, ALU.add))
                step(nc.vector.reciprocal(inv_den[:, :], den[:, :]))
                step(nc.vector.tensor_tensor(probs[:, :, :], expd[:, :, :], wide(inv_den[:, :], E), ALU.mult))
                for i in range(TT):
                    last = nc.vector.max(best[:, i, :], probs[:, i, :])
                step(last)
                for i in range(TT):
                    last = nc.vector.max_index(best_at[:, i, :], best[:, i, :], probs[:, i, :])
                step(last)
                step(nc.vector.tensor_copy(best_at_f[:, :, :], best_at[:, :, :]))
                step(nc.vector.tensor_tensor(pair_sum[:, :], best[:, :, 0], best[:, :, 1], ALU.add))
                step(nc.vector.reciprocal(pair_inv[:, :], pair_sum[:, :]))
                step(nc.vector.tensor_tensor(chosen_w[:, :, :], best[:, :, 0:2], wide(pair_inv[:, :], 2), ALU.mult))
                places = consts["places"][:, :].unsqueeze(1).to_broadcast([P, TT, E])
                for k in range(2):
                    step(nc.vector.tensor_tensor(hit[k][:, :, :], places, wide(best_at_f[:, :, k], E), ALU.is_equal))
                    step(nc.vector.tensor_tensor(hit_w[k][:, :, :], hit[k][:, :, :], wide(chosen_w[:, :, k], E),
                                                 ALU.mult))
                step(nc.vector.tensor_tensor(expert_w[:, :, :], hit_w[0][:, :, :], hit_w[1][:, :, :], ALU.add))

                def products(e, b):
                    for f, (_, rows) in enumerate(FT):
                        for n in range(2):
                            count = e * UNITS + 2 * f + n
                            dve.wait_ge(up_ready, count + 1)
                            dve.wait_ge(silu_done, count + 1)
                            nc.vector.tensor_tensor(acts[b][f][0:rows, n * BANK:(n + 1) * BANK], ps_up[n][0:rows, :],
                                                    silu[n][0:rows, :], ALU.mult).then_inc(acts_done, 1)

                def add(e):
                    for half in range(2):
                        dve.wait_ge(down_ready, e * 2 + half + 1)
                        for j in range(4):
                            i = half * 4 + j
                            at = slice(e, e + 1) if isinstance(e, int) else bass.ds(e, 1)
                            last = nc.vector.scalar_tensor_tensor(
                                x_res[:, i, :], ps_down[half][:, j * P:(j + 1) * P], expert_w[:, i, at],
                                x_res[:, i, :], ALU.mult, ALU.add)
                        last.then_inc(down_added, 1)

                products(0, 0)
                products(1, 1)
                with dve.Fori(1, E // 2) as i:
                    for b in range(2):
                        add(i * 2 + (b - 2))
                        products(i * 2 + b, b)
                add(E - 2)
                add(E - 1)


def linear_attention(nc, sems, x_res, xn_t, xn_tok, consts, ins):
    R = 64
    W = HEADS * D
    scale = float(R) ** -0.5
    with Phase(nc, sems, "la") as ph:
        w_v = ph.sb("w_v", [R, HEADS, D])
        w_o = ph.sb("w_o", [R, HEADS, D])
        w_q = ph.sb("w_q", [R, HEADS, D])
        w_k = ph.sb("w_k", [P, HEADS * R])
        b_v = ph.sb("b_v", [R, HEADS])
        b_q = ph.sb("b_q", [R, HEADS])
        b_k = ph.sb("b_k", [1, HEADS * R])
        b_o = ph.sb("b_o", [1, D])
        tokens = ph.sb("tokens", [1, 1])
        gram = ph.sb("gram", [P, D])
        s_col = ph.sb("s_col", [P, 1])
        s_row = ph.sb("s_row", [1, D])
        c_row = ph.sb("c_row", [1, W])
        vw = ph.sb("vw", [P, W])
        z = ph.sb("z", [P, W])
        z0 = ph.sb("z0", [1, W])
        n_all = ph.sb("n_all", [R, W])
        m_mat = ph.sb("m_mat", [P, D])
        b_row = ph.sb("b_row", [1, D])
        ps_w = ph.ps("ps_w", [P, W])
        ps_r = ph.ps("ps_r", [P, W])
        loaded = ph.sem("loaded")
        const_ready = ph.sem("const_ready")
        gram_ready = ph.sem("gram_ready")
        gram_kept = ph.sem("gram_kept")
        c_ready = ph.sem("c_ready")
        c_kept = ph.sem("c_kept")
        vw_ready = ph.sem("vw_ready")
        vw_kept = [ph.sem(f"vw_kept{b}") for b in range(2)]
        z_ready = ph.sem("z_ready")
        z_kept = ph.sem("z_kept")
        z0_ready = ph.sem("z0_ready")
        z0_kept = ph.sem("z0_kept")
        n_ready = ph.sem("n_ready")
        n_kept = [ph.sem(f"n_kept{b}") for b in range(2)]
        m_ready = ph.sem("m_ready")
        m_kept = ph.sem("m_kept")
        out_ready = ph.sem("out_ready")
        HALF = W // 2

        with ph.block() as block:

            @block.sync
            def _(sp):
                names = (("w_la_v", w_v), ("w_la_o", w_o), ("w_la_q", w_q))
                for name, tile in names:
                    sp.dma_start(tile[:, :, :], ins[name]).then_inc(loaded, 16)
                names = (("w_la_k", w_k), ("b_la_v", b_v), ("b_la_q", b_q), ("b_la_k", b_k), ("b_la_o", b_o))
                for name, tile in names:
                    sp.dma_start(tile[:, :], ins[name]).then_inc(loaded, 16)

            @block.tensor
            def _(pe):
                ones = consts["ones"]
                for i in range(TT):
                    last = nc.tensor.matmul(ps_w[:, 0:D], xn_tok[:, i, :], xn_tok[:, i, :],
                                            start=(i == 0), stop=(i == TT - 1))
                for i in range(TT):
                    last = nc.tensor.matmul(ps_w[:, BANK:BANK + 1], xn_tok[:, i, :], ones[:, 0:1],
                                            start=(i == 0), stop=(i == TT - 1))
                for i in range(TT):
                    last = nc.tensor.matmul(ps_w[0:1, 2 * BANK:2 * BANK + D], ones[:, 0:1], xn_tok[:, i, :],
                                            start=(i == 0), stop=(i == TT - 1))
                last.then_inc(gram_ready, 1)
                pe.wait_ge(loaded, 8 * 16)
                for h in range(HEADS):
                    last = nc.tensor.matmul(ps_r[0:1, h * D:(h + 1) * D], b_v[:, h:h + 1], w_o[:, h, :],
                                            start=True, stop=True)
                last.then_inc(c_ready, 1)
                pe.wait_ge(gram_kept, 1)
                for h in range(HEADS):
                    last = nc.tensor.matmul(ps_w[:, h * D:(h + 1) * D], w_v[:, h, :], w_o[:, h, :],
                                            start=True, stop=True)
                    if h % 8 == 7:
                        last.then_inc(vw_ready, 1)
                pe.wait_ge(c_kept, 1)
                pe.wait_ge(const_ready, 1)
                for b in range(2):
                    pe.wait_ge(vw_kept[b], 1)
                for c in range(W // BANK):
                    cut = slice(c * BANK, (c + 1) * BANK)
                    nc.tensor.matmul(ps_w[:, cut], gram[:, :], vw[:, cut], start=True, stop=False)
                    last = nc.tensor.matmul(ps_w[:, cut], s_row[:, :], c_row[:, cut], start=False, stop=True)
                last.then_inc(z_ready, 1)
                for c in range(W // BANK):
                    cut = slice(c * BANK, (c + 1) * BANK)
                    nc.tensor.matmul(ps_r[0:1, cut], s_col[:, :], vw[:, cut], start=True, stop=False)
                    last = nc.tensor.matmul(ps_r[0:1, cut], tokens[:, :], c_row[:, cut], start=False, stop=True)
                last.then_inc(z0_ready, 1)
                pe.wait_ge(z_kept, 1)
                pe.wait_ge(z0_kept, 1)
                for h in range(HEADS):
                    cut = slice(h * D, (h + 1) * D)
                    nc.tensor.matmul(ps_w[0:R, cut], w_k[:, h * R:(h + 1) * R], z[:, cut], start=True, stop=False)
                    last = nc.tensor.matmul(ps_w[0:R, cut], b_k[:, h * R:(h + 1) * R], z0[:, cut],
                                            start=False, stop=True)
                    if h % 8 == 7:
                        last.then_inc(n_ready, 1)
                for b in range(2):
                    pe.wait_ge(n_kept[b], 1)
                for h in range(HEADS):
                    nc.tensor.matmul(ps_r[:, 0:D], w_q[:, h, :], n_all[:, h * D:(h + 1) * D],
                                     start=(h == 0), stop=(h == HEADS - 1))
                for h in range(HEADS):
                    last = nc.tensor.matmul(ps_r[0:1, BANK:BANK + D], b_q[:, h:h + 1], n_all[:, h * D:(h + 1) * D],
                                            start=(h == 0), stop=(h == HEADS - 1))
                last.then_inc(m_ready, 1)
                pe.wait_ge(m_kept, 1)
                for i in range(TT):
                    nc.tensor.matmul(ps_w[:, i * D:(i + 1) * D], xn_t[:, i * P:(i + 1) * P], m_mat[:, :],
                                     start=True, stop=False)
                    last = nc.tensor.matmul(ps_w[:, i * D:(i + 1) * D], ones[0:1, :], b_row[:, :],
                                            start=False, stop=True)
                last.then_inc(out_ready, 1)

            @block.scalar
            def _(act):
                act.wait_ge(c_ready, 1)
                nc.scalar.activation(c_row[:, :], ps_r[0:1, :], ACT.Copy).then_inc(c_kept, 1)
                act.wait_ge(vw_ready, 2)
                nc.scalar.activation(vw[:, HALF:W], ps_w[:, HALF:W], ACT.Copy).then_inc(vw_kept[1], 1)
                act.wait_ge(z0_ready, 1)
                nc.scalar.activation(z0[:, :], ps_r[0:1, :], ACT.Copy).then_inc(z0_kept, 1)
                act.wait_ge(n_ready, 2)
                nc.scalar.activation(n_all[:, HALF:W], ps_w[0:R, HALF:W], ACT.Copy, scale=scale)\
                    .then_inc(n_kept[1], 1)

            @block.vector
            def _(dve):
                nc.vector.memset(tokens[:, :], float(T)).then_inc(const_ready, 1)
                dve.wait_ge(gram_ready, 1)
                nc.vector.tensor_copy(gram[:, :], ps_w[:, 0:D])
                nc.vector.tensor_copy(s_col[:, :], ps_w[:, BANK:BANK + 1])
                nc.vector.tensor_copy(s_row[:, :], ps_w[0:1, 2 * BANK:2 * BANK + D]).then_inc(gram_kept, 1)
                dve.wait_ge(vw_ready, 1)
                nc.vector.tensor_copy(vw[:, 0:HALF], ps_w[:, 0:HALF]).then_inc(vw_kept[0], 1)
                dve.wait_ge(z_ready, 1)
                nc.vector.tensor_copy(z[:, :], ps_w[:, :]).then_inc(z_kept, 1)
                dve.wait_ge(n_ready, 1)
                nc.vector.tensor_scalar(n_all[:, 0:HALF], ps_w[0:R, 0:HALF], scale, None, ALU.mult)\
                    .then_inc(n_kept[0], 1)
                dve.wait_ge(m_ready, 1)
                nc.vector.tensor_copy(m_mat[:, :], ps_r[:, 0:D])
                nc.vector.tensor_tensor(b_row[:, :], ps_r[0:1, BANK:BANK + D], b_o[:, :], ALU.add)\
                    .then_inc(m_kept, 1)
                dve.wait_ge(out_ready, 1)
                nc.vector.tensor_tensor(x_res[:, :, :], x_res[:, :, :],
                                        ps_w[:, 0:TT * D].rearrange("p (i d) -> p i d", d=D), ALU.add)


def cross_attention_1(nc, sems, x_res, xn_t, consts, ins):
    G, GH, HD, ROWS = 4, 4, 8, 32
    VC = HD + 1
    UNROLL = 3
    ROUNDS = KT // UNROLL
    assert KT % UNROLL == 0
    KCOLS = KT * P
    CHUNKS = KT * P // (UNROLL * P)
    CH = UNROLL * P
    LAST = S - (KT - 1) * P
    scale = float(D) ** -0.5
    E_RING, M_RING, P_RING = 3, 2, 6
    with Phase(nc, sems, "ca1") as outer:
        heads = [outer.sb(f"heads{g}", [P, T]) for g in range(G)]
        with Phase(nc, sems, "ca1s") as ph:
            keys = ph.sb("keys", [P, G, KCOLS], F32R)
            values = ph.sb("values", [P, KT * HEADS * VC])
            values4 = values[:, :].rearrange("p (k h c) -> p k h c", h=HEADS, c=VC)

            with Phase(nc, sems, "ca1k") as kp:
                w_k = kp.sb("w_k", [P, G, P])
                w_v = kp.sb("w_v", [P, D])
                ctx = [kp.sb(f"ctx{b}", [P, CH]) for b in range(2)]
                rounded = [kp.sb(f"rounded{b}", [P, CH], F32R) for b in range(2)]
                ps_k = [kp.ps(f"ps_k{b}", [P, CH]) for b in range(2)]
                ps_v = kp.ps("ps_v", [P, UNROLL * P])
                w_loaded = kp.sem("w_loaded")
                ctx_loaded = [kp.sem(f"ctx_loaded{b}") for b in range(2)]
                values_set = kp.sem("values_set")
                k_ready = kp.sem("k_ready")
                k_rounded = kp.sem("k_rounded")
                k_done = kp.sem("k_done")
                v_ready = kp.sem("v_ready")
                v_done = kp.sem("v_done")
                with ph.block() as block:

                    @block.sync
                    def _(sp):
                        sp.dma_start(w_k[:, :, :], ins["w_ca1_k"]).then_inc(w_loaded, 16)
                        sp.dma_start(w_v[:, :], ins["w_ca1_v"]).then_inc(w_loaded, 16)

                        def load(b, at):
                            sp.dma_start(ctx[b][:, :], ins["ctx_t"][:, at]).then_inc(ctx_loaded[b], 16)

                        for b in range(2):
                            load(b, slice(b * CH, (b + 1) * CH))
                        with sp.Fori(1, CHUNKS // 2) as i:
                            for b in range(2):
                                sp.wait_ge(v_ready, i * 2 + (b - 1))
                                load(b, bass.ds(i * (2 * CH) + b * CH, CH))
                        sp.wait_ge(v_ready, CHUNKS - 2)
                        load(0, slice((CHUNKS - 1) * CH, CHUNKS * CH))

                    @block.gpsimd
                    def _(pool):
                        nc.gpsimd.memset(values4[:, KT - 1, :, :], 0.0).then_inc(values_set, 1)
                        nc.gpsimd.memset(values4[:, 0:KT - 1, :, HD], 1.0).then_inc(values_set, 1)
                        pool.wait_ge(values_set, 2)
                        nc.gpsimd.memset(values4[0:LAST, KT - 1, :, HD], 1.0).then_inc(values_set, 1)

                    @block.tensor
                    def _(pe):
                        def chunk(c, b, first=False):
                            for g in range(G):
                                if not (first and c == 0 and g < 2):
                                    pe.wait_ge(k_done, c * G + (g - 1))
                                nc.tensor.matmul(ps_k[g % 2][:, :], w_k[:, g, :], ctx[b][:, :], start=True, stop=True)\
                                    .then_inc(k_ready, 1)
                            if not (first and c == 0):
                                pe.wait_ge(v_done, c)
                            for j in range(UNROLL):
                                last = nc.tensor.matmul(ps_v[:, j * P:(j + 1) * P], ctx[b][:, j * P:(j + 1) * P],
                                                        w_v[:, :], start=True, stop=True)
                            last.then_inc(v_ready, 1)

                        pe.wait_ge(w_loaded, 32)
                        for b in range(2):
                            pe.wait_ge(ctx_loaded[b], 16)
                            chunk(b, b, first=True)
                        with pe.Fori(1, CHUNKS // 2) as i:
                            for b in range(2):
                                pe.wait_ge(ctx_loaded[b], i * 16 + 16)
                                chunk(i * 2 + b, b)
                        pe.wait_ge(ctx_loaded[0], (CHUNKS // 2 + 1) * 16)
                        chunk(CHUNKS - 1, 0)

                    @block.scalar
                    def _(act):
                        def chunk(c, first=False):
                            for g in range(G):
                                act.wait_ge(k_ready, c * G + g + 1)
                                if not (first and c == 0 and g < 2):
                                    act.wait_ge(k_done, c * G + (g - 1))
                                nc.scalar.activation(rounded[g % 2][:, :], ps_k[g % 2][:, :], ACT.Identity,
                                                     bias=consts["masks"][:, 3:4]).then_inc(k_rounded, 1)

                        chunk(0, first=True)
                        with act.Fori(1, CHUNKS) as c:
                            chunk(c)

                    @block.vector
                    def _(dve):
                        def chunk(c, tail=False):
                            at = bass.ds(c * CH, CH) if not isinstance(c, int) else slice(c * CH, (c + 1) * CH)
                            for g in range(G):
                                dve.wait_ge(k_rounded, c * G + g + 1)
                                nc.vector.scalar_tensor_tensor(
                                    keys[:, g, at], rounded[g % 2][:, :].bitcast(F32), consts["masks"][:, 2:3],
                                    ps_k[g % 2][:, :], ALU.mult, ALU.add).then_inc(k_done, 1)
                            dve.wait_ge(v_ready, c + 1)
                            split = ps_v[:, :].rearrange("p (k h c) -> p k h c", k=UNROLL, c=HD)
                            if tail:
                                nc.vector.tensor_copy(values4[:, KT - UNROLL:KT - 1, :, 0:HD], split[:, 0:UNROLL - 1])
                                nc.vector.tensor_copy(values4[0:LAST, KT - 1, :, 0:HD], split[0:LAST, UNROLL - 1])\
                                    .then_inc(v_done, 1)
                            else:
                                wide = values[:, bass.ds(c * (UNROLL * HEADS * VC), UNROLL * HEADS * VC)]
                                nc.vector.tensor_copy(
                                    wide.rearrange("p (k h c) -> p k h c", h=HEADS, c=VC)[:, :, :, 0:HD], split)\
                                    .then_inc(v_done, 1)

                        with dve.Fori(0, CHUNKS - 1) as c:
                            chunk(c)
                        dve.wait_ge(values_set, 3)
                        chunk(CHUNKS - 1, tail=True)

            q_diag = [ph.sb(f"q_diag{b}", [P, GH, BANK], F32R) for b in range(2)]
            run_max = ph.sb("run_max", [P, GH, BANK])
            key_tile = [ph.sb(f"key_tile{s}", [P, P], F32R) for s in range(UNROLL)]
            next_key_tile = [ph.sb(f"next_key_tile{s}", [P, P], F32R) for s in range(UNROLL)]
            value_tile = [ph.sb(f"value_tile{s}", [P, GH * VC]) for s in range(UNROLL)]
            probs = [ph.sb(f"probs{r}", [P, BANK]) for r in range(P_RING)]
            w_q = ph.sb("w_q", [P, P])
            q_round = ph.sb("q_round", [P, BANK], F32R)
            q_rows = ph.sb("q_rows", [P, BANK], F32R)
            neg_max = ph.sb("neg_max", [P, P])
            max_hi = ph.sb("max_hi", [GH * 4, P], F32R)
            max_lo = ph.sb("max_lo", [GH * 4, P], F32R)
            ps_e = [ph.ps(f"ps_e{r}", [P, BANK]) for r in range(E_RING)]
            ps_m = [ph.ps(f"ps_m{r}", [P, 2, BANK]) for r in range(M_RING)]
            ps_o = ph.ps("ps_o", [P, BANK])
            cleared = ph.sem("cleared")
            w_q_loaded = ph.sem("w_q_loaded")
            key_loaded = [ph.sem(f"key_loaded{s}") for s in range(UNROLL)]
            next_key_loaded = [ph.sem(f"next_key_loaded{s}") for s in range(UNROLL)]
            value_loaded = [ph.sem(f"value_loaded{s}") for s in range(UNROLL)]
            e_ready = ph.sem("e_ready")
            m_ready = ph.sem("m_ready")
            exp_done = ph.sem("exp_done")
            max_done = ph.sem("max_done")
            pv_done = ph.sem("pv_done")
            q_ready = ph.sem("q_ready")
            q_rounded = ph.sem("q_rounded")
            q_rows_ready = ph.sem("q_rows_ready")
            q_placed = ph.sem("q_placed")
            run_turned = ph.sem("run_turned")
            max_found = ph.sem("max_found")
            max_turned = ph.sem("max_turned")
            hi_ready = ph.sem("hi_ready")
            max_split = ph.sem("max_split")
            max_placed = ph.sem("max_placed")
            heads_kept = ph.sem("heads_kept")
            PAIRS = 2 * G

            with ph.block() as block:

                @block.sync
                def _(sp):
                    def load(p, g, exp, top, i, s):
                        first = i is None
                        i = 0 if first else i
                        at = i * (UNROLL * P) + s * P
                        at = slice(at, at + P) if first else bass.ds(at, P)
                        of = lambda g: slice(g, g + 1) if isinstance(g, int) else bass.ds(g, 1)
                        if exp:
                            if top == "same" and not first:
                                sp.wait_ge(m_ready, (p + 1) * (KT * 2) + i * (UNROLL * 2) + 2 * (s + 1 - UNROLL))
                            elif top == "same" or not first:
                                if not (isinstance(p, int) and p == 0 and first):
                                    sp.wait_ge(e_ready, p * (KT * GH) + i * (UNROLL * GH) + GH * (s + 1 - UNROLL))
                            else:
                                sp.wait_ge(m_ready, (p + 1) * (KT * 2) + 2 * (s + 1 - UNROLL))
                            sp.dma_start(key_tile[s][:, :].bitcast(F32).unsqueeze(1), keys[:, of(g), at].bitcast(F32))\
                                .then_inc(key_loaded[s], 16)
                        if top == "next":
                            if not first:
                                sp.wait_ge(m_ready, (p + 1) * (KT * 2) + i * (UNROLL * 2) + 2 * (s + 1 - UNROLL))
                            sp.dma_start(next_key_tile[s][:, :].bitcast(F32).unsqueeze(1),
                                         keys[:, of(g + 1), at].bitcast(F32)).then_inc(next_key_loaded[s], 16)
                        if exp:
                            if not (isinstance(p, int) and p == 0 and first):
                                sp.wait_ge(pv_done, p * KT + i * UNROLL + (s + 1 - UNROLL))
                            at = i * (UNROLL * HEADS * VC) + g * (GH * VC) + s * HEADS * VC
                            at = slice(at, at + GH * VC) if isinstance(at, int) else bass.ds(at, GH * VC)
                            sp.dma_start(value_tile[s][:, :], values[:, at]).then_inc(value_loaded[s], 16)

                    def begin(p, g, exp, top):
                        for s in range(UNROLL):
                            load(p, g, exp, top, None, s)

                    def sweep(p, g, exp, top):
                        with sp.Fori(1, ROUNDS) as i:
                            for s in range(UNROLL):
                                load(p, g, exp, top, i, s)

                    def place_queries(p, count):
                        sp.wait_ge(q_rows_ready, count)
                        for j in range(GH):
                            rows = slice(j * ROWS, (j + 1) * ROWS)
                            sp.dma_start(q_diag[p][rows, j, :].bitcast(F32), q_rows[rows, :].bitcast(F32)).then_inc(q_placed, 16)

                    def place_maxima(p, count):
                        sp.wait_ge(max_split, count)
                        for j in range(GH):
                            for r, part in enumerate((max_hi, max_lo)):
                                row = j * ROWS + 3 * HD + r
                                sp.dma_start(q_diag[p][row:row + 1, j, :].bitcast(F32).rearrange("p (a q) -> p a q", q=P),
                                             part[j * 4:(j + 1) * 4, :].bitcast(F32)).then_inc(max_placed, 16)

                    def load_w_q(g, count):
                        if not isinstance(count, int) or count:
                            sp.wait_ge(q_ready, count)
                        group = slice(g, g + 1) if isinstance(g, int) else bass.ds(g, 1)
                        sp.dma_start(w_q[:, :], ins["w_ca1_q"][group].rearrange("g d n -> (g d) n"))\
                            .then_inc(w_q_loaded, 16)

                    load_w_q(0, 0)
                    sp.wait_ge(cleared, 1)
                    place_queries(0, 1)
                    place_queries(1, 2)
                    begin(-1, -1, False, "next")
                    sweep(-1, -1, False, "next")
                    begin(0, 0, True, "same")
                    place_maxima(0, 1)

                    def group(g):
                        load_w_q(g + 1, g * 2 + 2)
                        sweep(g * 2, g, True, "same")
                        begin(g * 2 + 1, g, True, "next")
                        place_queries(0, g * 2 + 3)
                        place_maxima(1, g * 2 + 2)
                        sweep(g * 2 + 1, g, True, "next")
                        begin(g * 2 + 2, g + 1, True, "same")
                        place_queries(1, g * 2 + 4)
                        place_maxima(0, g * 2 + 3)

                    group(0)
                    with sp.Fori(1, G - 1) as g:
                        group(g)
                    sweep(PAIRS - 2, G - 1, True, "same")
                    begin(PAIRS - 1, G - 1, True, None)
                    place_maxima(1, PAIRS)
                    sweep(PAIRS - 1, G - 1, True, None)

                @block.gpsimd
                def _(pool):
                    for b in range(2):
                        nc.gpsimd.memset(q_diag[b][:, :, :].bitcast(F32), 0.0)
                    nc.gpsimd.memset(neg_max[:, :], 0.0).then_inc(cleared, 1)

                @block.tensor
                def _(pe):
                    def sweep(p, half, exp, top):
                        def weigh(a, s, loads, start, stop):
                            pe.wait_ge(exp_done, a * GH + GH)
                            pe.wait_ge(value_loaded[s], loads * 16)
                            for j in range(GH):
                                last = nc.tensor.matmul(ps_o[j * ROWS:j * ROWS + VC, :],
                                                        value_tile[s][:, j * VC:(j + 1) * VC],
                                                        probs[(GH * s + j) % P_RING][:, :], start=start, stop=stop,
                                                        skip_group_check=True)
                            last.then_inc(pv_done, 1)

                        def tile(i, s, first):
                            a = p * KT + i * UNROLL + s
                            b = (p + 1) * (KT * 2) + i * (UNROLL * 2) + 2 * s
                            if exp:
                                pe.wait_ge(key_loaded[s], p * (ROUNDS * 16) + i * 16 + 16)
                            if top == "next":
                                pe.wait_ge(next_key_loaded[s], (p + 1) * (ROUNDS * 8) + i * 16 + 16)
                            for j in range(GH):
                                if exp:
                                    if not (first and isinstance(p, int) and p == 0 and s == 0 and j < E_RING):
                                        pe.wait_ge(exp_done, a * GH + (j + 1 - E_RING))
                                    nc.tensor.matmul(ps_e[(s + j) % E_RING][:, :], key_tile[s][:, :],
                                                     q_diag[half][:, j, :], start=True, stop=True).then_inc(e_ready, 1)
                                if top:
                                    if j % 2 == 0 and not (first and isinstance(p, int) and p == -1 and s == 0):
                                        pe.wait_ge(max_done, b + (j // 2 + 1 - M_RING))
                                    slot = next_key_tile[s] if top == "next" else key_tile[s]
                                    last = nc.tensor.matmul(ps_m[j // 2][:, j % 2, :], slot[:, :],
                                                            q_diag[1 - half][:, j, :], start=True, stop=True)
                                    if j % 2:
                                        last.then_inc(m_ready, 1)
                                if exp and j == 1 and not (first and s == 0):
                                    weigh(a - 1, (s - 1) % UNROLL, p * ROUNDS + i + (1 if s else 0), first and s == 1, False)

                        for s in range(UNROLL):
                            tile(0, s, True)
                        with pe.Fori(1, ROUNDS) as i:
                            for s in range(UNROLL):
                                tile(i, s, False)
                        if exp:
                            weigh(p * KT + (KT - 1), UNROLL - 1, p * ROUNDS + ROUNDS, False, True)

                    def project_half(half):
                        nc.tensor.matmul(ps_e[1][:, :], w_q[:, :], xn_t[:, half * BANK:(half + 1) * BANK],
                                         start=True, stop=True).then_inc(q_ready, 1)

                    def find_maxima(p):
                        pe.wait_ge(max_done, (p + 1) * (KT * 2))
                        for j in range(GH):
                            for i in range(4):
                                last = nc.tensor.transpose(ps_m[j // 2][:, j % 2, i * P:(i + 1) * P],
                                                           run_max[:, j, i * P:(i + 1) * P], consts["ident"][:, :])
                        last.then_inc(run_turned, 1)
                        pe.wait_ge(max_found, p + 1)
                        nc.tensor.transpose(ps_e[0][:, 0:P], neg_max[:, :], consts["ident"][:, :])\
                            .then_inc(max_turned, 1)

                    pe.wait_ge(w_q_loaded, 16)
                    project_half(0)
                    pe.wait_ge(q_rows_ready, 1)
                    project_half(1)
                    pe.wait_ge(q_placed, 128)
                    sweep(-1, 1, False, "next")
                    find_maxima(0)
                    pe.wait_ge(max_placed, 128)

                    def group(g):
                        pe.wait_ge(w_q_loaded, g * 16 + 32)
                        for half in range(2):
                            p = g * 2 + half
                            sweep(p, half, True, "next" if half else "same")
                            pe.wait_ge(exp_done, p * (KT * GH) + KT * GH)
                            project_half(half)
                            find_maxima(p + 1)
                            pe.wait_ge(heads_kept, p + 1)
                            pe.wait_ge(max_placed, p * 128 + 256)
                            pe.wait_ge(q_placed, p * 64 + 192)

                    group(0)
                    with pe.Fori(1, G - 1) as g:
                        group(g)
                    sweep(PAIRS - 2, 0, True, "same")
                    find_maxima(PAIRS - 1)
                    pe.wait_ge(heads_kept, PAIRS - 1)
                    pe.wait_ge(max_placed, PAIRS * 128)
                    sweep(PAIRS - 1, 1, True, None)

                @block.scalar
                def _(act):
                    def sweep(p):
                        def tile(i, s, first):
                            a = p * KT + i * UNROLL + s
                            for j in range(GH):
                                act.wait_ge(e_ready, a * GH + j + 1)
                                if not (isinstance(p, int) and p == 0 and first and (s == 0 or (s == 1 and j < 2))):
                                    act.wait_ge(pv_done, a + (j // 2 - 1))
                                nc.scalar.activation(probs[(GH * s + j) % P_RING][:, :], ps_e[(s + j) % E_RING][:, :],
                                                     ACT.Exp, scale=scale).then_inc(exp_done, 1)

                        for s in range(UNROLL):
                            tile(0, s, True)
                        with act.Fori(1, ROUNDS) as i:
                            for s in range(UNROLL):
                                tile(i, s, False)

                    def round_queries(count):
                        act.wait_ge(q_ready, count)
                        nc.scalar.activation(q_round[:, :], ps_e[1][:, :], ACT.Copy).then_inc(q_rounded, 1)

                    round_queries(1)
                    act.wait_ge(q_rows_ready, 1)
                    round_queries(2)
                    sweep(0)
                    round_queries(3)
                    with act.Fori(1, PAIRS - 2) as p:
                        sweep(p)
                        act.wait_ge(q_rows_ready, p + 2)
                        round_queries(p + 3)
                    sweep(PAIRS - 2)
                    sweep(PAIRS - 1)

                @block.vector
                def _(dve):
                    def sweep(p):
                        def tile(i, s, first):
                            for half in range(2):
                                b = p * (KT * 2) + i * (UNROLL * 2) + 2 * s + half
                                dve.wait_ge(m_ready, b + 1)
                                run = run_max[:, half * 2:half * 2 + 2, :]
                                if first and s == 0:
                                    nc.vector.tensor_copy(run, ps_m[half][:, :, :]).then_inc(max_done, 1)
                                else:
                                    dve.wait_ge(max_done, b - 1)
                                    nc.vector.tensor_tensor(run, ps_m[half][:, :, :], run, ALU.max)\
                                        .then_inc(max_done, 1)

                        for s in range(UNROLL):
                            tile(0, s, True)
                        with dve.Fori(1, ROUNDS) as i:
                            for s in range(UNROLL):
                                tile(i, s, False)

                    def split_queries(count):
                        dve.wait_ge(q_rounded, count)
                        if not (isinstance(count, int) and count == 1):
                            dve.wait_ge(q_placed, count * 64 - 64)
                        nc.vector.scalar_tensor_tensor(q_rows[:, :], q_round[:, :].bitcast(F32),
                                                       consts["masks"][:, 1:2], ps_e[1][:, :], ALU.mult, ALU.add)\
                            .then_inc(q_rows_ready, 1)

                    def find_maxima(p):
                        dve.wait_ge(run_turned, p + 1)
                        for half in range(2):
                            last = nc.vector.tensor_reduce(
                                neg_max[:, half * 8:half * 8 + 8],
                                ps_m[half][:, :, :].rearrange("p j (i k) -> p (j i) k", k=P), AX, ALU.max, negate=True)
                        last.then_inc(max_found, 1)
                        dve.wait_ge(max_turned, p + 1)
                        nc.vector.tensor_copy(max_hi[:, :], ps_e[0][0:GH * 4, 0:P]).then_inc(hi_ready, 1)
                        dve.wait_ge(hi_ready, p + 1)
                        nc.vector.tensor_tensor(max_lo[:, :], ps_e[0][0:GH * 4, 0:P], max_hi[:, :].bitcast(F32),
                                                ALU.subtract).then_inc(max_split, 1)

                    def keep_heads(p, g, half):
                        dve.wait_ge(pv_done, p * KT + KT)
                        nc.vector.tensor_copy(heads[g][:, half * BANK:(half + 1) * BANK], ps_o[:, :])\
                            .then_inc(heads_kept, 1)

                    dve.wait_ge(cleared, 1)
                    nc.vector.memset(ps_o[:, :], 0.0)
                    split_queries(1)
                    split_queries(2)
                    sweep(0)
                    find_maxima(0)
                    for g in range(G):
                        for half in range(2):
                            p = g * 2 + half
                            if p + 1 < PAIRS:
                                sweep(p + 1)
                                if p + 2 < PAIRS:
                                    split_queries(p + 3)
                                find_maxima(p + 1)
                            keep_heads(p, g, half)
        attend_out(nc, sems, x_res, heads, consts, ins, G, HD, ROWS)


def attend_out(nc, sems, x_res, heads, consts, ins, G, HD, ROWS):
    with Phase(nc, sems, "ao") as ph:
        w_o = ph.sb("w_o", [P, D])
        inv = [ph.sb(f"inv{b}", [P, HEADS]) for b in range(2)]
        normed = [ph.sb(f"normed{b}", [P, HEADS, HD]) for b in range(2)]
        normed_t = [ph.sb(f"normed_t{b}", [P, P]) for b in range(2)]
        ps_turn = [ph.ps(f"ps_turn{b}", [P, BANK]) for b in range(2)]
        ps_back = [ph.ps(f"ps_back{b}", [P, P]) for b in range(2)]
        ps_out = [ph.ps(f"ps_out{b}", [P, D]) for b in range(2)]
        loaded = ph.sem("loaded")
        turned = ph.sem("turned")
        inv_ready = ph.sem("inv_ready")
        normed_ready = ph.sem("normed_ready")
        back_ready = ph.sem("back_ready")
        back_kept = ph.sem("back_kept")
        out_ready = ph.sem("out_ready")
        out_added = ph.sem("out_added")
        with ph.block() as block:

            @block.sync
            def _(sp):
                sp.dma_start(w_o[:, :], ins["w_ca1_o"]).then_inc(loaded, 16)

            @block.tensor
            def _(pe):
                def turn(i):
                    if i >= 2:
                        pe.wait_ge(normed_ready, i - 1)
                    for g in range(G):
                        last = nc.tensor.transpose(ps_turn[i % 2][:, g * P:(g + 1) * P],
                                                   heads[g][:, i * P:(i + 1) * P], consts["ident"][:, :])
                    last.then_inc(turned, 1)

                pe.wait_ge(loaded, 16)
                turn(0)
                for i in range(TT):
                    if i + 1 < TT:
                        turn(i + 1)
                    pe.wait_ge(normed_ready, i + 1)
                    nc.tensor.transpose(ps_back[i % 2][:, :], normed[i % 2][:, :, :].rearrange("p h c -> p (h c)"),
                                        consts["ident"][:, :]).then_inc(back_ready, 1)
                    pe.wait_ge(back_kept, i + 1)
                    if i >= 2:
                        pe.wait_ge(out_added, i - 1)
                    nc.tensor.matmul(ps_out[i % 2][:, :], normed_t[i % 2][:, :], w_o[:, :], start=True, stop=True)\
                        .then_inc(out_ready, 1)

            @block.scalar
            def _(act):
                for i in range(TT):
                    act.wait_ge(back_ready, i + 1)
                    nc.scalar.activation(normed_t[i % 2][:, :], ps_back[i % 2][:, :], ACT.Copy).then_inc(back_kept, 1)

            @block.vector
            def _(dve):
                for i in range(TT + 1):
                    if i < TT:
                        dve.wait_ge(turned, i + 1)
                        by_head = ps_turn[i % 2][:, :].rearrange("p (h r) -> p h r", r=ROWS)
                        nc.vector.reciprocal(inv[i % 2][:, :], by_head[:, :, HD]).then_inc(inv_ready, 1)
                        dve.wait_ge(inv_ready, i + 1)
                        nc.vector.tensor_tensor(normed[i % 2][:, :, :], by_head[:, :, 0:HD],
                                                inv[i % 2][:, :].unsqueeze(2).to_broadcast([P, HEADS, HD]), ALU.mult)\
                            .then_inc(normed_ready, 1)
                    if i:
                        dve.wait_ge(out_ready, i)
                        nc.vector.tensor_tensor(x_res[:, i - 1, :], x_res[:, i - 1, :], ps_out[(i - 1) % 2][:, :],
                                                ALU.add).then_inc(out_added, 1)


def bit_linear_ffn(nc, sems, x_res, xn_tok, consts, ins):
    H = 512
    HC = H // P
    ROUND = 12582912.0
    with Phase(nc, sems, "bl") as ph:
        w1 = ph.sb("w1", [P, H])
        w2 = ph.sb("w2", [P, HC, D])
        b1 = ph.sb("b1", [P, H])
        b2 = ph.sb("b2", [P, D])
        w1_t = ph.sb("w1_t", [P, H], BF16)
        w2_t = ph.sb("w2_t", [P, HC * D], BF16)
        w_scaled = ph.sb("w_scaled", [P, H])
        w_scaled2 = ph.sb("w_scaled2", [P, HC * D])
        w_whole = ph.sb("w_whole", [P, H])
        w_whole2 = ph.sb("w_whole2", [P, HC * D])
        w_sums = ph.sb("w_sums", [P, 2])
        w_mean = ph.sb("w_mean", [P, 2])
        w_inv = ph.sb("w_inv", [P, 2])
        ident_b = ph.sb("ident_b", [P, P], BF16)
        squares = ph.sb("squares", [P, TT, D])
        x_scaled = ph.sb("x_scaled", [P, TT, D])
        x_shifted = ph.sb("x_shifted", [P, TT, D])
        x_whole = ph.sb("x_whole", [P, TT, D], BF16)
        x_turned = ph.sb("x_turned", [P, T], BF16)
        hidden_in = [ph.sb(f"hidden_in{b}", [P, H]) for b in range(2)]
        hidden = ph.sb("hidden", [P, TT, H])
        h_squares = ph.sb("h_squares", [P, H])
        h_scaled = [ph.sb(f"h_scaled{b}", [P, H]) for b in range(2)]
        h_shifted = [ph.sb(f"h_shifted{b}", [P, H]) for b in range(2)]
        h_whole = [ph.sb(f"h_whole{b}", [P, H], BF16) for b in range(2)]
        h_turned = [ph.sb(f"h_turned{b}", [P, H], BF16) for b in range(2)]
        summed = [ph.sb(f"summed{b}", [P, D]) for b in range(2)]
        ps_turn = [ph.ps(f"ps_turn{b}", [P, BANK]) for b in range(2)]
        ps_h = [ph.ps(f"ps_h{b}", [P, H]) for b in range(2)]
        ps_out = [ph.ps(f"ps_out{b}", [P, D]) for b in range(2)]
        ps_mean = ph.ps("ps_mean", [P, 2])

        loaded = ph.sem("loaded")
        chain_sem = ph.sem("chain")
        w_summed = ph.sem("w_summed")
        means_ready = ph.sem("means_ready")
        var_ready = ph.sem("var_ready")
        std_ready = ph.sem("std_ready")
        w_ready = ph.sem("w_ready")
        x_ready = ph.sem("x_ready")
        turn_ready = ph.sem("turn_ready")
        x_kept = ph.sem("x_kept")
        h_ready = ph.sem("h_ready")
        in_ready = ph.sem("in_ready")
        hidden_ready = ph.sem("hidden_ready")
        squared = ph.sem("squared")
        peaks_ready = ph.sem("peaks_ready")
        h_whole_ready = ph.sem("h_whole_ready")
        h_kept = ph.sem("h_kept")
        out_ready = ph.sem("out_ready")
        out_added = ph.sem("out_added")

        def stats(name):
            return {k: ph.sb(f"{name}_{k}", [P, TT]) for k in
                    ("sum_sq", "var", "std", "rstd", "sq", "vsq", "corr", "norm", "peak", "top", "clipped", "inv",
                     "step", "gain", "back")}

        x_stats, h_stats = stats("x"), stats("h")

        def wide(stat, width):
            return stat[:, :].unsqueeze(2).to_broadcast([P, TT, width])

        with ph.block() as block:

            @block.sync
            def _(sp):
                sp.dma_start(w1[:, :], ins["w_bl1"]).then_inc(loaded, 16)
                sp.dma_start(w2[:, :, :], ins["w_bl2"]).then_inc(loaded, 16)
                sp.dma_start(b1[:, :], ins["b_bl1"].to_broadcast([P, H])).then_inc(loaded, 16)
                sp.dma_start(b2[:, :], ins["b_bl2"].to_broadcast([P, D])).then_inc(loaded, 16)

            @block.tensor
            def _(pe):
                pe.wait_ge(w_summed, 1)
                nc.tensor.matmul(ps_mean[:, :], consts["ones"][:, :], w_sums[:, :], start=True, stop=True)\
                    .then_inc(means_ready, 1)
                pe.wait_ge(x_ready, 1)
                for i in range(TT):
                    last = nc.tensor.matmul(ps_turn[i // 4][:, i % 4 * P:(i % 4 + 1) * P], x_whole[:, i, :],
                                            ident_b[:, :], start=True, stop=True)
                    if i % 4 == 3:
                        last.then_inc(turn_ready, 1)
                pe.wait_ge(w_ready, 1)
                pe.wait_ge(x_kept, 2)
                for i in range(TT):
                    if i >= 2:
                        pe.wait_ge(in_ready, i - 1)
                    nc.tensor.matmul(ps_h[i % 2][:, :], x_turned[:, i * P:(i + 1) * P], w1_t[:, :],
                                     start=True, stop=True).then_inc(h_ready, 1)

                def turn(i):
                    pe.wait_ge(h_whole_ready, i + 1)
                    if i >= 2:
                        pe.wait_ge(h_kept, i - 1)
                    for c in range(HC):
                        last = nc.tensor.matmul(ps_turn[i % 2][:, c * P:(c + 1) * P],
                                                h_whole[i % 2][:, c * P:(c + 1) * P], ident_b[:, :],
                                                start=True, stop=True)
                    last.then_inc(turn_ready, 1)

                turn(0)
                for i in range(TT):
                    if i + 1 < TT:
                        turn(i + 1)
                    pe.wait_ge(h_kept, i + 1)
                    if i >= 2:
                        pe.wait_ge(out_added, i - 1)
                    for c in range(HC):
                        last = nc.tensor.matmul(ps_out[i % 2][:, :], h_turned[i % 2][:, c * P:(c + 1) * P],
                                                w2_t[:, c * D:(c + 1) * D], start=c == 0, stop=c == HC - 1)
                    last.then_inc(out_ready, 1)

            @block.scalar
            def _(act):
                act.wait_ge(var_ready, 1)
                nc.scalar.activation(x_stats["std"][:, :], x_stats["var"][:, :], ACT.Sqrt).then_inc(std_ready, 1)
                for b in range(2):
                    act.wait_ge(turn_ready, b + 1)
                    nc.scalar.activation(x_turned[:, b * BANK:(b + 1) * BANK], ps_turn[b][:, :], ACT.Copy)\
                        .then_inc(x_kept, 1)
                for i in range(TT):
                    act.wait_ge(in_ready, i + 1)
                    nc.scalar.activation(hidden[:, i, :], hidden_in[i % 2][:, :], ACT.Gelu).then_inc(hidden_ready, 1)
                    act.wait_ge(hidden_ready, i + 1)
                    if i:
                        act.wait_ge(squared, i)
                    nc.scalar.activation(h_squares[:, :], hidden[:, i, :], ACT.Square,
                                         accum_out=h_stats["sum_sq"][:, i:i + 1]).then_inc(squared, 1)
                act.wait_ge(var_ready, 2)
                nc.scalar.activation(h_stats["std"][:, :], h_stats["var"][:, :], ACT.Sqrt).then_inc(std_ready, 1)
                for i in range(TT):
                    act.wait_ge(turn_ready, i + 3)
                    if i >= 2:
                        act.wait_ge(out_ready, i - 1)
                    nc.scalar.activation(h_turned[i % 2][:, :], ps_turn[i % 2][:, :], ACT.Copy).then_inc(h_kept, 1)

            @block.vector
            def _(dve):
                step = Chain(dve, chain_sem)

                def norm_scales(s, width, turn, mean):
                    step(nc.vector.tensor_scalar(s["var"][:, :], s["sum_sq"][:, :], 1.0 / width, 1e-6,
                                                 ALU.mult, ALU.add))
                    nc.vector.tensor_copy(s["corr"][:, :], s["var"][:, :]).then_inc(var_ready, 1)
                    dve.wait_ge(std_ready, turn)
                    dve.wait_ge(var_ready, turn)
                    step(nc.vector.reciprocal(s["rstd"][:, :], s["std"][:, :]))
                    step(nc.vector.tensor_tensor(s["sq"][:, :], s["rstd"][:, :], s["rstd"][:, :], ALU.mult))
                    step(nc.vector.tensor_tensor(s["vsq"][:, :], s["sq"][:, :], s["var"][:, :], ALU.mult))
                    step(nc.vector.tensor_scalar(s["corr"][:, :], s["vsq"][:, :], -0.5, 1.5, ALU.mult, ALU.add))
                    step(nc.vector.tensor_tensor(s["norm"][:, :], s["rstd"][:, :], s["corr"][:, :], ALU.mult))
                    step(nc.vector.tensor_tensor(s["top"][:, :], s["peak"][:, :], s["norm"][:, :], ALU.mult))
                    step(nc.vector.tensor_scalar(s["clipped"][:, :], s["top"][:, :], 1e-5, 1.0 / 127.0,
                                                 ALU.max, ALU.mult))
                    step(nc.vector.reciprocal(s["inv"][:, :], s["clipped"][:, :]))
                    step(nc.vector.tensor_tensor(s["gain"][:, :], s["inv"][:, :], s["norm"][:, :], ALU.mult))
                    step(nc.vector.tensor_scalar(s["back"][:, :], s["clipped"][:, :], mean, None, ALU.mult))

                dve.wait_ge(loaded, 64)
                w2_flat = w2[:, :, :].rearrange("p c d -> p (c d)")
                nc.vector.tensor_reduce(w_sums[:, 0:1], w1[:, :], AX, ALU.add, apply_absolute_value=True)
                nc.vector.tensor_reduce(w_sums[:, 1:2], w2_flat, AX, ALU.add, apply_absolute_value=True)\
                    .then_inc(w_summed, 1)
                step(nc.vector.tensor_tensor(squares[:, :, :], xn_tok[:, :, :], xn_tok[:, :, :], ALU.mult))
                nc.vector.tensor_copy(ident_b[:, :], consts["ident"][:, :])
                nc.vector.tensor_reduce(x_stats["peak"][:, :], xn_tok[:, :, :], AX, ALU.max, apply_absolute_value=True)
                step(nc.vector.tensor_reduce(x_stats["sum_sq"][:, :], squares[:, :, :], AX, ALU.add))
                dve.wait_ge(means_ready, 1)
                step(nc.vector.tensor_scalar(w_mean[:, :], ps_mean[:, :], 1.0 / (H * D), 1e-5, ALU.mult, ALU.max))
                norm_scales(x_stats, D, 1, w_mean[:, 0:1])
                step(nc.vector.tensor_tensor(x_scaled[:, :, :], xn_tok[:, :, :], wide(x_stats["gain"], D), ALU.mult))
                step(nc.vector.tensor_scalar(x_shifted[:, :, :], x_scaled[:, :, :], ROUND, ROUND + 127.0,
                                             ALU.add, ALU.min))
                nc.vector.tensor_scalar(x_whole[:, :, :], x_shifted[:, :, :], ROUND, -128.0,
                                        ALU.subtract, ALU.max).then_inc(x_ready, 1)
                step(nc.vector.reciprocal(w_inv[:, :], w_mean[:, :]))
                nc.vector.tensor_scalar(w_scaled[:, :], w1[:, :], w_inv[:, 0:1], ROUND, ALU.mult, ALU.add)
                step(nc.vector.tensor_scalar(w_scaled2[:, :], w2_flat, w_inv[:, 1:2], ROUND, ALU.mult, ALU.add))
                nc.vector.tensor_scalar(w_whole[:, :], w_scaled[:, :], ROUND, -1.0, ALU.subtract, ALU.max)
                step(nc.vector.tensor_scalar(w_whole2[:, :], w_scaled2[:, :], ROUND, -1.0, ALU.subtract, ALU.max))
                nc.vector.tensor_scalar(w1_t[:, :], w_whole[:, :], 1.0, None, ALU.min)
                nc.vector.tensor_scalar(w2_t[:, :], w_whole2[:, :], 1.0, None, ALU.min).then_inc(w_ready, 1)
                for i in range(TT + 1):
                    if i < TT:
                        dve.wait_ge(h_ready, i + 1)
                        if i >= 2:
                            dve.wait_ge(hidden_ready, i - 1)
                        nc.vector.scalar_tensor_tensor(hidden_in[i % 2][:, :], ps_h[i % 2][:, :],
                                                       x_stats["back"][:, i:i + 1], b1[:, :], ALU.mult, ALU.add)\
                            .then_inc(in_ready, 1)
                    if i:
                        dve.wait_ge(hidden_ready, i)
                        nc.vector.tensor_reduce(h_stats["peak"][:, i - 1:i], hidden[:, i - 1, :], AX, ALU.max,
                                                apply_absolute_value=True).then_inc(peaks_ready, 1)
                dve.wait_ge(squared, TT)
                dve.wait_ge(peaks_ready, TT)
                norm_scales(h_stats, H, 2, w_mean[:, 1:2])

                def add_out(i):
                    dve.wait_ge(out_ready, i + 1)
                    nc.vector.scalar_tensor_tensor(summed[i % 2][:, :], ps_out[i % 2][:, :],
                                                   h_stats["back"][:, i:i + 1], b2[:, :], ALU.mult, ALU.add)\
                        .then_inc(out_added, 1)
                    dve.wait_ge(out_added, i + 1)
                    nc.vector.tensor_tensor(x_res[:, i, :], x_res[:, i, :], summed[i % 2][:, :], ALU.add)

                for i in range(TT):
                    b = i % 2
                    step(nc.vector.tensor_scalar(h_scaled[b][:, :], hidden[:, i, :], h_stats["gain"][:, i:i + 1],
                                                 ROUND, ALU.mult, ALU.add))
                    step(nc.vector.tensor_scalar(h_shifted[b][:, :], h_scaled[b][:, :], ROUND, -128.0,
                                                 ALU.subtract, ALU.max))
                    if i >= 2:
                        dve.wait_ge(turn_ready, i + 1)
                    nc.vector.tensor_scalar(h_whole[b][:, :], h_shifted[b][:, :], 127.0, None, ALU.min)\
                        .then_inc(h_whole_ready, 1)
                    if i >= 2:
                        add_out(i - 2)
                add_out(TT - 2)
                add_out(TT - 1)


def program(nc, ins, out):
    with ExitStack() as sems, Phase(nc, sems, "main") as ph:
        x_res = ph.sb("x_res", [P, TT, D])
        xn_t = ph.sb("xn_t", [P, T])
        ident = ph.sb("ident", [P, P])
        masks = ph.sb("masks", [P, 8])
        ones = ph.sb("ones", [P, P])
        places = ph.sb("places", [P, 8])
        consts = {"ones": ones, "places": places, "masks": masks, "ident": ident}
        norm_sems = [ph.sem(f"norm_{name}") for name in NORM_SEMS]
        loaded = ph.sem("loaded")
        stored = ph.sem("stored")
        ctx_loaded = ph.sem("ctx_loaded")
        ctx_tok_loaded = ph.sem("ctx_tok_loaded")
        tail_cleared = ph.sem("tail_cleared")
        with Phase(nc, sems, "early") as early:
            ctx_t = early.sb("ctx_t", [P, S])
            ctx_tok = early.sb("ctx_tok", [P, KT, D])
            with ph.block() as block:

                @block.sync
                def _(sp):
                    sp.dma_start(x_res[:, :, :], ins["x"].rearrange("a (i p) d -> p (a i) d", p=P)).then_inc(loaded, 16)
                    sp.dma_start(ident[:, :], ins["ident"]).then_inc(loaded, 16)
                    sp.dma_start(masks[:, :], ins["masks"]).then_inc(loaded, 16)
                    sp.dma_start(ones[:, :], ins["ones"]).then_inc(loaded, 16)
                    sp.dma_start(places[:, :], ins["places"]).then_inc(loaded, 16)
                    sp.wait_ge(loaded, 80)

                    sp.dma_start(ctx_t[:, :], ins["ctx_t"][:, 0:S]).then_inc(ctx_loaded, 16)
                    sp.dma_start(ctx_tok[:, 0:KT - 1, :],
                                 ins["ctx"][0, 0:(KT - 1) * P, :].rearrange("(k p) d -> p k d", p=P))\
                        .then_inc(ctx_tok_loaded, 16)
                    sp.wait_ge(tail_cleared, 1)
                    sp.dma_start(ctx_tok[0:S - (KT - 1) * P, KT - 1, :], ins["ctx"][0, (KT - 1) * P:S, :])\
                        .then_inc(ctx_tok_loaded, 16)

                @block.gpsimd
                def _(pool):
                    nc.gpsimd.memset(ctx_tok[:, KT - 1, :], 0.0).then_inc(tail_cleared, 1)

            layernorm(nc, norm_sems, 0, x_res, ident, xn_t)
            self_attention_0(nc, sems, x_res, xn_t, ident, masks, ins["w_heads"])
            layernorm(nc, norm_sems, 1, x_res, ident, xn_t)
            cross_attention_0(nc, sems, x_res, xn_t, ident, ones, ctx_t, ctx_tok, ctx_loaded, ctx_tok_loaded, ins)

        layernorm(nc, norm_sems, 2, x_res, ident, xn_t)
        experts(nc, sems, x_res, xn_t, consts, ins)
        with Phase(nc, sems, "la_in") as la:
            xn_tok = la.sb("xn_tok", [P, TT, D])
            layernorm(nc, norm_sems, 3, x_res, ident, xn_t, xn_tok)
            linear_attention(nc, sems, x_res, xn_t, xn_tok, consts, ins)

        layernorm(nc, norm_sems, 4, x_res, ident, xn_t)
        cross_attention_1(nc, sems, x_res, xn_t, consts, ins)
        with Phase(nc, sems, "bl_in") as bl:
            xn_tok = bl.sb("xn_tok", [P, TT, D])
            layernorm(nc, norm_sems, 5, x_res, ident, xn_t, xn_tok)
            bit_linear_ffn(nc, sems, x_res, xn_tok, consts, ins)

        with ph.block() as block:

            @block.sync
            def _(sp):
                sp.dma_start(out.rearrange("a (i p) d -> p (a i) d", p=P), x_res[:, :, :]).then_inc(stored, 16)
                sp.wait_ge(stored, 16)


def layouts(np, given):
    a = {"x": given["x"]}
    turn = lambda w: np.transpose(w, (0, 2, 1))
    q, k = turn(given["L0_attn_Q"]), turn(given["L0_attn_K"])
    a["w_heads"] = np.concatenate([q, q, k, k, given["L0_attn_VO"]], axis=2)
    a["ident"] = np.eye(P, dtype=np.float32)
    masks = np.zeros((P, 8), np.float32)
    masks[64:, 0] = -1.0
    for head in range(0, P, 32):
        masks[head + 16:head + 24, 1] = -1.0
        masks[head + 8:head + 16, 2] = -1.0
        masks[head + 24:head + 26, 2] = 1.0
        masks[head + 24:head + 26, 3] = 1.0
    a["masks"] = masks
    a["ones"] = np.ones((P, P), np.float32)
    a["places"] = np.tile(np.arange(8, dtype=np.float32), (P, 1))
    a["ctx"] = given["ctx_1024"]
    ctx = given["ctx_1024"][0]
    a["ctx_t"] = np.concatenate([ctx, ctx[:KT * P - S]]).T
    a["w_gate"] = given["L0_xattn_Wg"]
    a["b_gate"] = given["L0_xattn_bg"].reshape(D, 1)
    a["w_ca0_out"] = given["L0_xattn_Wo"]
    a["b_ca0_out"] = given["L0_xattn_bo"].reshape(1, D)
    a["router"] = given["L0_ffn_router_w"]
    a["w_moe_in"] = np.concatenate([given["L0_ffn_gate_proj"], given["L0_ffn_up_proj"]], axis=2)
    down = given["L0_ffn_down_proj"]
    padded = np.zeros((down.shape[0], 3 * P, D), np.float32)
    padded[:, :down.shape[1]] = down
    a["w_moe_down"] = padded.reshape(-1, 3, P, D).transpose(0, 2, 1, 3)
    by_head = lambda w: w.reshape(D, HEADS, -1).transpose(2, 1, 0)
    a["w_la_v"] = by_head(given["L1_attn_Wv"])
    a["w_la_q"] = by_head(given["L1_attn_Wq"])
    a["w_la_o"] = given["L1_attn_Wo"].reshape(HEADS, -1, D).transpose(1, 0, 2)
    a["w_la_k"] = given["L1_attn_Wk"]
    a["b_la_v"] = given["L1_attn_bv"].reshape(HEADS, -1).T
    a["b_la_q"] = given["L1_attn_bq"].reshape(HEADS, -1).T
    a["b_la_k"] = given["L1_attn_bk"].reshape(1, -1)
    a["b_la_o"] = given["L1_attn_bo"].reshape(1, -1)

    def in_rows(w):
        by = w.T.reshape(D, 4, 4, 1, 8)
        return np.concatenate([by, by, by, np.zeros_like(by)], axis=3).reshape(D, 4, P)

    a["w_ca1_q"] = in_rows(given["L1_xattn_Wq"]).transpose(1, 0, 2)
    a["w_ca1_k"] = in_rows(given["L1_xattn_Wk"])
    a["w_ca1_v"] = given["L1_xattn_Wv"].T
    a["w_ca1_o"] = given["L1_xattn_Wo"].T
    a["w_bl1"] = given["L1_ffn_w1"].T
    a["w_bl2"] = given["L1_ffn_w2"].T.reshape(-1, P, D).transpose(1, 0, 2)
    a["b_bl1"] = given["L1_ffn_b1"].reshape(1, -1)
    a["b_bl2"] = given["L1_ffn_b2"].reshape(1, -1)
    return a


def kernel(**inputs):
    import numpy as np
    import concourse.bacc as bacc
    from concourse.bass_utils import run_bass_kernel_spmd

    given = {k: np.asarray(v) for k, v in inputs.items()}
    arrays = {f"in_{k}": np.ascontiguousarray(v) for k, v in layouts(np, given).items()}
    nc = bacc.Bacc("TRN2", target_bir_lowering=False, num_devices=1)
    ins = {k[3:]: nc.dram_tensor(k, v.shape, mybir.dt.from_np(v.dtype), kind="ExternalInput").ap()
           for k, v in arrays.items()}
    out = nc.dram_tensor("out_x", (1, T, D), F32, kind="ExternalOutput").ap()
    program(nc, ins, out)
    result = run_bass_kernel_spmd(nc, [arrays], core_ids=[0])
    return result.results[0]["out_x"]
```

```python
from contextlib import ExitStack

import concourse.bass as bass
from concourse import mybir

F32 = mybir.dt.float32
F32R = mybir.dt.float32r
BF16 = mybir.dt.bfloat16
U32 = mybir.dt.uint32
ALU = mybir.AluOpType
ACT = mybir.ActivationFunctionType
AX = mybir.AxisListType.X

P = 128
BANK = 512
T = 1024
D = 128
TT = T // P
S = 6404
KT = -(-S // P)
HEADS = 16
LN_EPS = 1e-5


class Phase:

    def __init__(self, nc, sems, prefix):
        self.nc, self.sems, self.prefix = nc, sems, prefix
        self.stack = ExitStack()

    def __enter__(self):
        self.stack.__enter__()
        return self

    def __exit__(self, *exc):
        return self.stack.__exit__(*exc)

    def sb(self, name, shape, dtype=F32):
        return self.stack.enter_context(self.nc.sbuf_tensor(f"{self.prefix}_{name}", shape, dtype))

    def ps(self, name, shape):
        return self.stack.enter_context(self.nc.psum_tensor(f"{self.prefix}_{name}", shape, F32))

    def sem(self, name):
        return self.sems.enter_context(self.nc.semaphore(f"{self.prefix}_{name}"))

    def block(self):
        return self.nc.Block()


class Chain:

    def __init__(self, engine, sem, count=0):
        self.engine, self.sem, self.count = engine, sem, count

    def __call__(self, instruction):
        self.count += 1
        instruction.then_inc(self.sem, 1)
        self.engine.wait_ge(self.sem, self.count)


NORM_SEMS = ("chain", "var_ready", "std_ready", "normed_ready", "turned_ready")
NORM_STEPS = 10


def layernorm(nc, norm_sems, n, x_res, ident, xn_t, xn_tok=None):
    chain_sem, var_ready, std_ready, normed_ready, turned_ready = norm_sems
    with Phase(nc, None, f"norm{n}") as ph:
        centred = ph.sb("centred", [P, TT, D])
        squares = ph.sb("squares", [P, TT, D])
        normed = xn_tok if xn_tok is not None else ph.sb("normed", [P, TT, D])
        total = ph.sb("total", [P, TT])
        mean = ph.sb("mean", [P, TT])
        sum_sq = ph.sb("sum_sq", [P, TT])
        var = ph.sb("var", [P, TT])
        std = ph.sb("std", [P, TT])
        rstd = ph.sb("rstd", [P, TT])
        newton = ph.sb("newton", [P, TT])
        newton2 = ph.sb("newton2", [P, TT])
        newton3 = ph.sb("newton3", [P, TT])
        rstd2 = ph.sb("rstd2", [P, TT])
        turned = [ph.ps(f"turned{b}", [P, BANK]) for b in range(2)]

        def wide(stat):
            return stat[:, :].unsqueeze(2).to_broadcast([P, TT, D])

        with ph.block() as block:

            @block.vector
            def _(dve):
                step = Chain(dve, chain_sem, n * NORM_STEPS)
                step(nc.vector.tensor_reduce(total[:, :], x_res[:, :, :], AX, ALU.add))
                step(nc.vector.tensor_scalar(mean[:, :], total[:, :], 1.0 / D, None, ALU.mult))
                step(nc.vector.tensor_tensor(centred[:, :, :], x_res[:, :, :], wide(mean), ALU.subtract))
                step(nc.vector.tensor_tensor(squares[:, :, :], centred[:, :, :], centred[:, :, :], ALU.mult))
                step(nc.vector.tensor_reduce(sum_sq[:, :], squares[:, :, :], AX, ALU.add))
                nc.vector.tensor_scalar(var[:, :], sum_sq[:, :], 1.0 / D, LN_EPS, ALU.mult, ALU.add)\
                    .then_inc(var_ready, 1)
                dve.wait_ge(std_ready, n + 1)
                step(nc.vector.reciprocal(rstd[:, :], std[:, :]))
                step(nc.vector.tensor_tensor(newton[:, :], rstd[:, :], rstd[:, :], ALU.mult))
                step(nc.vector.tensor_tensor(newton2[:, :], newton[:, :], var[:, :], ALU.mult))
                step(nc.vector.tensor_scalar(newton3[:, :], newton2[:, :], -0.5, 1.5, ALU.mult, ALU.add))
                step(nc.vector.tensor_tensor(rstd2[:, :], rstd[:, :], newton3[:, :], ALU.mult))
                nc.vector.tensor_tensor(normed[:, :, :], centred[:, :, :], wide(rstd2), ALU.mult)\
                    .then_inc(normed_ready, 1)
                dve.wait_ge(turned_ready, n * 2 + 1)
                assert step.count == (n + 1) * NORM_STEPS
                nc.vector.tensor_copy(xn_t[:, 0:BANK], turned[0][:, :])

            @block.scalar
            def _(act):
                act.wait_ge(var_ready, n + 1)
                nc.scalar.activation(std[:, :], var[:, :], ACT.Sqrt).then_inc(std_ready, 1)
                act.wait_ge(turned_ready, n * 2 + 2)
                nc.scalar.activation(xn_t[:, BANK:T], turned[1][:, :], ACT.Copy)

            @block.tensor
            def _(pe):
                pe.wait_ge(normed_ready, n + 1)
                for i in range(TT):
                    turn = nc.tensor.transpose(turned[i // 4][:, i % 4 * P:(i % 4 + 1) * P],
                                               normed[:, i, :], ident[:, :])
                    if i % 4 == 3:
                        turn.then_inc(turned_ready, 1)


def self_attention_0(nc, sems, x_res, xn_t, ident, masks, w_heads):
    scale = float(D) ** -0.5
    with Phase(nc, sems, "sa0") as ph:
        w = [ph.sb(f"w{b}", [P, 3 * P]) for b in range(2)]
        q_round = ph.sb("q_round", [P, BANK], F32R)
        q_stack = [ph.sb(f"q_stack{b}", [P, T], F32R) for b in range(2)]
        k_hi = [ph.sb(f"k_hi{b}", [P, T], F32R) for b in range(2)]
        k_lo = [ph.sb(f"k_lo{b}", [P, T], F32R) for b in range(2)]
        values = [ph.sb(f"values{b}", [P, TT, D]) for b in range(2)]
        probs = [ph.sb(f"probs{b}", [P, T]) for b in range(2)]
        probs_t = ph.sb("probs_t", [P, T])
        neg_max = [ph.sb(f"neg_max{b}", [P, 1]) for b in range(2)]
        den = [ph.sb(f"den{b}", [P, 1]) for b in range(2)]
        inv_den = [ph.sb(f"inv_den{b}", [P, 1]) for b in range(2)]
        ps_scores = [ph.ps(f"ps_scores{b}", [P, T]) for b in range(2)]
        ps_turn = [ph.ps(f"ps_turn{b}", [P, BANK]) for b in range(2)]
        ps_out = ph.ps("ps_out", [P, D])
        ps_prep = ph.ps("ps_prep", [P, BANK])
        w_loaded = [ph.sem(f"w_loaded{b}") for b in range(2)]
        prep_ready = ph.sem("prep_ready")
        prep_rounded = ph.sem("prep_rounded")
        prep_done = ph.sem("prep_done")
        scores_ready = ph.sem("scores_ready")
        max_ready = ph.sem("max_ready")
        exp_done = ph.sem("exp_done")
        turned = [ph.sem(f"turned{b}") for b in range(2)]
        probs_t_ready = [ph.sem(f"probs_t_ready{b}") for b in range(2)]
        inv_ready = ph.sem("inv_ready")
        pv_done = ph.sem("pv_done")
        out_added = ph.sem("out_added")

        PIECES = 6
        PAIRS = HEADS // 2

        def rounds(u):
            return u % TT, u // TT

        with ph.block() as block:

            @block.sync
            def _(sp):
                for h in range(2):
                    sp.dma_start(w[h][:, :], w_heads[h]).then_inc(w_loaded[h], 16)
                with sp.Fori(1, PAIRS) as i:
                    for b in range(2):
                        sp.wait_ge(prep_done, i * (2 * PIECES) + PIECES * (b - 1))
                        sp.dma_start(w[b][:, :], w_heads[bass.ds(i * 2 + b, 1)].rearrange("a d n -> (a d) n"))\
                            .then_inc(w_loaded[b], 16)

            @block.tensor
            def _(pe):
                def piece(k, slot, count):
                    pe.wait_ge(prep_done, count + k)
                    if k < 4:
                        half = k % 2 * BANK
                        nc.tensor.matmul(ps_prep[:, :], w[slot][:, k // 2 * P:(k // 2 + 1) * P],
                                         xn_t[:, half:half + BANK], start=True, stop=True)\
                            .then_inc(prep_ready, 1)
                    else:
                        for j in range(4):
                            ut = (k - 4) * 4 + j
                            last = nc.tensor.matmul(ps_prep[:, j * P:(j + 1) * P], xn_t[:, ut * P:(ut + 1) * P],
                                                    w[slot][:, 2 * P:3 * P], start=True, stop=True)
                        last.then_inc(prep_ready, 1)

                def scores(n, u, first=False):
                    q, slot = rounds(u % (2 * TT))
                    if not first:
                        pe.wait_ge(exp_done, n - 1)
                    buf = ps_scores[u % 2]
                    for half in range(2):
                        cut = slice(half * BANK, (half + 1) * BANK)
                        for m, keys in enumerate((k_hi, k_lo)):
                            last = nc.tensor.matmul(buf[:, cut], q_stack[slot][:, q * P:(q + 1) * P],
                                                    keys[slot][:, cut], start=(m == 0), stop=(m == 1))
                    last.then_inc(scores_ready, 1)

                def turn(n, u):
                    pe.wait_ge(exp_done, n + 1)
                    for j in range(TT):
                        if j % 4 == 0:
                            pe.wait_ge(probs_t_ready[j // 4], n + 1)
                        last = nc.tensor.transpose(ps_turn[j // 4][:, j % 4 * P:(j % 4 + 1) * P],
                                                   probs[u % 2][:, j * P:(j + 1) * P], ident[:, :])
                        if j % 4 == 3:
                            last.then_inc(turned[j // 4], 1)

                def times_values(n, u):
                    slot = u // TT
                    pe.wait_ge(out_added, n + 1)
                    for j in range(TT):
                        if j % 4 == 0:
                            pe.wait_ge(probs_t_ready[j // 4], n + 2)
                        last = nc.tensor.matmul(ps_out[:, :], probs_t[:, j * P:(j + 1) * P], values[slot][:, j, :],
                                                start=(j == 0), stop=(j == TT - 1))
                    last.then_inc(pv_done, 1)

                def pair(i, final):
                    for u in range(2 * TT):
                        n = i * (2 * TT) + u
                        turn(n, u)
                        if not (final and u + 2 >= 2 * TT):
                            if u in (TT - 2, 2 * TT - 2):
                                pe.wait_ge(prep_done, i * (2 * PIECES) + PIECES * (u // TT + 1) + 4)
                            scores(n + 2, u + 2)
                        if u % TT < PIECES and not (final and u >= TT):
                            if u == 0:
                                pe.wait_ge(w_loaded[1], i * 16 + 16)
                            if u == TT:
                                pe.wait_ge(w_loaded[0], i * 16 + 32)
                            piece(u % TT, 1 - u // TT, i * (2 * PIECES) + PIECES * (u // TT + 1))
                        times_values(n, u)

                pe.wait_ge(w_loaded[0], 16)
                for k in range(PIECES):
                    if k == 0:
                        nc.tensor.matmul(ps_prep[:, :], w[0][:, 0:P], xn_t[:, 0:BANK], start=True, stop=True)\
                            .then_inc(prep_ready, 1)
                    else:
                        piece(k, 0, 0)
                pe.wait_ge(prep_done, 4)
                scores(0, 0, first=True)
                scores(1, 1, first=True)
                pe.wait_ge(prep_done, PIECES)
                with pe.Fori(0, PAIRS - 1) as i:
                    pair(i, False)
                pair(PAIRS - 1, True)

            @block.scalar
            def _(act):
                act.sem_inc(probs_t_ready[1], 1)

                def exp(n, u):
                    act.wait_ge(max_ready, n + 1)
                    nc.scalar.activation(probs[u % 2][:, :], ps_scores[u % 2][:, :], ACT.Exp,
                                         bias=neg_max[u % 2][:, :], accum_out=den[u % 2][:, :])\
                        .then_inc(exp_done, 1)

                def round_piece(k, slot, count):
                    act.wait_ge(prep_ready, count + k + 1)
                    half = slice(k % 2 * BANK, (k % 2 + 1) * BANK)
                    if k < 2:
                        nc.scalar.activation(q_round[:, :], ps_prep[:, :], ACT.Copy).then_inc(prep_rounded, 1)
                    else:
                        nc.scalar.activation(k_hi[slot][:, half], ps_prep[:, :], ACT.Copy, scale=scale)\
                            .then_inc(prep_rounded, 1)

                def pair(i, final):
                    for u in range(2 * TT):
                        n = i * (2 * TT) + u
                        act.wait_ge(turned[1], n + 1)
                        nc.scalar.activation(probs_t[:, BANK:T], ps_turn[1][:, :], ACT.Copy)\
                            .then_inc(probs_t_ready[1], 1)
                        if u % TT < 4 and not (final and u >= TT):
                            round_piece(u % TT, 1 - u // TT, i * (2 * PIECES) + PIECES * (u // TT + 1))
                        if not (final and u + 2 >= 2 * TT):
                            exp(n + 2, u + 2)

                for k in range(4):
                    round_piece(k, 0, 0)
                exp(0, 0)
                exp(1, 1)
                with act.Fori(0, PAIRS - 1) as i:
                    pair(i, False)
                pair(PAIRS - 1, True)

            @block.vector
            def _(dve):
                dve.sem_inc(probs_t_ready[0], 1)
                dve.sem_inc(out_added, 1)

                def top(n, u):
                    dve.wait_ge(scores_ready, n + 1)
                    nc.vector.tensor_reduce(neg_max[u % 2][:, :], ps_scores[u % 2][:, :], AX, ALU.max, negate=True)\
                        .then_inc(max_ready, 1)

                def rest_piece(k, slot, rounded, ready):
                    half = slice(k % 2 * BANK, (k % 2 + 1) * BANK)
                    if k < 4:
                        dve.wait_ge(prep_rounded, rounded + k + 1)
                    else:
                        dve.wait_ge(prep_ready, ready + k + 1)
                    if k < 2:
                        out = nc.vector.scalar_tensor_tensor(
                            q_stack[slot][:, half], q_round[:, :].bitcast(F32), masks[:, 0:1], ps_prep[:, :],
                            ALU.mult, ALU.add)
                    elif k < 4:
                        out = nc.vector.scalar_tensor_tensor(
                            k_lo[slot][:, half], ps_prep[:, :], scale, k_hi[slot][:, half].bitcast(F32),
                            ALU.mult, ALU.subtract)
                    else:
                        ut = (k - 4) * 4
                        out = nc.vector.tensor_copy(values[slot][:, ut:ut + 4, :],
                                                    ps_prep[:, :].rearrange("p (a d) -> p a d", a=4))
                    out.then_inc(prep_done, 1)

                def pair(i, final):
                    for u in range(2 * TT):
                        n = i * (2 * TT) + u
                        dve.wait_ge(turned[0], n + 1)
                        nc.vector.tensor_copy(probs_t[:, 0:BANK], ps_turn[0][:, :]).then_inc(probs_t_ready[0], 1)
                        nc.vector.reciprocal(inv_den[u % 2][:, :], den[u % 2][:, :]).then_inc(inv_ready, 1)
                        if not (final and u + 2 >= 2 * TT):
                            top(n + 2, u + 2)
                        if u % TT < PIECES and not (final and u >= TT):
                            rest_piece(u % TT, 1 - u // TT, i * 8 + 4 * (u // TT + 1),
                                       i * (2 * PIECES) + PIECES * (u // TT + 1))
                        dve.wait_ge(pv_done, n + 1)
                        dve.wait_ge(inv_ready, n + 1)
                        nc.vector.scalar_tensor_tensor(x_res[:, u % TT, :], ps_out[:, :], inv_den[u % 2][:, :],
                                                       x_res[:, u % TT, :], ALU.mult, ALU.add)\
                            .then_inc(out_added, 1)

                for k in range(PIECES):
                    rest_piece(k, 0, 0, 0)
                top(0, 0)
                top(1, 1)
                with dve.Fori(0, PAIRS - 1) as i:
                    pair(i, False)
                pair(PAIRS - 1, True)


def cross_attention_0(nc, sems, x_res, xn_t, ident, ones, ctx_t, ctx_tok, ctx_loaded, ctx_tok_loaded, ins):
    CHUNKS = -(-S // BANK)
    TAIL = S - (CHUNKS - 1) * BANK
    TAIL_TILES = -(-TAIL // P)
    PROB_RING = 3
    assert (CHUNKS - 1) % PROB_RING == 0
    with Phase(nc, sems, "ca0") as ph:
        w_gate = ph.sb("w_gate", [P, D])
        b_gate = ph.sb("b_gate", [P, 1])
        w_out = ph.sb("w_out", [P, D])
        b_out = ph.sb("b_out", [1, D])
        gate_hi = ph.sb("gate_hi", [P, S], F32R)
        gate_lo = ph.sb("gate_lo", [P, S], F32R)
        xn_hi = ph.sb("xn_hi", [P, T], F32R)
        xn_lo = ph.sb("xn_lo", [P, T], F32R)
        q_hi = ph.sb("q_hi", [P, P], F32R)
        q_lo = ph.sb("q_lo", [P, P], F32R)
        scores = ph.sb("scores", [P, S])
        probs = [ph.sb(f"probs{b}", [P, BANK]) for b in range(PROB_RING)]
        probs_tail = ph.sb("probs_tail", [P, TAIL_TILES * P])
        probs_t = [ph.sb(f"probs_t{b}", [P, BANK]) for b in range(2)]
        chunk_max = ph.sb("chunk_max", [P, CHUNKS])
        chunk_den = ph.sb("chunk_den", [P, CHUNKS])
        neg_max = ph.sb("neg_max", [P, 1])
        den = ph.sb("den", [P, 1])
        inv_den = ph.sb("inv_den", [P, 1])
        attended = ph.sb("attended", [P, TT, D])
        attended_t = ph.sb("attended_t", [P, T])
        ps_scores = [ph.ps(f"ps_scores{b}", [P, BANK]) for b in range(2)]
        ps_turn = [ph.ps(f"ps_turn{b}", [P, BANK]) for b in range(2)]
        ps_out = ph.ps("ps_out", [P, D])
        ps_proj = [ph.ps(f"ps_proj{b}", [P, BANK]) for b in range(2)]
        loaded = ph.sem("loaded")
        gate_ready = ph.sem("gate_ready")
        gate_rounded = ph.sem("gate_rounded")
        gate_done = ph.sem("gate_done")
        split_hi = ph.sem("split_hi")
        split_done = ph.sem("split_done")
        tail_cleared = ph.sem("tail_cleared")
        q_ready = ph.sem("q_ready")
        scores_ready = ph.sem("scores_ready")
        scores_kept = ph.sem("scores_kept")
        chunk_max_ready = ph.sem("chunk_max_ready")
        max_ready = ph.sem("max_ready")
        exp_done = ph.sem("exp_done")
        turned = ph.sem("turned")
        probs_t_ready = ph.sem("probs_t_ready")
        pv_done = ph.sem("pv_done")
        den_ready = ph.sem("den_ready")
        inv_ready = ph.sem("inv_ready")
        attended_ready = ph.sem("attended_ready")
        out_turned = ph.sem("out_turned")
        attended_t_ready = [ph.sem(f"attended_t_ready{b}") for b in range(2)]
        projected = ph.sem("projected")

        def width(c):
            return BANK if c < CHUNKS - 1 else TAIL

        def prob_tile(c):
            return probs[c % PROB_RING] if c < CHUNKS - 1 else probs_tail

        def tiles(c):
            return 4 if c < CHUNKS - 1 else TAIL_TILES

        with ph.block() as block:

            @block.sync
            def _(sp):
                sp.dma_start(w_gate[:, :], ins["w_gate"]).then_inc(loaded, 16)
                sp.dma_start(b_gate[:, :], ins["b_gate"]).then_inc(loaded, 16)
                sp.dma_start(w_out[:, :], ins["w_ca0_out"]).then_inc(loaded, 16)
                sp.dma_start(b_out[:, :], ins["b_ca0_out"]).then_inc(loaded, 16)

            @block.tensor
            def _(pe):
                def gate(n, b, at, w):
                    nc.tensor.matmul(ps_scores[b][:, 0:w], w_gate[:, :], ctx_t[:, at], start=True, stop=True)\
                        .then_inc(gate_ready, 1)

                def score(t, c, first=False):
                    if c == 0:
                        pe.wait_ge(q_ready, t + 1)
                    if c != 1 and not (first and c < 2):
                        pe.wait_ge(scores_kept, t * CHUNKS + (c - 1 if c else 0))
                    w, at = width(c), slice(c * BANK, c * BANK + width(c))
                    for m, (q, g) in enumerate(((q_hi, gate_hi), (q_hi, gate_lo), (q_lo, gate_hi))):
                        last = nc.tensor.matmul(ps_scores[c % 2][:, 0:w], q[:, :], g[:, at],
                                                start=(m == 0), stop=(m == 2))
                    last.then_inc(scores_ready, 1)

                def turn(t, c):
                    pe.wait_ge(exp_done, t * CHUNKS + c + 1)
                    if c != 1:
                        pe.wait_ge(probs_t_ready, t * CHUNKS + (c if c else 1))
                    for j in range(tiles(c)):
                        last = nc.tensor.transpose(ps_turn[c % 2][:, j * P:(j + 1) * P],
                                                   prob_tile(c)[:, j * P:(j + 1) * P], ident[:, :])
                    last.then_inc(turned, 1)

                def times_context(t, c):
                    pe.wait_ge(probs_t_ready, t * CHUNKS + c + 2)
                    if c == 0:
                        pe.wait_ge(attended_ready, t + 1)
                    for j in range(tiles(c)):
                        last = nc.tensor.matmul(ps_out[:, :], probs_t[c % 2][:, j * P:(j + 1) * P],
                                                ctx_tok[:, c * 4 + j, :], start=(c == 0 and j == 0),
                                                stop=(c == CHUNKS - 1 and j == TAIL_TILES - 1))
                    if c == CHUNKS - 1:
                        last.then_inc(pv_done, 1)

                pe.wait_ge(loaded, 64)
                pe.wait_ge(ctx_loaded, 16)
                pe.wait_ge(ctx_tok_loaded, 32)
                gate(0, 0, slice(0, BANK), BANK)
                gate(1, 1, slice(BANK, 2 * BANK), BANK)
                with pe.Fori(1, CHUNKS // 2) as i:
                    for b in range(2):
                        pe.wait_ge(gate_done, i * 2 + (b - 1))
                        gate(i * 2 + b, b, bass.ds(i * (2 * BANK) + b * BANK, BANK), BANK)
                pe.wait_ge(gate_done, CHUNKS - 2)
                gate(CHUNKS - 1, 0, slice((CHUNKS - 1) * BANK, S), TAIL)
                pe.wait_ge(gate_done, CHUNKS)
                for c in range(CHUNKS):
                    score(0, c, first=True)
                with pe.Fori(0, TT - 1) as t:
                    for c in range(CHUNKS):
                        turn(t, c)
                        if c == 0:
                            score(t + 1, 0)
                        if c + 1 < CHUNKS:
                            score(t + 1, c + 1)
                        if c:
                            times_context(t, c - 1)
                    times_context(t, CHUNKS - 1)
                for c in range(CHUNKS):
                    turn(TT - 1, c)
                    if c:
                        times_context(TT - 1, c - 1)
                times_context(TT - 1, CHUNKS - 1)
                pe.wait_ge(attended_ready, TT + 1)
                for i in range(TT):
                    last = nc.tensor.transpose(ps_turn[i // 4][:, i % 4 * P:(i % 4 + 1) * P],
                                               attended[:, i, :], ident[:, :])
                    if i % 4 == 3:
                        last.then_inc(out_turned, 1)
                for half in range(2):
                    pe.wait_ge(attended_t_ready[half], 1)
                    for j in range(4):
                        i = half * 4 + j
                        nc.tensor.matmul(ps_proj[half][:, j * P:(j + 1) * P], attended_t[:, i * P:(i + 1) * P],
                                         w_out[:, :], start=True, stop=False)
                        last = nc.tensor.matmul(ps_proj[half][:, j * P:(j + 1) * P], ones[0:1, :],
                                                b_out[:, :], start=False, stop=True)
                    last.then_inc(projected, 1)

            @block.scalar
            def _(act):
                def round_gate(n, b, at, w):
                    act.wait_ge(gate_ready, n + 1)
                    nc.scalar.activation(gate_hi[:, at], ps_scores[b][:, 0:w], ACT.Identity, bias=b_gate[:, :])\
                        .then_inc(gate_rounded, 1)

                def keep(t, c, first=False):
                    act.wait_ge(scores_ready, t * CHUNKS + c + 1)
                    if not first:
                        act.wait_ge(exp_done, t * CHUNKS + (c + 1 - CHUNKS))
                    w, at = width(c), slice(c * BANK, c * BANK + width(c))
                    nc.scalar.activation(scores[:, at], ps_scores[c % 2][:, 0:w], ACT.Copy).then_inc(scores_kept, 1)

                def exp(t, c, first=False):
                    if c == 0:
                        act.wait_ge(max_ready, t + 1)
                    if c == CHUNKS - 1:
                        if not first:
                            act.wait_ge(turned, t * CHUNKS)
                    elif c >= PROB_RING:
                        act.wait_ge(turned, t * CHUNKS + (c - PROB_RING + 1))
                    elif not first:
                        act.wait_ge(turned, t * CHUNKS + (c - PROB_RING))
                    w, at = width(c), slice(c * BANK, c * BANK + width(c))
                    nc.scalar.activation(prob_tile(c)[:, 0:w], scores[:, at], ACT.Exp, bias=neg_max[:, :],
                                         accum_out=chunk_den[:, c:c + 1]).then_inc(exp_done, 1)

                nc.scalar.activation(xn_hi[:, :], xn_t[:, :], ACT.Copy).then_inc(split_hi, 1)
                act.wait_ge(loaded, 64)
                with act.Fori(0, CHUNKS // 2) as i:
                    for b in range(2):
                        round_gate(i * 2 + b, b, bass.ds(i * (2 * BANK) + b * BANK, BANK), BANK)
                round_gate(CHUNKS - 1, 0, slice((CHUNKS - 1) * BANK, S), TAIL)
                act.wait_ge(tail_cleared, 1)
                for c in range(CHUNKS):
                    keep(0, c, first=True)

                def tile(t, first):
                    exp(t, 0, first)
                    exp(t, 1, first)
                    for c in range(CHUNKS):
                        if c == 0:
                            keep(t + 1, 0)
                        if c + 2 < CHUNKS:
                            exp(t, c + 2, first)
                        if c + 1 < CHUNKS:
                            keep(t + 1, c + 1)

                tile(0, True)
                with act.Fori(1, TT - 1) as t:
                    tile(t, False)
                for c in range(CHUNKS):
                    exp(TT - 1, c)
                act.wait_ge(out_turned, 2)
                nc.scalar.activation(attended_t[:, BANK:T], ps_turn[1][:, :], ACT.Copy).then_inc(attended_t_ready[1], 1)

            @block.vector
            def _(dve):
                dve.sem_inc(probs_t_ready, 1)
                dve.sem_inc(attended_ready, 1)

                def rest_gate(n, b, at, w):
                    dve.wait_ge(gate_rounded, n + 1)
                    nc.vector.scalar_tensor_tensor(gate_lo[:, at], ps_scores[b][:, 0:w], b_gate[:, :],
                                                   gate_hi[:, at].bitcast(F32), ALU.add, ALU.subtract)\
                        .then_inc(gate_done, 1)

                def top(t, c):
                    w, at = width(c), slice(c * BANK, c * BANK + width(c))
                    dve.wait_ge(scores_kept, t * CHUNKS + c + 1)
                    nc.vector.tensor_reduce(chunk_max[:, c:c + 1], scores[:, at], AX, ALU.max)\
                        .then_inc(chunk_max_ready, 1)

                def top_of_all(t):
                    dve.wait_ge(chunk_max_ready, t * CHUNKS + CHUNKS)
                    nc.vector.tensor_reduce(neg_max[:, :], chunk_max[:, :], AX, ALU.max, negate=True)\
                        .then_inc(max_ready, 1)

                def query(t, first=False):
                    if not first:
                        dve.wait_ge(scores_ready, t * CHUNKS)
                    at = slice(0, P) if first else bass.ds(t * P, P)
                    nc.vector.tensor_copy(q_hi[:, :], xn_hi[:, at].bitcast(F32))
                    nc.vector.tensor_copy(q_lo[:, :], xn_lo[:, at].bitcast(F32)).then_inc(q_ready, 1)

                def copy_turned(t, c):
                    dve.wait_ge(turned, t * CHUNKS + c + 1)
                    w = tiles(c) * P
                    nc.vector.tensor_copy(probs_t[c % 2][:, 0:w], ps_turn[c % 2][:, 0:w]).then_inc(probs_t_ready, 1)

                def invert(t):
                    dve.wait_ge(exp_done, t * CHUNKS + CHUNKS)
                    nc.vector.tensor_reduce(den[:, :], chunk_den[:, :], AX, ALU.add).then_inc(den_ready, 1)
                    dve.wait_ge(den_ready, t + 1)
                    nc.vector.reciprocal(inv_den[:, :], den[:, :]).then_inc(inv_ready, 1)

                def normalise(t, at):
                    dve.wait_ge(pv_done, t + 1)
                    dve.wait_ge(inv_ready, t + 1)
                    nc.vector.tensor_scalar(attended[:, at, :], ps_out[:, :].unsqueeze(1), inv_den[:, :], None, ALU.mult)\
                        .then_inc(attended_ready, 1)

                dve.wait_ge(split_hi, 1)
                nc.vector.tensor_tensor(xn_lo[:, :], xn_t[:, :], xn_hi[:, :].bitcast(F32), ALU.subtract)\
                    .then_inc(split_done, 1)
                nc.vector.memset(probs_tail[:, :], 0.0).then_inc(tail_cleared, 1)
                dve.wait_ge(loaded, 64)
                with dve.Fori(0, CHUNKS // 2) as i:
                    for b in range(2):
                        rest_gate(i * 2 + b, b, bass.ds(i * (2 * BANK) + b * BANK, BANK), BANK)
                rest_gate(CHUNKS - 1, 0, slice((CHUNKS - 1) * BANK, S), TAIL)
                dve.wait_ge(split_done, 1)
                query(0, first=True)
                for c in range(CHUNKS):
                    top(0, c)
                top_of_all(0)
                query(1)

                def tile(t, at):
                    for c in range(CHUNKS):
                        copy_turned(t, c)
                        if c == 0:
                            top(t + 1, 0)
                        if c + 1 < CHUNKS:
                            top(t + 1, c + 1)
                    invert(t)
                    top_of_all(t + 1)
                    normalise(t, at)

                with dve.Fori(0, TT - 2) as t:
                    tile(t, bass.ds(t, 1))
                    query(t + 2)
                tile(TT - 2, slice(TT - 2, TT - 1))
                for c in range(CHUNKS):
                    copy_turned(TT - 1, c)
                invert(TT - 1)
                normalise(TT - 1, slice(TT - 1, TT))
                dve.wait_ge(out_turned, 1)
                nc.vector.tensor_copy(attended_t[:, 0:BANK], ps_turn[0][:, :]).then_inc(attended_t_ready[0], 1)
                for half in range(2):
                    dve.wait_ge(projected, half + 1)
                    cut = slice(half * 4, half * 4 + 4)
                    nc.vector.tensor_tensor(x_res[:, cut, :], x_res[:, cut, :],
                                            ps_proj[half][:, :].rearrange("p (a d) -> p a d", a=4), ALU.add)


def experts(nc, sems, x_res, xn_t, consts, ins):
    E, F = 8, 352
    FT = [(0, P), (P, P), (2 * P, F - 2 * P)]
    UNITS = 2 * len(FT)
    with Phase(nc, sems, "moe") as ph:
        router = ph.sb("router", [P, E])
        w_in = [ph.sb(f"w_in{b}", [P, 2 * F]) for b in range(2)]
        w_down = [ph.sb(f"w_down{b}", [P, len(FT), D]) for b in range(2)]
        logit_max = ph.sb("logit_max", [P, TT])
        shifted = ph.sb("shifted", [P, TT, E])
        expd = ph.sb("expd", [P, TT, E])
        den = ph.sb("den", [P, TT])
        inv_den = ph.sb("inv_den", [P, TT])
        probs = ph.sb("probs", [P, TT, E])
        best = ph.sb("best", [P, TT, 8])
        best_at = ph.sb("best_at", [P, TT, 8], U32)
        best_at_f = ph.sb("best_at_f", [P, TT, 8])
        pair_sum = ph.sb("pair_sum", [P, TT])
        pair_inv = ph.sb("pair_inv", [P, TT])
        chosen_w = ph.sb("chosen_w", [P, TT, 2])
        hit = [ph.sb(f"hit{k}", [P, TT, E]) for k in range(2)]
        hit_w = [ph.sb(f"hit_w{k}", [P, TT, E]) for k in range(2)]
        expert_w = ph.sb("expert_w", [P, TT, E])
        silu = [ph.sb(f"silu{n}", [P, BANK]) for n in range(2)]
        acts = [[ph.sb(f"acts{b}_{f}", [P, T]) for f in range(len(FT))] for b in range(2)]
        ps_gate = [ph.ps(f"ps_gate{n}", [P, BANK]) for n in range(2)]
        ps_up = [ph.ps(f"ps_up{n}", [P, BANK]) for n in range(2)]
        ps_down = [ph.ps(f"ps_down{n}", [P, BANK]) for n in range(2)]
        ps_router = ph.ps("ps_router", [P, TT * E])
        chain_sem = ph.sem("chain")
        router_loaded = ph.sem("router_loaded")
        in_loaded = [ph.sem(f"in_loaded{b}") for b in range(2)]
        down_loaded = [ph.sem(f"down_loaded{b}") for b in range(2)]
        logits_ready = ph.sem("logits_ready")
        shifted_ready = ph.sem("shifted_ready")
        exp_done = ph.sem("exp_done")
        gate_ready = ph.sem("gate_ready")
        up_ready = ph.sem("up_ready")
        silu_done = ph.sem("silu_done")
        acts_done = ph.sem("acts_done")
        down_ready = ph.sem("down_ready")
        down_added = ph.sem("down_added")

        def wide(stat, n):
            return stat.unsqueeze(2).to_broadcast([P, TT, n])

        with ph.block() as block:

            @block.sync
            def _(sp):
                sp.dma_start(router[:, :], ins["router"]).then_inc(router_loaded, 16)

                def load(e, b):
                    at = slice(e, e + 1) if isinstance(e, int) else bass.ds(e, 1)
                    sp.dma_start(w_in[b][:, :], ins["w_moe_in"][at].rearrange("a d f -> (a d) f"))\
                        .then_inc(in_loaded[b], 16)

                def load_down(e, b):
                    at = slice(e, e + 1) if isinstance(e, int) else bass.ds(e, 1)
                    sp.dma_start(w_down[b][:, :, :], ins["w_moe_down"][at].rearrange("a f k d -> (a f) k d"))\
                        .then_inc(down_loaded[b], 16)

                for e in range(2):
                    load(e, e)
                    load_down(e, e)
                with sp.Fori(1, E // 2) as i:
                    for b in range(2):
                        sp.wait_ge(up_ready, i * (2 * UNITS) + UNITS * (b - 1))
                        load(i * 2 + b, b)
                        sp.wait_ge(down_ready, i * 4 + 2 * (b - 1))
                        load_down(i * 2 + b, b)

            @block.tensor
            def _(pe):
                def expert_in(e, b):
                    for f, (start, rows) in enumerate(FT):
                        for n in range(2):
                            count = e * UNITS + 2 * f + n
                            first = isinstance(e, int) and count < 2
                            cols = xn_t[:, n * BANK:(n + 1) * BANK]
                            if not first:
                                pe.wait_ge(silu_done, count - 1)
                            nc.tensor.matmul(ps_gate[n][0:rows, :], w_in[b][:, start:start + rows], cols,
                                             start=True, stop=True).then_inc(gate_ready, 1)
                            if not first:
                                pe.wait_ge(acts_done, count - 1)
                            nc.tensor.matmul(ps_up[n][0:rows, :], w_in[b][:, F + start:F + start + rows], cols,
                                             start=True, stop=True).then_inc(up_ready, 1)

                def expert_out(e, b):
                    pe.wait_ge(acts_done, e * UNITS + UNITS)
                    for half in range(2):
                        if not (isinstance(e, int) and e == 0):
                            pe.wait_ge(down_added, e * 2 + half - 1)
                        for j in range(4):
                            i = half * 4 + j
                            for f, (_, rows) in enumerate(FT):
                                last = nc.tensor.matmul(ps_down[half][:, j * P:(j + 1) * P],
                                                        acts[b][f][0:rows, i * P:(i + 1) * P],
                                                        w_down[b][0:rows, f, :], start=(f == 0), stop=(f == 2))
                        last.then_inc(down_ready, 1)

                pe.wait_ge(router_loaded, 16)
                for i in range(TT):
                    last = nc.tensor.matmul(ps_router[:, i * E:(i + 1) * E], xn_t[:, i * P:(i + 1) * P],
                                            router[:, :], start=True, stop=True)
                last.then_inc(logits_ready, 1)
                pe.wait_ge(in_loaded[0], 16)
                expert_in(0, 0)
                pe.wait_ge(in_loaded[1], 16)
                expert_in(1, 1)
                pe.wait_ge(down_loaded[0], 16)
                expert_out(0, 0)
                with pe.Fori(1, E // 2) as i:
                    for b in range(2):
                        pe.wait_ge(in_loaded[b], i * 16 + 16)
                        expert_in(i * 2 + b, b)
                        pe.wait_ge(down_loaded[1 - b], i * 16 + 16 * b)
                        expert_out(i * 2 + (b - 1), 1 - b)
                pe.wait_ge(down_loaded[1], E // 2 * 16)
                expert_out(E - 1, 1)

            @block.scalar
            def _(act):
                act.wait_ge(shifted_ready, 1)
                nc.scalar.activation(expd[:, :, :], shifted[:, :, :], ACT.Exp).then_inc(exp_done, 1)

                def gates(e):
                    for f, (_, rows) in enumerate(FT):
                        for n in range(2):
                            count = e * UNITS + 2 * f + n
                            act.wait_ge(gate_ready, count + 1)
                            if not (isinstance(e, int) and count < 2):
                                act.wait_ge(acts_done, count - 1)
                            nc.scalar.activation(silu[n][0:rows, :], ps_gate[n][0:rows, :], ACT.Silu)\
                                .then_inc(silu_done, 1)

                gates(0)
                with act.Fori(1, E) as e:
                    gates(e)

            @block.vector
            def _(dve):
                step = Chain(dve, chain_sem)
                logits = ps_router[:, :].rearrange("p (i e) -> p i e", e=E)
                dve.wait_ge(logits_ready, 1)
                step(nc.vector.tensor_reduce(logit_max[:, :], logits, AX, ALU.max))
                nc.vector.tensor_tensor(shifted[:, :, :], logits, wide(logit_max[:, :], E), ALU.subtract)\
                    .then_inc(shifted_ready, 1)
                dve.wait_ge(exp_done, 1)
                step(nc.vector.tensor_reduce(den[:, :], expd[:, :, :], AX, ALU.add))
                step(nc.vector.reciprocal(inv_den[:, :], den[:, :]))
                step(nc.vector.tensor_tensor(probs[:, :, :], expd[:, :, :], wide(inv_den[:, :], E), ALU.mult))
                for i in range(TT):
                    last = nc.vector.max(best[:, i, :], probs[:, i, :])
                step(last)
                for i in range(TT):
                    last = nc.vector.max_index(best_at[:, i, :], best[:, i, :], probs[:, i, :])
                step(last)
                step(nc.vector.tensor_copy(best_at_f[:, :, :], best_at[:, :, :]))
                step(nc.vector.tensor_tensor(pair_sum[:, :], best[:, :, 0], best[:, :, 1], ALU.add))
                step(nc.vector.reciprocal(pair_inv[:, :], pair_sum[:, :]))
                step(nc.vector.tensor_tensor(chosen_w[:, :, :], best[:, :, 0:2], wide(pair_inv[:, :], 2), ALU.mult))
                places = consts["places"][:, :].unsqueeze(1).to_broadcast([P, TT, E])
                for k in range(2):
                    step(nc.vector.tensor_tensor(hit[k][:, :, :], places, wide(best_at_f[:, :, k], E), ALU.is_equal))
                    step(nc.vector.tensor_tensor(hit_w[k][:, :, :], hit[k][:, :, :], wide(chosen_w[:, :, k], E),
                                                 ALU.mult))
                step(nc.vector.tensor_tensor(expert_w[:, :, :], hit_w[0][:, :, :], hit_w[1][:, :, :], ALU.add))

                def products(e, b):
                    for f, (_, rows) in enumerate(FT):
                        for n in range(2):
                            count = e * UNITS + 2 * f + n
                            dve.wait_ge(up_ready, count + 1)
                            dve.wait_ge(silu_done, count + 1)
                            nc.vector.tensor_tensor(acts[b][f][0:rows, n * BANK:(n + 1) * BANK], ps_up[n][0:rows, :],
                                                    silu[n][0:rows, :], ALU.mult).then_inc(acts_done, 1)

                def add(e):
                    for half in range(2):
                        dve.wait_ge(down_ready, e * 2 + half + 1)
                        for j in range(4):
                            i = half * 4 + j
                            at = slice(e, e + 1) if isinstance(e, int) else bass.ds(e, 1)
                            last = nc.vector.scalar_tensor_tensor(
                                x_res[:, i, :], ps_down[half][:, j * P:(j + 1) * P], expert_w[:, i, at],
                                x_res[:, i, :], ALU.mult, ALU.add)
                        last.then_inc(down_added, 1)

                products(0, 0)
                products(1, 1)
                with dve.Fori(1, E // 2) as i:
                    for b in range(2):
                        add(i * 2 + (b - 2))
                        products(i * 2 + b, b)
                add(E - 2)
                add(E - 1)


def linear_attention(nc, sems, x_res, xn_t, xn_tok, consts, ins):
    R = 64
    W = HEADS * D
    scale = float(R) ** -0.5
    with Phase(nc, sems, "la") as ph:
        w_v = ph.sb("w_v", [R, HEADS, D])
        w_o = ph.sb("w_o", [R, HEADS, D])
        w_q = ph.sb("w_q", [R, HEADS, D])
        w_k = ph.sb("w_k", [P, HEADS * R])
        b_v = ph.sb("b_v", [R, HEADS])
        b_q = ph.sb("b_q", [R, HEADS])
        b_k = ph.sb("b_k", [1, HEADS * R])
        b_o = ph.sb("b_o", [1, D])
        tokens = ph.sb("tokens", [1, 1])
        gram = ph.sb("gram", [P, D])
        s_col = ph.sb("s_col", [P, 1])
        s_row = ph.sb("s_row", [1, D])
        c_row = ph.sb("c_row", [1, W])
        vw = ph.sb("vw", [P, W])
        z = ph.sb("z", [P, W])
        z0 = ph.sb("z0", [1, W])
        n_all = ph.sb("n_all", [R, W])
        m_mat = ph.sb("m_mat", [P, D])
        b_row = ph.sb("b_row", [1, D])
        ps_w = ph.ps("ps_w", [P, W])
        ps_r = ph.ps("ps_r", [P, W])
        loaded = ph.sem("loaded")
        const_ready = ph.sem("const_ready")
        gram_ready = ph.sem("gram_ready")
        gram_kept = ph.sem("gram_kept")
        c_ready = ph.sem("c_ready")
        c_kept = ph.sem("c_kept")
        vw_ready = ph.sem("vw_ready")
        vw_kept = [ph.sem(f"vw_kept{b}") for b in range(2)]
        z_ready = ph.sem("z_ready")
        z_kept = ph.sem("z_kept")
        z0_ready = ph.sem("z0_ready")
        z0_kept = ph.sem("z0_kept")
        n_ready = ph.sem("n_ready")
        n_kept = [ph.sem(f"n_kept{b}") for b in range(2)]
        m_ready = ph.sem("m_ready")
        m_kept = ph.sem("m_kept")
        out_ready = ph.sem("out_ready")
        HALF = W // 2

        with ph.block() as block:

            @block.sync
            def _(sp):
                names = (("w_la_v", w_v), ("w_la_o", w_o), ("w_la_q", w_q))
                for name, tile in names:
                    sp.dma_start(tile[:, :, :], ins[name]).then_inc(loaded, 16)
                names = (("w_la_k", w_k), ("b_la_v", b_v), ("b_la_q", b_q), ("b_la_k", b_k), ("b_la_o", b_o))
                for name, tile in names:
                    sp.dma_start(tile[:, :], ins[name]).then_inc(loaded, 16)

            @block.tensor
            def _(pe):
                ones = consts["ones"]
                for i in range(TT):
                    last = nc.tensor.matmul(ps_w[:, 0:D], xn_tok[:, i, :], xn_tok[:, i, :],
                                            start=(i == 0), stop=(i == TT - 1))
                for i in range(TT):
                    last = nc.tensor.matmul(ps_w[:, BANK:BANK + 1], xn_tok[:, i, :], ones[:, 0:1],
                                            start=(i == 0), stop=(i == TT - 1))
                for i in range(TT):
                    last = nc.tensor.matmul(ps_w[0:1, 2 * BANK:2 * BANK + D], ones[:, 0:1], xn_tok[:, i, :],
                                            start=(i == 0), stop=(i == TT - 1))
                last.then_inc(gram_ready, 1)
                pe.wait_ge(loaded, 8 * 16)
                for h in range(HEADS):
                    last = nc.tensor.matmul(ps_r[0:1, h * D:(h + 1) * D], b_v[:, h:h + 1], w_o[:, h, :],
                                            start=True, stop=True)
                last.then_inc(c_ready, 1)
                pe.wait_ge(gram_kept, 1)
                for h in range(HEADS):
                    last = nc.tensor.matmul(ps_w[:, h * D:(h + 1) * D], w_v[:, h, :], w_o[:, h, :],
                                            start=True, stop=True)
                    if h % 8 == 7:
                        last.then_inc(vw_ready, 1)
                pe.wait_ge(c_kept, 1)
                pe.wait_ge(const_ready, 1)
                for b in range(2):
                    pe.wait_ge(vw_kept[b], 1)
                for c in range(W // BANK):
                    cut = slice(c * BANK, (c + 1) * BANK)
                    nc.tensor.matmul(ps_w[:, cut], gram[:, :], vw[:, cut], start=True, stop=False)
                    last = nc.tensor.matmul(ps_w[:, cut], s_row[:, :], c_row[:, cut], start=False, stop=True)
                last.then_inc(z_ready, 1)
                for c in range(W // BANK):
                    cut = slice(c * BANK, (c + 1) * BANK)
                    nc.tensor.matmul(ps_r[0:1, cut], s_col[:, :], vw[:, cut], start=True, stop=False)
                    last = nc.tensor.matmul(ps_r[0:1, cut], tokens[:, :], c_row[:, cut], start=False, stop=True)
                last.then_inc(z0_ready, 1)
                pe.wait_ge(z_kept, 1)
                pe.wait_ge(z0_kept, 1)
                for h in range(HEADS):
                    cut = slice(h * D, (h + 1) * D)
                    nc.tensor.matmul(ps_w[0:R, cut], w_k[:, h * R:(h + 1) * R], z[:, cut], start=True, stop=False)
                    last = nc.tensor.matmul(ps_w[0:R, cut], b_k[:, h * R:(h + 1) * R], z0[:, cut],
                                            start=False, stop=True)
                    if h % 8 == 7:
                        last.then_inc(n_ready, 1)
                for b in range(2):
                    pe.wait_ge(n_kept[b], 1)
                for h in range(HEADS):
                    nc.tensor.matmul(ps_r[:, 0:D], w_q[:, h, :], n_all[:, h * D:(h + 1) * D],
                                     start=(h == 0), stop=(h == HEADS - 1))
                for h in range(HEADS):
                    last = nc.tensor.matmul(ps_r[0:1, BANK:BANK + D], b_q[:, h:h + 1], n_all[:, h * D:(h + 1) * D],
                                            start=(h == 0), stop=(h == HEADS - 1))
                last.then_inc(m_ready, 1)
                pe.wait_ge(m_kept, 1)
                for i in range(TT):
                    nc.tensor.matmul(ps_w[:, i * D:(i + 1) * D], xn_t[:, i * P:(i + 1) * P], m_mat[:, :],
                                     start=True, stop=False)
                    last = nc.tensor.matmul(ps_w[:, i * D:(i + 1) * D], ones[0:1, :], b_row[:, :],
                                            start=False, stop=True)
                last.then_inc(out_ready, 1)

            @block.scalar
            def _(act):
                act.wait_ge(c_ready, 1)
                nc.scalar.activation(c_row[:, :], ps_r[0:1, :], ACT.Copy).then_inc(c_kept, 1)
                act.wait_ge(vw_ready, 2)
                nc.scalar.activation(vw[:, HALF:W], ps_w[:, HALF:W], ACT.Copy).then_inc(vw_kept[1], 1)
                act.wait_ge(z0_ready, 1)
                nc.scalar.activation(z0[:, :], ps_r[0:1, :], ACT.Copy).then_inc(z0_kept, 1)
                act.wait_ge(n_ready, 2)
                nc.scalar.activation(n_all[:, HALF:W], ps_w[0:R, HALF:W], ACT.Copy, scale=scale)\
                    .then_inc(n_kept[1], 1)

            @block.vector
            def _(dve):
                nc.vector.memset(tokens[:, :], float(T)).then_inc(const_ready, 1)
                dve.wait_ge(gram_ready, 1)
                nc.vector.tensor_copy(gram[:, :], ps_w[:, 0:D])
                nc.vector.tensor_copy(s_col[:, :], ps_w[:, BANK:BANK + 1])
                nc.vector.tensor_copy(s_row[:, :], ps_w[0:1, 2 * BANK:2 * BANK + D]).then_inc(gram_kept, 1)
                dve.wait_ge(vw_ready, 1)
                nc.vector.tensor_copy(vw[:, 0:HALF], ps_w[:, 0:HALF]).then_inc(vw_kept[0], 1)
                dve.wait_ge(z_ready, 1)
                nc.vector.tensor_copy(z[:, :], ps_w[:, :]).then_inc(z_kept, 1)
                dve.wait_ge(n_ready, 1)
                nc.vector.tensor_scalar(n_all[:, 0:HALF], ps_w[0:R, 0:HALF], scale, None, ALU.mult)\
                    .then_inc(n_kept[0], 1)
                dve.wait_ge(m_ready, 1)
                nc.vector.tensor_copy(m_mat[:, :], ps_r[:, 0:D])
                nc.vector.tensor_tensor(b_row[:, :], ps_r[0:1, BANK:BANK + D], b_o[:, :], ALU.add)\
                    .then_inc(m_kept, 1)
                dve.wait_ge(out_ready, 1)
                nc.vector.tensor_tensor(x_res[:, :, :], x_res[:, :, :],
                                        ps_w[:, 0:TT * D].rearrange("p (i d) -> p i d", d=D), ALU.add)


def cross_attention_1(nc, sems, x_res, xn_t, consts, ins):
    G, GH, HD, ROWS = 4, 4, 8, 32
    VC = HD + 1
    UNROLL = 3
    ROUNDS = KT // UNROLL
    LAG = 2
    PAIRS = 2 * G
    assert KT % UNROLL == 0
    CHUNKS = ROUNDS
    CH = UNROLL * P
    LAST = S - (KT - 1) * P
    scale = float(D) ** -0.5
    E_RING, M_RING, P_RING, Q_RING = 3, 2, 6, 3
    with Phase(nc, sems, "ca1") as outer:
        q_heads = [outer.sb(f"q_heads{g}", [P, T], F32R) for g in range(G)]
        with Phase(nc, sems, "ca1s") as ph:
            keys = ph.sb("keys", [P, G, KT * P], F32R)
            values = ph.sb("values", [P, KT * HEADS * VC])
            values4 = values[:, :].rearrange("p (k h c) -> p k h c", h=HEADS, c=VC)

            q_diag = [ph.sb(f"q_diag{b}", [P, GH, BANK], F32R) for b in range(Q_RING)]
            neg_max = ph.sb("neg_max", [P, P])
            cleared = ph.sem("cleared")
            q_placed = ph.sem("q_placed")

            def put_on_diagonal(pool, p):
                for j in range(GH):
                    rows = slice(j * ROWS, (j + 1) * ROWS)
                    pool.dma_start(q_diag[p % Q_RING][rows, j, :].bitcast(F32),
                                   q_heads[p // 2][rows, p % 2 * BANK:(p % 2 + 1) * BANK].bitcast(F32))\
                        .then_inc(q_placed, 16)

            with Phase(nc, sems, "ca1k") as kp:
                w_q = kp.sb("w_q", [P, G, P])
                w_k = kp.sb("w_k", [P, G, P])
                w_v = kp.sb("w_v", [P, D])
                ctx = [kp.sb(f"ctx{b}", [P, CH]) for b in range(2)]
                rounded = [kp.sb(f"rounded{g}", [P, BANK], F32R) for g in range(G)]
                ps_k = [kp.ps(f"ps_k{g}", [P, BANK]) for g in range(G)]
                ps_v = [kp.ps(f"ps_v{b}", [P, UNROLL * P]) for b in range(2)]
                w_loaded = kp.sem("w_loaded")
                ctx_loaded = [kp.sem(f"ctx_loaded{b}") for b in range(2)]
                values_set = kp.sem("values_set")
                k_ready = kp.sem("k_ready")
                k_rounded = kp.sem("k_rounded")
                k_done = kp.sem("k_done")
                v_ready = kp.sem("v_ready")
                v_done = kp.sem("v_done")
                with ph.block() as block:

                    @block.sync
                    def _(sp):
                        sp.dma_start(w_q[:, :, :], ins["w_ca1_q"]).then_inc(w_loaded, 16)
                        sp.dma_start(w_k[:, :, :], ins["w_ca1_k"]).then_inc(w_loaded, 16)
                        sp.dma_start(w_v[:, :], ins["w_ca1_v"]).then_inc(w_loaded, 16)

                        def load(b, at):
                            sp.dma_start(ctx[b][:, :], ins["ctx_t"][:, at]).then_inc(ctx_loaded[b], 16)

                        for b in range(2):
                            load(b, slice(b * CH, (b + 1) * CH))
                        with sp.Fori(1, CHUNKS // 2) as i:
                            for b in range(2):
                                sp.wait_ge(v_ready, i * 2 + (b - 1))
                                load(b, bass.ds(i * (2 * CH) + b * CH, CH))
                        sp.wait_ge(v_ready, CHUNKS - 2)
                        load(0, slice((CHUNKS - 1) * CH, CHUNKS * CH))

                    @block.gpsimd
                    def _(pool):
                        nc.gpsimd.memset(values4[:, KT - 1, :, :], 0.0).then_inc(values_set, 1)
                        nc.gpsimd.memset(values4[:, 0:KT - 1, :, HD], 1.0).then_inc(values_set, 1)
                        pool.wait_ge(values_set, 2)
                        nc.gpsimd.memset(values4[0:LAST, KT - 1, :, HD], 1.0).then_inc(values_set, 1)
                        for b in range(Q_RING):
                            nc.gpsimd.memset(q_diag[b][:, :, :].bitcast(F32), 0.0)
                        nc.gpsimd.memset(neg_max[:, :], 0.0).then_inc(cleared, 1)
                        pool.wait_ge(cleared, 1)
                        for p in range(2):
                            pool.wait_ge(k_done, p + 1)
                            put_on_diagonal(pool, p)

                    @block.tensor
                    def _(pe):
                        def chunk(c, b, first=False):
                            for g in range(G):
                                pe.wait_ge(k_done, c * G + (PAIRS + g - (G - 1)))
                                nc.tensor.matmul(ps_k[g][:, 0:CH], w_k[:, g, :], ctx[b][:, :], start=True, stop=True)\
                                    .then_inc(k_ready, 1)
                            if not first:
                                pe.wait_ge(v_done, c - 1)
                            for j in range(UNROLL):
                                last = nc.tensor.matmul(ps_v[b][:, j * P:(j + 1) * P], ctx[b][:, j * P:(j + 1) * P],
                                                        w_v[:, :], start=True, stop=True)
                            last.then_inc(v_ready, 1)

                        pe.wait_ge(w_loaded, 48)
                        for p in range(PAIRS):
                            if p >= G:
                                pe.wait_ge(k_done, p - G + 1)
                            nc.tensor.matmul(ps_k[p % G][:, :], w_q[:, p // 2, :],
                                             xn_t[:, p % 2 * BANK:(p % 2 + 1) * BANK], start=True, stop=True)\
                                .then_inc(k_ready, 1)
                        for b in range(2):
                            pe.wait_ge(ctx_loaded[b], 16)
                            chunk(b, b, first=True)
                        with pe.Fori(1, CHUNKS // 2) as i:
                            for b in range(2):
                                pe.wait_ge(ctx_loaded[b], i * 16 + 16)
                                chunk(i * 2 + b, b)
                        pe.wait_ge(ctx_loaded[0], (CHUNKS // 2 + 1) * 16)
                        chunk(CHUNKS - 1, 0)

                    @block.scalar
                    def _(act):
                        for p in range(PAIRS):
                            act.wait_ge(k_ready, p + 1)
                            if p >= G:
                                act.wait_ge(k_done, p - G + 1)
                            nc.scalar.activation(rounded[p % G][:, :], ps_k[p % G][:, :], ACT.Copy)\
                                .then_inc(k_rounded, 1)
                        with act.Fori(0, CHUNKS) as c:
                            for g in range(G):
                                act.wait_ge(k_ready, c * G + (PAIRS + g + 1))
                                nc.scalar.activation(rounded[g][:, 0:CH], ps_k[g][:, 0:CH], ACT.Identity,
                                                     bias=consts["masks"][:, 3:4]).then_inc(k_rounded, 1)

                    @block.vector
                    def _(dve):
                        def chunk(c, b, tail=False):
                            at = bass.ds(c * CH, CH) if not isinstance(c, int) else slice(c * CH, (c + 1) * CH)
                            for g in range(G):
                                dve.wait_ge(k_rounded, c * G + (PAIRS + g + 1))
                                nc.vector.scalar_tensor_tensor(
                                    keys[:, g, at], rounded[g][:, 0:CH].bitcast(F32), consts["masks"][:, 2:3],
                                    ps_k[g][:, 0:CH], ALU.mult, ALU.add).then_inc(k_done, 1)
                            dve.wait_ge(v_ready, c + 1)
                            split = ps_v[b][:, :].rearrange("p (k h c) -> p k h c", k=UNROLL, c=HD)
                            if tail:
                                nc.vector.tensor_copy(values4[:, KT - UNROLL:KT - 1, :, 0:HD], split[:, 0:UNROLL - 1])
                                nc.vector.tensor_copy(values4[0:LAST, KT - 1, :, 0:HD], split[0:LAST, UNROLL - 1])
                            else:
                                wide = values[:, bass.ds(c * (UNROLL * HEADS * VC), UNROLL * HEADS * VC)]
                                nc.vector.tensor_copy(
                                    wide.rearrange("p (k h c) -> p k h c", h=HEADS, c=VC)[:, :, :, 0:HD], split)\
                                    .then_inc(v_done, 1)

                        for p in range(PAIRS):
                            dve.wait_ge(k_rounded, p + 1)
                            nc.vector.scalar_tensor_tensor(
                                q_heads[p // 2][:, p % 2 * BANK:(p % 2 + 1) * BANK],
                                rounded[p % G][:, :].bitcast(F32), consts["masks"][:, 1:2], ps_k[p % G][:, :],
                                ALU.mult, ALU.add).then_inc(k_done, 1)
                        with dve.Fori(0, CHUNKS // 2) as i:
                            for b in range(2):
                                chunk(i * 2 + b, b)
                        dve.wait_ge(values_set, 3)
                        chunk(CHUNKS - 1, 0, tail=True)

            run_max = ph.sb("run_max", [P, GH, BANK])
            key_tile = [ph.sb(f"key_tile{s}", [P, P], F32R) for s in range(UNROLL)]
            max_key_tile = [ph.sb(f"max_key_tile{s}", [P, P], F32R) for s in range(UNROLL)]
            value_tile = [ph.sb(f"value_tile{s}", [P, GH * VC]) for s in range(UNROLL)]
            probs = [ph.sb(f"probs{r}", [P, BANK]) for r in range(P_RING)]
            max_hi = ph.sb("max_hi", [GH * 4, P], F32R)
            max_lo = ph.sb("max_lo", [GH * 4, P], F32R)
            ps_e = [ph.ps(f"ps_e{r}", [P, BANK]) for r in range(E_RING)]
            ps_m = [ph.ps(f"ps_m{r}", [P, 2, BANK]) for r in range(M_RING)]
            ps_o = ph.ps("ps_o", [P, BANK])
            sums_cleared = ph.sem("sums_cleared")
            key_loaded = [ph.sem(f"key_loaded{s}") for s in range(UNROLL)]
            max_key_loaded = [ph.sem(f"max_key_loaded{s}") for s in range(UNROLL)]
            value_loaded = [ph.sem(f"value_loaded{s}") for s in range(UNROLL)]
            e_ready = ph.sem("e_ready")
            m_ready = ph.sem("m_ready")
            exp_done = ph.sem("exp_done")
            max_done = ph.sem("max_done")
            pv_done = ph.sem("pv_done")
            run_turned = ph.sem("run_turned")
            max_found = ph.sem("max_found")
            max_turned = ph.sem("max_turned")
            hi_ready = ph.sem("hi_ready")
            max_split = ph.sem("max_split")
            max_placed = ph.sem("max_placed")
            heads_kept = ph.sem("heads_kept")

            def wait(engine, sem, count):
                if not isinstance(count, int) or count > 0:
                    engine.wait_ge(sem, count)

            def parts(w):
                head = (w - 2 if w >= 2 else None, ROUNDS - LAG, range(0, LAG))
                body = (w - 1 if 1 <= w <= PAIRS else None, 0, range(LAG, ROUNDS))
                return head, body

            def rounds(engine, w, part, step):
                e, e_start, span = part
                m = w if w < PAIRS else None
                if e is None and m is None:
                    return
                step(e, e_start, m, span[0])
                with engine.Fori(1, len(span)) as i:
                    step(e, i + e_start, m, i + span[0])

            with ph.block() as block:

                @block.sync
                def _(sp):
                    def step(e, er, m, mr):
                        for s in range(UNROLL):
                            def tiles(r):
                                at = r * (UNROLL * P) + s * P
                                return slice(at, at + P) if isinstance(at, int) else bass.ds(at, P)

                            if m is not None:
                                wait(sp, m_ready, mr * (UNROLL * 2) + (m * (KT * 2) + 2 * (s + 1 - UNROLL)))
                                sp.dma_start(max_key_tile[s][:, :].bitcast(F32), keys[:, m // 2, tiles(mr)].bitcast(F32))\
                                    .then_inc(max_key_loaded[s], 16)
                            if e is not None:
                                wait(sp, e_ready, er * (UNROLL * GH) + (e * (KT * GH) + GH * (s + 1 - UNROLL)))
                                sp.dma_start(key_tile[s][:, :].bitcast(F32), keys[:, e // 2, tiles(er)].bitcast(F32))\
                                    .then_inc(key_loaded[s], 16)
                                wait(sp, pv_done, er * UNROLL + (e * KT + (s + 1 - UNROLL)))
                                at = er * (UNROLL * HEADS * VC) + (e // 2 * (GH * VC) + s * HEADS * VC)
                                at = slice(at, at + GH * VC) if isinstance(at, int) else bass.ds(at, GH * VC)
                                sp.dma_start(value_tile[s][:, :], values[:, at]).then_inc(value_loaded[s], 16)

                    for w in range(PAIRS + 2):
                        for part in parts(w):
                            rounds(sp, w, part, step)

                @block.gpsimd
                def _(pool):
                    def place_queries(p):
                        wait(pool, e_ready, (p - Q_RING + 1) * (KT * GH))
                        put_on_diagonal(pool, p)

                    def place_maxima(p):
                        pool.wait_ge(max_split, p + 1)
                        for j in range(GH):
                            for r, part in enumerate((max_hi, max_lo)):
                                row = j * ROWS + 3 * HD + r
                                pool.dma_start(
                                    q_diag[p % Q_RING][row:row + 1, j, :].bitcast(F32).rearrange("p (a q) -> p a q", q=P),
                                    part[j * 4:(j + 1) * 4, :].bitcast(F32)).then_inc(max_placed, 16)

                    for w in range(1, PAIRS + 1):
                        place_maxima(w - 1)
                        if w + 1 < PAIRS:
                            place_queries(w + 1)

                @block.tensor
                def _(pe):
                    def weigh(a, s, loads, start, stop):
                        pe.wait_ge(exp_done, a * GH + GH)
                        pe.wait_ge(value_loaded[s], loads * 16)
                        for j in range(GH):
                            last = nc.tensor.matmul(ps_o[j * ROWS:j * ROWS + VC, :],
                                                    value_tile[s][:, j * VC:(j + 1) * VC],
                                                    probs[(GH * s + j) % P_RING][:, :], start=start, stop=stop,
                                                    skip_group_check=True)
                        last.then_inc(pv_done, 1)

                    def weigh_before(e, er, s):
                        a = er * UNROLL + (e * KT + s - 1)
                        r = er + e * ROUNDS + (1 if s else 0)
                        if not isinstance(a, int):
                            weigh(a, (s - 1) % UNROLL, r, False, False)
                        elif a >= 0:
                            if a % KT == 0 and a:
                                pe.wait_ge(heads_kept, a // KT)
                            weigh(a, (s - 1) % UNROLL, r, a % KT == 0, a % KT == KT - 1)

                    def exp_scores(e, er, s, j):
                        wait(pe, exp_done, er * (UNROLL * GH) + (e * (KT * GH) + s * GH + j + 1 - E_RING))
                        nc.tensor.matmul(ps_e[(s + j) % E_RING][:, :], key_tile[s][:, :],
                                         q_diag[e % Q_RING][:, j, :], start=True, stop=True).then_inc(e_ready, 1)

                    def max_scores(m, mr, s, j):
                        if j % 2 == 0:
                            wait(pe, max_done, mr * (UNROLL * 2) + (m * (KT * 2) + 2 * s + j // 2 + 1 - M_RING))
                        last = nc.tensor.matmul(ps_m[j // 2][:, j % 2, :], max_key_tile[s][:, :],
                                                q_diag[m % Q_RING][:, j, :], start=True, stop=True)
                        if j % 2:
                            last.then_inc(m_ready, 1)

                    def turn_maxima(p, half):
                        pe.wait_ge(max_done, (p + 1) * (KT * 2) - 1 + half)
                        for j in range(2):
                            for i in range(4):
                                last = nc.tensor.transpose(ps_m[half][:, j, i * P:(i + 1) * P],
                                                           run_max[:, half * 2 + j, i * P:(i + 1) * P],
                                                           consts["ident"][:, :])
                        last.then_inc(run_turned, 1)

                    def step(e, er, m, mr):
                        for s in range(UNROLL):
                            if e is not None:
                                pe.wait_ge(key_loaded[s], er * 16 + (e * ROUNDS + 1) * 16)
                            if m is not None:
                                pe.wait_ge(max_key_loaded[s], mr * 16 + (m * ROUNDS + 1) * 16)
                            turning = s == 0 and isinstance(mr, int) and mr == 0 and 0 < window <= PAIRS
                            if turning:
                                if e is not None:
                                    exp_scores(e, er, s, 0)
                                    exp_scores(e, er, s, 1)
                                    weigh_before(e, er, s)
                                turn_maxima(window - 1, 0)
                                turn_maxima(window - 1, 1)
                                if e is not None:
                                    exp_scores(e, er, s, 2)
                                    exp_scores(e, er, s, 3)
                                pe.wait_ge(max_found, window)
                                nc.tensor.transpose(ps_m[1][:, 0, 0:P], neg_max[:, :], consts["ident"][:, :])\
                                    .then_inc(max_turned, 1)
                                if m is not None:
                                    pe.wait_ge(max_split, window)
                                    for j in range(GH):
                                        max_scores(m, mr, s, j)
                                continue
                            for j in range(GH):
                                if e is not None:
                                    exp_scores(e, er, s, j)
                                if m is not None:
                                    max_scores(m, mr, s, j)
                                if e is not None and j == (2 if m is None else 1):
                                    weigh_before(e, er, s)

                    pe.wait_ge(sums_cleared, 1)
                    for window in range(PAIRS + 2):
                        if window < PAIRS:
                            pe.wait_ge(q_placed, (window + 1) * 64 if window else 128)
                        head, body = parts(window)
                        rounds(pe, window, head, step)
                        if body[0] is not None:
                            pe.wait_ge(max_placed, (body[0] + 1) * 128)
                        rounds(pe, window, body, step)
                    weigh(PAIRS * KT - 1, UNROLL - 1, PAIRS * ROUNDS, False, True)

                @block.scalar
                def _(act):
                    def step(r):
                        for s in range(UNROLL):
                            for j in range(GH):
                                act.wait_ge(e_ready, r * (UNROLL * GH) + (s * GH + j + 1))
                                wait(act, pv_done, r * UNROLL + (s + j // 2 - 1))
                                nc.scalar.activation(probs[(GH * s + j) % P_RING][:, :], ps_e[(s + j) % E_RING][:, :],
                                                     ACT.Exp, scale=scale).then_inc(exp_done, 1)

                    step(0)
                    with act.Fori(1, PAIRS * ROUNDS) as r:
                        step(r)

                @block.vector
                def _(dve):
                    def find_maxima(p):
                        for half in range(2):
                            dve.wait_ge(run_turned, p * 2 + half + 1)
                            last = nc.vector.tensor_reduce(
                                neg_max[:, half * 8:half * 8 + 8],
                                ps_m[half][:, :, :].rearrange("p j (i k) -> p (j i) k", k=P), AX, ALU.max, negate=True)
                        last.then_inc(max_found, 1)
                        dve.wait_ge(max_turned, p + 1)
                        if p:
                            dve.wait_ge(max_placed, p * 128)
                        nc.vector.tensor_copy(max_hi[:, :], ps_m[1][0:GH * 4, 0, 0:P]).then_inc(hi_ready, 1)
                        dve.wait_ge(hi_ready, p + 1)
                        nc.vector.tensor_tensor(max_lo[:, :], ps_m[1][0:GH * 4, 0, 0:P], max_hi[:, :].bitcast(F32),
                                                ALU.subtract).then_inc(max_split, 1)

                    def keep_heads(p):
                        dve.wait_ge(pv_done, p * KT + KT)
                        dve.wait_ge(q_placed, (p + 1) * 64 if p else 128)
                        nc.vector.tensor_copy(q_heads[p // 2][:, p % 2 * BANK:(p % 2 + 1) * BANK].bitcast(F32),
                                              ps_o[:, :]).then_inc(heads_kept, 1)

                    def step(e, er, m, mr):
                        for s in range(UNROLL):
                            for half in range(2):
                                if m is not None:
                                    b = mr * (UNROLL * 2) + (m * (KT * 2) + 2 * s + half)
                                    dve.wait_ge(m_ready, b + 1)
                                    run = run_max[:, half * 2:half * 2 + 2, :]
                                    if s == 0 and isinstance(mr, int) and mr == 0:
                                        nc.vector.tensor_copy(run, ps_m[half][:, :, :]).then_inc(max_done, 1)
                                    else:
                                        dve.wait_ge(max_done, b - 1)
                                        nc.vector.tensor_tensor(run, ps_m[half][:, :, :], run, ALU.max)\
                                            .then_inc(max_done, 1)
                                if s == 0 and half == 0 and isinstance(er, int) and er == 0 and e:
                                    keep_heads(e - 1)

                    dve.wait_ge(cleared, 1)
                    nc.vector.memset(ps_o[:, :], 0.0).then_inc(sums_cleared, 1)
                    for w in range(PAIRS + 2):
                        head, body = parts(w)
                        if 1 <= w <= PAIRS:
                            find_maxima(w - 1)
                        if w < PAIRS:
                            rounds(dve, w, head, step)
                            rounds(dve, w, body, step)
                        elif body[0]:
                            keep_heads(body[0] - 1)
                    keep_heads(PAIRS - 1)
        attend_out(nc, sems, x_res, [heads[:, :].bitcast(F32) for heads in q_heads], consts, ins, G, HD, ROWS)


def attend_out(nc, sems, x_res, heads, consts, ins, G, HD, ROWS):
    with Phase(nc, sems, "ao") as ph:
        w_o = ph.sb("w_o", [P, D])
        inv = [ph.sb(f"inv{b}", [P, HEADS]) for b in range(2)]
        normed = [ph.sb(f"normed{b}", [P, HEADS, HD]) for b in range(2)]
        normed_t = [ph.sb(f"normed_t{b}", [P, P]) for b in range(2)]
        ps_turn = [ph.ps(f"ps_turn{b}", [P, BANK]) for b in range(2)]
        ps_back = [ph.ps(f"ps_back{b}", [P, P]) for b in range(2)]
        ps_out = [ph.ps(f"ps_out{b}", [P, D]) for b in range(2)]
        loaded = ph.sem("loaded")
        turned = ph.sem("turned")
        inv_ready = ph.sem("inv_ready")
        normed_ready = ph.sem("normed_ready")
        back_ready = ph.sem("back_ready")
        back_kept = ph.sem("back_kept")
        out_ready = ph.sem("out_ready")
        out_added = ph.sem("out_added")
        with ph.block() as block:

            @block.sync
            def _(sp):
                sp.dma_start(w_o[:, :], ins["w_ca1_o"]).then_inc(loaded, 16)

            @block.tensor
            def _(pe):
                def turn(i):
                    if i >= 2:
                        pe.wait_ge(normed_ready, i - 1)
                    for g in range(G):
                        last = nc.tensor.transpose(ps_turn[i % 2][:, g * P:(g + 1) * P],
                                                   heads[g][:, i * P:(i + 1) * P], consts["ident"][:, :])
                    last.then_inc(turned, 1)

                pe.wait_ge(loaded, 16)
                turn(0)
                for i in range(TT):
                    if i + 1 < TT:
                        turn(i + 1)
                    pe.wait_ge(normed_ready, i + 1)
                    nc.tensor.transpose(ps_back[i % 2][:, :], normed[i % 2][:, :, :].rearrange("p h c -> p (h c)"),
                                        consts["ident"][:, :]).then_inc(back_ready, 1)
                    pe.wait_ge(back_kept, i + 1)
                    if i >= 2:
                        pe.wait_ge(out_added, i - 1)
                    nc.tensor.matmul(ps_out[i % 2][:, :], normed_t[i % 2][:, :], w_o[:, :], start=True, stop=True)\
                        .then_inc(out_ready, 1)

            @block.scalar
            def _(act):
                for i in range(TT):
                    act.wait_ge(back_ready, i + 1)
                    nc.scalar.activation(normed_t[i % 2][:, :], ps_back[i % 2][:, :], ACT.Copy).then_inc(back_kept, 1)

            @block.vector
            def _(dve):
                for i in range(TT + 1):
                    if i < TT:
                        dve.wait_ge(turned, i + 1)
                        by_head = ps_turn[i % 2][:, :].rearrange("p (h r) -> p h r", r=ROWS)
                        nc.vector.reciprocal(inv[i % 2][:, :], by_head[:, :, HD]).then_inc(inv_ready, 1)
                        dve.wait_ge(inv_ready, i + 1)
                        nc.vector.tensor_tensor(normed[i % 2][:, :, :], by_head[:, :, 0:HD],
                                                inv[i % 2][:, :].unsqueeze(2).to_broadcast([P, HEADS, HD]), ALU.mult)\
                            .then_inc(normed_ready, 1)
                    if i:
                        dve.wait_ge(out_ready, i)
                        nc.vector.tensor_tensor(x_res[:, i - 1, :], x_res[:, i - 1, :], ps_out[(i - 1) % 2][:, :],
                                                ALU.add).then_inc(out_added, 1)


def bit_linear_ffn(nc, sems, x_res, xn_tok, consts, ins):
    H = 512
    HC = H // P
    ROUND = 12582912.0
    with Phase(nc, sems, "bl") as ph:
        w1 = ph.sb("w1", [P, H])
        w2 = ph.sb("w2", [P, HC, D])
        b1 = ph.sb("b1", [P, H])
        b2 = ph.sb("b2", [P, D])
        w1_t = ph.sb("w1_t", [P, H], BF16)
        w2_t = ph.sb("w2_t", [P, HC * D], BF16)
        w_scaled = ph.sb("w_scaled", [P, H])
        w_scaled2 = ph.sb("w_scaled2", [P, HC * D])
        w_whole = ph.sb("w_whole", [P, H])
        w_whole2 = ph.sb("w_whole2", [P, HC * D])
        w_sums = ph.sb("w_sums", [P, 2])
        w_mean = ph.sb("w_mean", [P, 2])
        w_inv = ph.sb("w_inv", [P, 2])
        ident_b = ph.sb("ident_b", [P, P], BF16)
        squares = ph.sb("squares", [P, TT, D])
        x_scaled = ph.sb("x_scaled", [P, TT, D])
        x_shifted = ph.sb("x_shifted", [P, TT, D])
        x_whole = ph.sb("x_whole", [P, TT, D], BF16)
        x_turned = ph.sb("x_turned", [P, T], BF16)
        hidden_in = [ph.sb(f"hidden_in{b}", [P, H]) for b in range(2)]
        hidden = ph.sb("hidden", [P, TT, H])
        h_squares = ph.sb("h_squares", [P, H])
        h_scaled = [ph.sb(f"h_scaled{b}", [P, H]) for b in range(2)]
        h_shifted = [ph.sb(f"h_shifted{b}", [P, H]) for b in range(2)]
        h_whole = [ph.sb(f"h_whole{b}", [P, H], BF16) for b in range(2)]
        h_turned = [ph.sb(f"h_turned{b}", [P, H], BF16) for b in range(2)]
        summed = [ph.sb(f"summed{b}", [P, D]) for b in range(2)]
        ps_turn = [ph.ps(f"ps_turn{b}", [P, BANK]) for b in range(2)]
        ps_h = [ph.ps(f"ps_h{b}", [P, H]) for b in range(2)]
        ps_out = [ph.ps(f"ps_out{b}", [P, D]) for b in range(2)]
        ps_mean = ph.ps("ps_mean", [P, 2])

        loaded = ph.sem("loaded")
        chain_sem = ph.sem("chain")
        w_summed = ph.sem("w_summed")
        means_ready = ph.sem("means_ready")
        var_ready = ph.sem("var_ready")
        std_ready = ph.sem("std_ready")
        w_ready = ph.sem("w_ready")
        x_ready = ph.sem("x_ready")
        turn_ready = ph.sem("turn_ready")
        x_kept = ph.sem("x_kept")
        h_ready = ph.sem("h_ready")
        in_ready = ph.sem("in_ready")
        hidden_ready = ph.sem("hidden_ready")
        squared = ph.sem("squared")
        peaks_ready = ph.sem("peaks_ready")
        h_whole_ready = ph.sem("h_whole_ready")
        h_kept = ph.sem("h_kept")
        out_ready = ph.sem("out_ready")
        out_added = ph.sem("out_added")

        def stats(name):
            return {k: ph.sb(f"{name}_{k}", [P, TT]) for k in
                    ("sum_sq", "var", "std", "rstd", "sq", "vsq", "corr", "norm", "peak", "top", "clipped", "inv",
                     "step", "gain", "back")}

        x_stats, h_stats = stats("x"), stats("h")

        def wide(stat, width):
            return stat[:, :].unsqueeze(2).to_broadcast([P, TT, width])

        with ph.block() as block:

            @block.sync
            def _(sp):
                sp.dma_start(w1[:, :], ins["w_bl1"]).then_inc(loaded, 16)
                sp.dma_start(w2[:, :, :], ins["w_bl2"]).then_inc(loaded, 16)
                sp.dma_start(b1[:, :], ins["b_bl1"].to_broadcast([P, H])).then_inc(loaded, 16)
                sp.dma_start(b2[:, :], ins["b_bl2"].to_broadcast([P, D])).then_inc(loaded, 16)

            @block.tensor
            def _(pe):
                pe.wait_ge(w_summed, 1)
                nc.tensor.matmul(ps_mean[:, :], consts["ones"][:, :], w_sums[:, :], start=True, stop=True)\
                    .then_inc(means_ready, 1)
                pe.wait_ge(x_ready, 1)
                for i in range(TT):
                    last = nc.tensor.matmul(ps_turn[i // 4][:, i % 4 * P:(i % 4 + 1) * P], x_whole[:, i, :],
                                            ident_b[:, :], start=True, stop=True)
                    if i % 4 == 3:
                        last.then_inc(turn_ready, 1)
                pe.wait_ge(w_ready, 1)
                pe.wait_ge(x_kept, 2)
                for i in range(TT):
                    if i >= 2:
                        pe.wait_ge(in_ready, i - 1)
                    nc.tensor.matmul(ps_h[i % 2][:, :], x_turned[:, i * P:(i + 1) * P], w1_t[:, :],
                                     start=True, stop=True).then_inc(h_ready, 1)

                def turn(i):
                    pe.wait_ge(h_whole_ready, i + 1)
                    if i >= 2:
                        pe.wait_ge(h_kept, i - 1)
                    for c in range(HC):
                        last = nc.tensor.matmul(ps_turn[i % 2][:, c * P:(c + 1) * P],
                                                h_whole[i % 2][:, c * P:(c + 1) * P], ident_b[:, :],
                                                start=True, stop=True)
                    last.then_inc(turn_ready, 1)

                turn(0)
                for i in range(TT):
                    if i + 1 < TT:
                        turn(i + 1)
                    pe.wait_ge(h_kept, i + 1)
                    if i >= 2:
                        pe.wait_ge(out_added, i - 1)
                    for c in range(HC):
                        last = nc.tensor.matmul(ps_out[i % 2][:, :], h_turned[i % 2][:, c * P:(c + 1) * P],
                                                w2_t[:, c * D:(c + 1) * D], start=c == 0, stop=c == HC - 1)
                    last.then_inc(out_ready, 1)

            @block.scalar
            def _(act):
                act.wait_ge(var_ready, 1)
                nc.scalar.activation(x_stats["std"][:, :], x_stats["var"][:, :], ACT.Sqrt).then_inc(std_ready, 1)
                for b in range(2):
                    act.wait_ge(turn_ready, b + 1)
                    nc.scalar.activation(x_turned[:, b * BANK:(b + 1) * BANK], ps_turn[b][:, :], ACT.Copy)\
                        .then_inc(x_kept, 1)
                for i in range(TT):
                    act.wait_ge(in_ready, i + 1)
                    nc.scalar.activation(hidden[:, i, :], hidden_in[i % 2][:, :], ACT.Gelu).then_inc(hidden_ready, 1)
                    act.wait_ge(hidden_ready, i + 1)
                    if i:
                        act.wait_ge(squared, i)
                    nc.scalar.activation(h_squares[:, :], hidden[:, i, :], ACT.Square,
                                         accum_out=h_stats["sum_sq"][:, i:i + 1]).then_inc(squared, 1)
                act.wait_ge(var_ready, 2)
                nc.scalar.activation(h_stats["std"][:, :], h_stats["var"][:, :], ACT.Sqrt).then_inc(std_ready, 1)
                for i in range(TT):
                    act.wait_ge(turn_ready, i + 3)
                    if i >= 2:
                        act.wait_ge(out_ready, i - 1)
                    nc.scalar.activation(h_turned[i % 2][:, :], ps_turn[i % 2][:, :], ACT.Copy).then_inc(h_kept, 1)

            @block.vector
            def _(dve):
                step = Chain(dve, chain_sem)

                def norm_scales(s, width, turn, mean):
                    step(nc.vector.tensor_scalar(s["var"][:, :], s["sum_sq"][:, :], 1.0 / width, 1e-6,
                                                 ALU.mult, ALU.add))
                    nc.vector.tensor_copy(s["corr"][:, :], s["var"][:, :]).then_inc(var_ready, 1)
                    dve.wait_ge(std_ready, turn)
                    dve.wait_ge(var_ready, turn)
                    step(nc.vector.reciprocal(s["rstd"][:, :], s["std"][:, :]))
                    step(nc.vector.tensor_tensor(s["sq"][:, :], s["rstd"][:, :], s["rstd"][:, :], ALU.mult))
                    step(nc.vector.tensor_tensor(s["vsq"][:, :], s["sq"][:, :], s["var"][:, :], ALU.mult))
                    step(nc.vector.tensor_scalar(s["corr"][:, :], s["vsq"][:, :], -0.5, 1.5, ALU.mult, ALU.add))
                    step(nc.vector.tensor_tensor(s["norm"][:, :], s["rstd"][:, :], s["corr"][:, :], ALU.mult))
                    step(nc.vector.tensor_tensor(s["top"][:, :], s["peak"][:, :], s["norm"][:, :], ALU.mult))
                    step(nc.vector.tensor_scalar(s["clipped"][:, :], s["top"][:, :], 1e-5, 1.0 / 127.0,
                                                 ALU.max, ALU.mult))
                    step(nc.vector.reciprocal(s["inv"][:, :], s["clipped"][:, :]))
                    step(nc.vector.tensor_tensor(s["gain"][:, :], s["inv"][:, :], s["norm"][:, :], ALU.mult))
                    step(nc.vector.tensor_scalar(s["back"][:, :], s["clipped"][:, :], mean, None, ALU.mult))

                dve.wait_ge(loaded, 64)
                w2_flat = w2[:, :, :].rearrange("p c d -> p (c d)")
                nc.vector.tensor_reduce(w_sums[:, 0:1], w1[:, :], AX, ALU.add, apply_absolute_value=True)
                nc.vector.tensor_reduce(w_sums[:, 1:2], w2_flat, AX, ALU.add, apply_absolute_value=True)\
                    .then_inc(w_summed, 1)
                step(nc.vector.tensor_tensor(squares[:, :, :], xn_tok[:, :, :], xn_tok[:, :, :], ALU.mult))
                nc.vector.tensor_copy(ident_b[:, :], consts["ident"][:, :])
                nc.vector.tensor_reduce(x_stats["peak"][:, :], xn_tok[:, :, :], AX, ALU.max, apply_absolute_value=True)
                step(nc.vector.tensor_reduce(x_stats["sum_sq"][:, :], squares[:, :, :], AX, ALU.add))
                dve.wait_ge(means_ready, 1)
                step(nc.vector.tensor_scalar(w_mean[:, :], ps_mean[:, :], 1.0 / (H * D), 1e-5, ALU.mult, ALU.max))
                norm_scales(x_stats, D, 1, w_mean[:, 0:1])
                step(nc.vector.tensor_tensor(x_scaled[:, :, :], xn_tok[:, :, :], wide(x_stats["gain"], D), ALU.mult))
                step(nc.vector.tensor_scalar(x_shifted[:, :, :], x_scaled[:, :, :], ROUND, ROUND + 127.0,
                                             ALU.add, ALU.min))
                nc.vector.tensor_scalar(x_whole[:, :, :], x_shifted[:, :, :], ROUND, -128.0,
                                        ALU.subtract, ALU.max).then_inc(x_ready, 1)
                step(nc.vector.reciprocal(w_inv[:, :], w_mean[:, :]))
                nc.vector.tensor_scalar(w_scaled[:, :], w1[:, :], w_inv[:, 0:1], ROUND, ALU.mult, ALU.add)
                step(nc.vector.tensor_scalar(w_scaled2[:, :], w2_flat, w_inv[:, 1:2], ROUND, ALU.mult, ALU.add))
                nc.vector.tensor_scalar(w_whole[:, :], w_scaled[:, :], ROUND, -1.0, ALU.subtract, ALU.max)
                step(nc.vector.tensor_scalar(w_whole2[:, :], w_scaled2[:, :], ROUND, -1.0, ALU.subtract, ALU.max))
                nc.vector.tensor_scalar(w1_t[:, :], w_whole[:, :], 1.0, None, ALU.min)
                nc.vector.tensor_scalar(w2_t[:, :], w_whole2[:, :], 1.0, None, ALU.min).then_inc(w_ready, 1)
                for i in range(TT + 1):
                    if i < TT:
                        dve.wait_ge(h_ready, i + 1)
                        if i >= 2:
                            dve.wait_ge(hidden_ready, i - 1)
                        nc.vector.scalar_tensor_tensor(hidden_in[i % 2][:, :], ps_h[i % 2][:, :],
                                                       x_stats["back"][:, i:i + 1], b1[:, :], ALU.mult, ALU.add)\
                            .then_inc(in_ready, 1)
                    if i:
                        dve.wait_ge(hidden_ready, i)
                        nc.vector.tensor_reduce(h_stats["peak"][:, i - 1:i], hidden[:, i - 1, :], AX, ALU.max,
                                                apply_absolute_value=True).then_inc(peaks_ready, 1)
                dve.wait_ge(squared, TT)
                dve.wait_ge(peaks_ready, TT)
                norm_scales(h_stats, H, 2, w_mean[:, 1:2])

                def add_out(i):
                    dve.wait_ge(out_ready, i + 1)
                    nc.vector.scalar_tensor_tensor(summed[i % 2][:, :], ps_out[i % 2][:, :],
                                                   h_stats["back"][:, i:i + 1], b2[:, :], ALU.mult, ALU.add)\
                        .then_inc(out_added, 1)
                    dve.wait_ge(out_added, i + 1)
                    nc.vector.tensor_tensor(x_res[:, i, :], x_res[:, i, :], summed[i % 2][:, :], ALU.add)

                for i in range(TT):
                    b = i % 2
                    step(nc.vector.tensor_scalar(h_scaled[b][:, :], hidden[:, i, :], h_stats["gain"][:, i:i + 1],
                                                 ROUND, ALU.mult, ALU.add))
                    step(nc.vector.tensor_scalar(h_shifted[b][:, :], h_scaled[b][:, :], ROUND, -128.0,
                                                 ALU.subtract, ALU.max))
                    if i >= 2:
                        dve.wait_ge(turn_ready, i + 1)
                    nc.vector.tensor_scalar(h_whole[b][:, :], h_shifted[b][:, :], 127.0, None, ALU.min)\
                        .then_inc(h_whole_ready, 1)
                    if i >= 2:
                        add_out(i - 2)
                add_out(TT - 2)
                add_out(TT - 1)


def program(nc, ins, out):
    with ExitStack() as sems, Phase(nc, sems, "main") as ph:
        x_res = ph.sb("x_res", [P, TT, D])
        xn_t = ph.sb("xn_t", [P, T])
        ident = ph.sb("ident", [P, P])
        masks = ph.sb("masks", [P, 8])
        ones = ph.sb("ones", [P, P])
        places = ph.sb("places", [P, 8])
        consts = {"ones": ones, "places": places, "masks": masks, "ident": ident}
        norm_sems = [ph.sem(f"norm_{name}") for name in NORM_SEMS]
        loaded = ph.sem("loaded")
        stored = ph.sem("stored")
        ctx_loaded = ph.sem("ctx_loaded")
        ctx_tok_loaded = ph.sem("ctx_tok_loaded")
        tail_cleared = ph.sem("tail_cleared")
        with Phase(nc, sems, "early") as early:
            ctx_t = early.sb("ctx_t", [P, S])
            ctx_tok = early.sb("ctx_tok", [P, KT, D])
            with ph.block() as block:

                @block.sync
                def _(sp):
                    sp.dma_start(x_res[:, :, :], ins["x"].rearrange("a (i p) d -> p (a i) d", p=P)).then_inc(loaded, 16)
                    sp.dma_start(ident[:, :], ins["ident"]).then_inc(loaded, 16)
                    sp.dma_start(masks[:, :], ins["masks"]).then_inc(loaded, 16)
                    sp.dma_start(ones[:, :], ins["ones"]).then_inc(loaded, 16)
                    sp.dma_start(places[:, :], ins["places"]).then_inc(loaded, 16)
                    sp.wait_ge(loaded, 80)

                    sp.dma_start(ctx_t[:, :], ins["ctx_t"][:, 0:S]).then_inc(ctx_loaded, 16)
                    sp.dma_start(ctx_tok[:, 0:KT - 1, :],
                                 ins["ctx"][0, 0:(KT - 1) * P, :].rearrange("(k p) d -> p k d", p=P))\
                        .then_inc(ctx_tok_loaded, 16)
                    sp.wait_ge(tail_cleared, 1)
                    sp.dma_start(ctx_tok[0:S - (KT - 1) * P, KT - 1, :], ins["ctx"][0, (KT - 1) * P:S, :])\
                        .then_inc(ctx_tok_loaded, 16)

                @block.gpsimd
                def _(pool):
                    nc.gpsimd.memset(ctx_tok[:, KT - 1, :], 0.0).then_inc(tail_cleared, 1)

            layernorm(nc, norm_sems, 0, x_res, ident, xn_t)
            self_attention_0(nc, sems, x_res, xn_t, ident, masks, ins["w_heads"])
            layernorm(nc, norm_sems, 1, x_res, ident, xn_t)
            cross_attention_0(nc, sems, x_res, xn_t, ident, ones, ctx_t, ctx_tok, ctx_loaded, ctx_tok_loaded, ins)

        layernorm(nc, norm_sems, 2, x_res, ident, xn_t)
        experts(nc, sems, x_res, xn_t, consts, ins)
        with Phase(nc, sems, "la_in") as la:
            xn_tok = la.sb("xn_tok", [P, TT, D])
            layernorm(nc, norm_sems, 3, x_res, ident, xn_t, xn_tok)
            linear_attention(nc, sems, x_res, xn_t, xn_tok, consts, ins)

        layernorm(nc, norm_sems, 4, x_res, ident, xn_t)
        cross_attention_1(nc, sems, x_res, xn_t, consts, ins)
        with Phase(nc, sems, "bl_in") as bl:
            xn_tok = bl.sb("xn_tok", [P, TT, D])
            layernorm(nc, norm_sems, 5, x_res, ident, xn_t, xn_tok)
            bit_linear_ffn(nc, sems, x_res, xn_tok, consts, ins)

        with ph.block() as block:

            @block.sync
            def _(sp):
                sp.dma_start(out.rearrange("a (i p) d -> p (a i) d", p=P), x_res[:, :, :]).then_inc(stored, 16)
                sp.wait_ge(stored, 16)


def layouts(np, given):
    a = {"x": given["x"]}
    turn = lambda w: np.transpose(w, (0, 2, 1))
    q, k = turn(given["L0_attn_Q"]), turn(given["L0_attn_K"])
    a["w_heads"] = np.concatenate([q, q, k, k, given["L0_attn_VO"]], axis=2)
    a["ident"] = np.eye(P, dtype=np.float32)
    masks = np.zeros((P, 8), np.float32)
    masks[64:, 0] = -1.0
    for head in range(0, P, 32):
        masks[head + 16:head + 24, 1] = -1.0
        masks[head + 8:head + 16, 2] = -1.0
        masks[head + 24:head + 26, 2] = 1.0
        masks[head + 24:head + 26, 3] = 1.0
    a["masks"] = masks
    a["ones"] = np.ones((P, P), np.float32)
    a["places"] = np.tile(np.arange(8, dtype=np.float32), (P, 1))
    a["ctx"] = given["ctx_1024"]
    ctx = given["ctx_1024"][0]
    a["ctx_t"] = np.concatenate([ctx, ctx[:KT * P - S]]).T
    a["w_gate"] = given["L0_xattn_Wg"]
    a["b_gate"] = given["L0_xattn_bg"].reshape(D, 1)
    a["w_ca0_out"] = given["L0_xattn_Wo"]
    a["b_ca0_out"] = given["L0_xattn_bo"].reshape(1, D)
    a["router"] = given["L0_ffn_router_w"]
    a["w_moe_in"] = np.concatenate([given["L0_ffn_gate_proj"], given["L0_ffn_up_proj"]], axis=2)
    down = given["L0_ffn_down_proj"]
    padded = np.zeros((down.shape[0], 3 * P, D), np.float32)
    padded[:, :down.shape[1]] = down
    a["w_moe_down"] = padded.reshape(-1, 3, P, D).transpose(0, 2, 1, 3)
    by_head = lambda w: w.reshape(D, HEADS, -1).transpose(2, 1, 0)
    a["w_la_v"] = by_head(given["L1_attn_Wv"])
    a["w_la_q"] = by_head(given["L1_attn_Wq"])
    a["w_la_o"] = given["L1_attn_Wo"].reshape(HEADS, -1, D).transpose(1, 0, 2)
    a["w_la_k"] = given["L1_attn_Wk"]
    a["b_la_v"] = given["L1_attn_bv"].reshape(HEADS, -1).T
    a["b_la_q"] = given["L1_attn_bq"].reshape(HEADS, -1).T
    a["b_la_k"] = given["L1_attn_bk"].reshape(1, -1)
    a["b_la_o"] = given["L1_attn_bo"].reshape(1, -1)

    def in_rows(w):
        by = w.T.reshape(D, 4, 4, 1, 8)
        return np.concatenate([by, by, by, np.zeros_like(by)], axis=3).reshape(D, 4, P)

    a["w_ca1_q"] = in_rows(given["L1_xattn_Wq"])
    a["w_ca1_k"] = in_rows(given["L1_xattn_Wk"])
    a["w_ca1_v"] = given["L1_xattn_Wv"].T
    a["w_ca1_o"] = given["L1_xattn_Wo"].T
    a["w_bl1"] = given["L1_ffn_w1"].T
    a["w_bl2"] = given["L1_ffn_w2"].T.reshape(-1, P, D).transpose(1, 0, 2)
    a["b_bl1"] = given["L1_ffn_b1"].reshape(1, -1)
    a["b_bl2"] = given["L1_ffn_b2"].reshape(1, -1)
    return a


def kernel(**inputs):
    import numpy as np
    import concourse.bacc as bacc
    from concourse.bass_utils import run_bass_kernel_spmd

    given = {k: np.asarray(v) for k, v in inputs.items()}
    arrays = {f"in_{k}": np.ascontiguousarray(v) for k, v in layouts(np, given).items()}
    nc = bacc.Bacc("TRN2", target_bir_lowering=False, num_devices=1)
    ins = {k[3:]: nc.dram_tensor(k, v.shape, mybir.dt.from_np(v.dtype), kind="ExternalInput").ap()
           for k, v in arrays.items()}
    out = nc.dram_tensor("out_x", (1, T, D), F32, kind="ExternalOutput").ap()
    program(nc, ins, out)
    result = run_bass_kernel_spmd(nc, [arrays], core_ids=[0])
    return result.results[0]["out_x"]
```

```python
from contextlib import ExitStack

import concourse.bass as bass
from concourse import mybir

F32 = mybir.dt.float32
F32R = mybir.dt.float32r
BF16 = mybir.dt.bfloat16
U32 = mybir.dt.uint32
ALU = mybir.AluOpType
ACT = mybir.ActivationFunctionType
AX = mybir.AxisListType.X

P = 128
BANK = 512
T = 1024
D = 128
TT = T // P
S = 6404
KT = -(-S // P)
HEADS = 16
LN_EPS = 1e-5
WHOLE = 12582912.0


class Phase:

    def __init__(self, nc, sems, prefix):
        self.nc, self.sems, self.prefix = nc, sems, prefix
        self.stack = ExitStack()

    def __enter__(self):
        self.stack.__enter__()
        return self

    def __exit__(self, *exc):
        return self.stack.__exit__(*exc)

    def sb(self, name, shape, dtype=F32):
        return self.stack.enter_context(self.nc.sbuf_tensor(f"{self.prefix}_{name}", shape, dtype))

    def ps(self, name, shape):
        return self.stack.enter_context(self.nc.psum_tensor(f"{self.prefix}_{name}", shape, F32))

    def sem(self, name):
        return self.sems.enter_context(self.nc.semaphore(f"{self.prefix}_{name}"))

    def block(self):
        return self.nc.Block()


class Chain:

    def __init__(self, engine, sem, count=0):
        self.engine, self.sem, self.count = engine, sem, count

    def __call__(self, instruction):
        self.count += 1
        instruction.then_inc(self.sem, 1)
        self.engine.wait_ge(self.sem, self.count)


NORM_SEMS = ("chain", "var_ready", "std_ready", "normed_ready", "turned_ready", "kept0", "kept1")
NORM_STEPS = 7


class LayerNorm:

    def __init__(self, ph, norm_sems, n, x_res, ident, xn_t=None, banks=None, xn_tok=None):
        (self.chain_sem, self.var_ready, self.std_ready, self.normed_ready, self.turned_ready, self.kept0,
         self.kept1) = norm_sems
        self.nc, self.n, self.x_res, self.ident = ph.nc, n, x_res, ident
        self.xn_t, self.banks = xn_t, banks
        self.normed = ph.sb("norm_normed", [P, TT, D]) if xn_tok is None else xn_tok
        self.stats = ph.sb("norm_stats", [P, TT, 6])
        self.moments = ph.sb("norm_moments", [P, TT, 2])
        self.var, self.std = [ph.sb(f"norm_{name}", [P, TT]) for name in ("var", "std")]
        self.rstd, self.newton, self.newton2, self.newton3, self.rstd2 = [
            ph.sb(f"norm_{name}", [P, TT]) for name in ("rstd", "newton", "newton2", "newton3", "rstd2")]

    def wait_normed(self, engine):
        engine.wait_ge(self.normed_ready, self.n * 2 + 2)

    def wait_turned(self, engine):
        engine.wait_ge(self.kept0, self.n + 1)
        engine.wait_ge(self.kept1, self.n + 1)

    def vector(self, dve):
        nc, n, x_res = self.nc, self.n, self.x_res
        step = Chain(dve, self.chain_sem, n * NORM_STEPS)
        for i in range(TT):
            last = nc.vector.bn_stats(self.stats[:, i, :], x_res[:, i, :])
        step(last)
        for i in range(TT):
            last = nc.vector.bn_aggr(self.moments[:, i, :], self.stats[:, i, :])
        step(last)
        nc.vector.tensor_scalar(self.var[:, :], self.moments[:, :, 1], LN_EPS, None, ALU.add)\
            .then_inc(self.var_ready, 1)
        dve.wait_ge(self.std_ready, n + 1)
        step(nc.vector.reciprocal(self.rstd[:, :], self.std[:, :]))
        step(nc.vector.tensor_tensor(self.newton[:, :], self.rstd[:, :], self.rstd[:, :], ALU.mult))
        step(nc.vector.tensor_tensor(self.newton2[:, :], self.newton[:, :], self.var[:, :], ALU.mult))
        step(nc.vector.tensor_scalar(self.newton3[:, :], self.newton2[:, :], -0.5, 1.5, ALU.mult, ALU.add))
        step(nc.vector.tensor_tensor(self.rstd2[:, :], self.rstd[:, :], self.newton3[:, :], ALU.mult))
        assert step.count == (n + 1) * NORM_STEPS
        for i in range(TT):
            last = nc.vector.tensor_scalar(self.normed[:, i, :], x_res[:, i, :], self.moments[:, i, 0:1],
                                           self.rstd2[:, i:i + 1], ALU.subtract, ALU.mult)
            if i % 4 == 3:
                last.then_inc(self.normed_ready, 1)
        if self.xn_t is not None:
            dve.wait_ge(self.turned_ready, n * 2 + 1)
            nc.vector.tensor_copy(self.xn_t[:, 0:BANK], self.banks[0]).then_inc(self.kept0, 1)

    def scalar_root(self, act):
        act.wait_ge(self.var_ready, self.n + 1)
        self.nc.scalar.activation(self.std[:, :], self.var[:, :], ACT.Sqrt).then_inc(self.std_ready, 1)

    def scalar_keep(self, act):
        act.wait_ge(self.turned_ready, self.n * 2 + 2)
        self.nc.scalar.activation(self.xn_t[:, BANK:T], self.banks[1], ACT.Copy).then_inc(self.kept1, 1)

    def tensor(self, pe):
        for i in range(TT):
            if i % 4 == 0:
                pe.wait_ge(self.normed_ready, self.n * 2 + i // 4 + 1)
            turn = self.nc.tensor.transpose(self.banks[i // 4][:, i % 4 * P:(i % 4 + 1) * P],
                                            self.normed[:, i, :], self.ident[:, :])
            if i % 4 == 3:
                turn.then_inc(self.turned_ready, 1)


def self_attention_0(nc, sems, norm_sems, x_res, xn_t, ident, masks, w_heads, load_context):
    QUAD = BANK // P
    scale = float(D) ** -0.5
    with Phase(nc, sems, "sa0") as ph:
        w = [ph.sb(f"w{b}", [P, 3 * P]) for b in range(2)]
        w_hi = ph.sb("w_hi", [P, 2 * P], F32R)
        w_lo = ph.sb("w_lo", [P, 2 * P], F32R)
        xn_hi = ph.sb("xn_hi", [P, T], F32R)
        xn_lo = ph.sb("xn_lo", [P, T], F32R)
        q_round = ph.sb("q_round", [P, BANK], F32R)
        q_stack = [ph.sb(f"q_stack{b}", [P, T], F32R) for b in range(2)]
        k_hi = [ph.sb(f"k_hi{b}", [P, T], F32R) for b in range(2)]
        k_lo = [ph.sb(f"k_lo{b}", [P, T], F32R) for b in range(2)]
        v_hi = [ph.sb(f"v_hi{b}", [P, TT, D], F32R) for b in range(2)]
        v_lo = [ph.sb(f"v_lo{b}", [P, TT, D], F32R) for b in range(2)]
        probs = [ph.sb(f"probs{b}", [P, T]) for b in range(2)]
        turned_hi = [ph.sb(f"turned_hi{b}", [P, TT, BANK], F32R) for b in range(2)]
        turned_lo = [ph.sb(f"turned_lo{b}", [P, TT, BANK], F32R) for b in range(2)]
        summed = ph.sb("summed", [P, BANK])
        neg_max = [ph.sb(f"neg_max{b}", [P, 1]) for b in range(2)]
        den = [ph.sb(f"den{b}", [P, QUAD]) for b in range(2)]
        inv_den = [ph.sb(f"inv_den{b}", [P, QUAD]) for b in range(2)]
        ps_scores = [ph.ps(f"ps_scores{b}", [P, T]) for b in range(2)]
        ps_turn = [ph.ps(f"ps_turn{b}", [P, BANK]) for b in range(2)]
        ps_out = ph.ps("ps_out", [P, BANK])
        ps_prep = ph.ps("ps_prep", [P, BANK])
        w_loaded = [ph.sem(f"w_loaded{b}") for b in range(2)]
        first_banks = [ps_prep[:, :], ps_turn[0][:, :], ps_turn[1][:, :], ps_scores[1][:, 0:BANK],
                       ps_scores[1][:, BANK:T], ps_prep[:, :]]

        def piece_bank(k, first):
            return first_banks[k] if first else ps_prep[:, :]

        norm = LayerNorm(ph, norm_sems, 0, x_res, ident, xn_t, [bank[:, :] for bank in ps_turn])
        xn_rounded = ph.sem("xn_rounded")
        xn_split = ph.sem("xn_split")
        w_rounded = ph.sem("w_rounded")
        w_split = ph.sem("w_split")
        prep_ready = ph.sem("prep_ready")
        prep_rounded = ph.sem("prep_rounded")
        prep_done = ph.sem("prep_done")
        scores_ready = ph.sem("scores_ready")
        max_ready = ph.sem("max_ready")
        exp_done = ph.sem("exp_done")
        turned = [ph.sem(f"turned{b}") for b in range(2)]
        turned_rounded = ph.sem("turned_rounded")
        turned_split = [ph.sem(f"turned_split{b}") for b in range(2)]
        inv_ready = ph.sem("inv_ready")
        pv_done = ph.sem("pv_done")
        out_kept = ph.sem("out_kept")
        back_ready = ph.sem("back_ready")
        out_added = ph.sem("out_added")

        PIECES = 6
        PAIRS = HEADS // 2
        UNITS = 2 * TT
        GROUPS = UNITS // QUAD

        def rounds(u):
            return u % TT, u // TT

        def wait(engine, sem, count):
            if not isinstance(count, int) or count > 0:
                engine.wait_ge(sem, count)

        with ph.block() as block:

            @block.sync
            def _(sp):
                for h in range(2):
                    sp.dma_start(w[h][:, :], w_heads[h]).then_inc(w_loaded[h], 16)
                load_context(sp)
                with sp.Fori(1, PAIRS) as i:
                    for b in range(2):
                        sp.wait_ge(prep_done, i * (2 * PIECES) + PIECES * (b - 1))
                        sp.dma_start(w[b][:, :], w_heads[bass.ds(i * 2 + b, 1)].rearrange("a d n -> (a d) n"))\
                            .then_inc(w_loaded[b], 16)

            @block.tensor
            def _(pe):
                def piece(k, slot, count, first=False):
                    bank = piece_bank(k, first)
                    if not first:
                        pe.wait_ge(prep_done, count + k)
                    elif k == PIECES - 1:
                        pe.wait_ge(prep_done, 1)
                    if k < 4:
                        half = slice(k % 2 * BANK, (k % 2 + 1) * BANK)
                        for m, (weights, x) in enumerate(((w_hi, xn_hi), (w_hi, xn_lo), (w_lo, xn_hi))):
                            last = nc.tensor.matmul(bank, weights[:, k // 2 * P:(k // 2 + 1) * P],
                                                    x[:, half], start=(m == 0), stop=(m == 2))
                        last.then_inc(prep_ready, 1)
                    else:
                        for j in range(4):
                            ut = (k - 4) * 4 + j
                            last = nc.tensor.matmul(bank[:, j * P:(j + 1) * P], xn_t[:, ut * P:(ut + 1) * P],
                                                    w[slot][:, 2 * P:3 * P], start=True, stop=True)
                        last.then_inc(prep_ready, 1)

                def scores(n, u, first=False):
                    q, slot = rounds(u % (2 * TT))
                    if not first:
                        pe.wait_ge(exp_done, n - 1)
                    buf = ps_scores[u % 2]
                    for half in range(2):
                        cut = slice(half * BANK, (half + 1) * BANK)
                        for m, keys in enumerate((k_hi, k_lo)):
                            last = nc.tensor.matmul(buf[:, cut], q_stack[slot][:, q * P:(q + 1) * P],
                                                    keys[slot][:, cut], start=(m == 0), stop=(m == 1))
                    last.then_inc(scores_ready, 1)

                def turn(n, u):
                    pe.wait_ge(exp_done, n + 1)
                    for j in range(TT):
                        if j % 4 == 0:
                            wait(pe, turned_split[j // 4], n)
                        last = nc.tensor.transpose(ps_turn[j // 4][:, j % 4 * P:(j % 4 + 1) * P],
                                                   probs[u % 2][:, j * P:(j + 1) * P], ident[:, :])
                        if j % 4 == 3:
                            last.then_inc(turned[j // 4], 1)

                def times_values(g, k, v):
                    if v == 0:
                        for half in range(2):
                            pe.wait_ge(turned_split[half], g * QUAD + QUAD)
                        wait(pe, out_added, g)
                    slot = k // 2
                    for j in (2 * v, 2 * v + 1):
                        for m, (values, turned_part) in enumerate(((v_hi, turned_hi), (v_hi, turned_lo),
                                                                   (v_lo, turned_hi))):
                            last = nc.tensor.matmul(ps_out[:, :], values[slot][:, j, :], turned_part[k % 2][:, j, :],
                                                    start=(j == 0 and m == 0), stop=(j == TT - 1 and m == 2))
                    if v == QUAD - 1:
                        last.then_inc(pv_done, 1)

                def back(g):
                    pe.wait_ge(out_kept, g + 1)
                    for v in range(QUAD):
                        last = nc.tensor.transpose(ps_out[:, v * P:(v + 1) * P], summed[:, v * P:(v + 1) * P],
                                                   ident[:, :])
                    last.then_inc(back_ready, 1)

                def pair(i, first, final):
                    for u in range(UNITS):
                        n = i * UNITS + u
                        g, v = i * GROUPS + u // QUAD, u % QUAD
                        if not (final and u + 2 >= UNITS):
                            if u in (TT - 2, 2 * TT - 2):
                                pe.wait_ge(prep_done, i * (2 * PIECES) + PIECES * (u // TT + 1) + 4)
                            scores(n + 2, u + 2)
                        if v == 0 and not (first and u < 2 * QUAD):
                            back(g - 2)
                        turn(n, u)
                        if u % TT < PIECES and not (final and u >= TT):
                            if u == 0:
                                pe.wait_ge(w_loaded[1], i * 16 + 16)
                            if u == TT:
                                pe.wait_ge(w_loaded[0], i * 16 + 32)
                            if u % TT == 0:
                                pe.wait_ge(w_split, i * 2 + (u // TT + 2))
                            piece(u % TT, 1 - u // TT, i * (2 * PIECES) + PIECES * (u // TT + 1))
                        if not (first and u < QUAD):
                            times_values(g - 1, (u // QUAD - 1) % GROUPS, v)

                norm.tensor(pe)
                norm.wait_turned(pe)
                pe.wait_ge(w_loaded[0], 16)
                pe.wait_ge(xn_split, 1)
                pe.wait_ge(w_split, 1)
                for k in range(PIECES):
                    piece(k, 0, 0, first=True)
                pe.wait_ge(prep_done, 4)
                scores(0, 0, first=True)
                pe.wait_ge(prep_done, PIECES)
                scores(1, 1, first=True)
                pair(0, True, False)
                with pe.Fori(1, PAIRS - 1) as i:
                    pair(i, False, False)
                pair(PAIRS - 1, False, True)
                back(PAIRS * GROUPS - 2)
                for v in range(QUAD):
                    times_values(PAIRS * GROUPS - 1, GROUPS - 1, v)
                back(PAIRS * GROUPS - 1)

            @block.scalar
            def _(act):
                def exp(n, u, inverted=None):
                    act.wait_ge(max_ready, n + 1)
                    if u % QUAD == 0:
                        wait(act, inv_ready, inverted)
                    group = den[u // QUAD % 2]
                    nc.scalar.activation(probs[u % 2][:, :], ps_scores[u % 2][:, :], ACT.Exp,
                                         bias=neg_max[u % 2][:, :], accum_out=group[:, u % QUAD:u % QUAD + 1])\
                        .then_inc(exp_done, 1)

                def round_weights(slot, loads):
                    act.wait_ge(w_loaded[slot], loads)
                    nc.scalar.activation(w_hi[:, :], w[slot][:, 0:2 * P], ACT.Copy).then_inc(w_rounded, 1)

                def round_piece(k, slot, count, first=False):
                    bank = piece_bank(k, first)
                    act.wait_ge(prep_ready, count + k + 1)
                    half = slice(k % 2 * BANK, (k % 2 + 1) * BANK)
                    if k >= 4:
                        ut = (k - 4) * 4
                        nc.scalar.activation(v_hi[slot][:, ut:ut + 4, :], bank.rearrange("p (a d) -> p a d", a=4),
                                             ACT.Copy).then_inc(prep_rounded, 1)
                    elif k < 2:
                        if first and k:
                            act.wait_ge(prep_done, 1)
                        nc.scalar.activation(q_round[:, :], bank, ACT.Copy).then_inc(prep_rounded, 1)
                    else:
                        nc.scalar.activation(k_hi[slot][:, half], bank, ACT.Copy, scale=scale)\
                            .then_inc(prep_rounded, 1)

                def keep(g):
                    act.wait_ge(pv_done, g + 1)
                    nc.scalar.activation(summed[:, :], ps_out[:, :], ACT.Copy).then_inc(out_kept, 1)

                def pair(i, first, final):
                    for u in range(UNITS):
                        n = i * UNITS + u
                        g, v = i * GROUPS + u // QUAD, u % QUAD
                        if v == 0 and not (first and u < 2 * QUAD):
                            keep(g - 2)
                        for half in range(2):
                            act.wait_ge(turned[half], n + 1)
                            nc.scalar.activation(turned_hi[u // QUAD % 2][:, half * 4:half * 4 + 4, v * P:(v + 1) * P],
                                                 ps_turn[half][:, :].rearrange("p (j q) -> p j q", q=P), ACT.Copy)\
                                .then_inc(turned_rounded, 1)
                        count = i * (2 * PIECES) + PIECES * (u // TT + 1)
                        if u % TT < PIECES and not (final and u >= TT):
                            round_piece(u % TT, 1 - u // TT, count)
                        if u % TT == PIECES and not final:
                            act.wait_ge(prep_ready, count + 4)
                            round_weights(u // TT, i * 16 + 32)
                        if not (final and u + 2 >= UNITS):
                            exp(n + 2, u + 2, i * GROUPS + ((u + 2) // QUAD - 1))

                norm.scalar_root(act)
                norm.scalar_keep(act)
                norm.wait_turned(act)
                nc.scalar.activation(xn_hi[:, :], xn_t[:, :], ACT.Copy).then_inc(xn_rounded, 1)
                round_weights(0, 16)
                for k in range(PIECES):
                    round_piece(k, 0, 0, first=True)
                round_weights(1, 16)
                exp(0, 0, -1)
                exp(1, 1)
                pair(0, True, False)
                with act.Fori(1, PAIRS - 1) as i:
                    pair(i, False, False)
                pair(PAIRS - 1, False, True)
                keep(PAIRS * GROUPS - 2)
                keep(PAIRS * GROUPS - 1)

            @block.vector
            def _(dve):
                def top(n, u):
                    dve.wait_ge(scores_ready, n + 1)
                    nc.vector.tensor_reduce(neg_max[u % 2][:, :], ps_scores[u % 2][:, :], AX, ALU.max, negate=True)\
                        .then_inc(max_ready, 1)

                def rest_weights(slot, heads):
                    dve.wait_ge(w_rounded, heads)
                    nc.vector.tensor_tensor(w_lo[:, :], w[slot][:, 0:2 * P], w_hi[:, :].bitcast(F32), ALU.subtract)\
                        .then_inc(w_split, 1)

                def rest_piece(k, slot, rounded, first=False):
                    bank = piece_bank(k, first)
                    half = slice(k % 2 * BANK, (k % 2 + 1) * BANK)
                    dve.wait_ge(prep_rounded, rounded + k + 1)
                    if k < 2:
                        out = nc.vector.scalar_tensor_tensor(
                            q_stack[slot][:, half], q_round[:, :].bitcast(F32), masks[:, 0:1], bank,
                            ALU.mult, ALU.add)
                    elif k < 4:
                        out = nc.vector.scalar_tensor_tensor(
                            k_lo[slot][:, half], bank, scale, k_hi[slot][:, half].bitcast(F32),
                            ALU.mult, ALU.subtract)
                    else:
                        ut = (k - 4) * 4
                        out = nc.vector.tensor_tensor(v_lo[slot][:, ut:ut + 4, :],
                                                      bank.rearrange("p (a d) -> p a d", a=4),
                                                      v_hi[slot][:, ut:ut + 4, :].bitcast(F32), ALU.subtract)
                    out.then_inc(prep_done, 1)

                def add(g, k):
                    dve.wait_ge(back_ready, g + 1)
                    dve.wait_ge(inv_ready, g + 1)
                    for v in range(QUAD):
                        t = k % 2 * QUAD + v
                        last = nc.vector.scalar_tensor_tensor(x_res[:, t, :], ps_out[:, v * P:(v + 1) * P],
                                                              inv_den[k % 2][:, v:v + 1], x_res[:, t, :],
                                                              ALU.mult, ALU.add)
                    last.then_inc(out_added, 1)

                def invert(n, k):
                    dve.wait_ge(exp_done, n)
                    nc.vector.reciprocal(inv_den[k % 2][:, :], den[k % 2][:, :]).then_inc(inv_ready, 1)

                def pair(i, first, final):
                    for u in range(UNITS):
                        n = i * UNITS + u
                        g, k, v = i * GROUPS + u // QUAD, u // QUAD, u % QUAD
                        if v == 0:
                            if not (first and u < 2 * QUAD):
                                add(g - 2, (k - 2) % GROUPS)
                            if not (first and u == 0):
                                invert(n, (k - 1) % GROUPS)
                        if not (final and u + 2 >= UNITS):
                            top(n + 2, u + 2)
                        for half in range(2):
                            dve.wait_ge(turned_rounded, n * 2 + half + 1)
                            cut = (slice(None), slice(half * 4, half * 4 + 4), slice(v * P, (v + 1) * P))
                            nc.vector.tensor_tensor(turned_lo[k % 2][cut],
                                                    ps_turn[half][:, :].rearrange("p (j q) -> p j q", q=P),
                                                    turned_hi[k % 2][cut].bitcast(F32), ALU.subtract)\
                                .then_inc(turned_split[half], 1)
                        if u % TT < PIECES and not (final and u >= TT):
                            rest_piece(u % TT, 1 - u // TT, i * (2 * PIECES) + PIECES * (u // TT + 1))
                        if u % TT == PIECES and not final:
                            rest_weights(u // TT, i * 2 + (u // TT + 3))

                norm.vector(dve)
                norm.wait_turned(dve)
                dve.wait_ge(xn_rounded, 1)
                nc.vector.tensor_tensor(xn_lo[:, :], xn_t[:, :], xn_hi[:, :].bitcast(F32), ALU.subtract)\
                    .then_inc(xn_split, 1)
                rest_weights(0, 1)
                for k in range(PIECES):
                    rest_piece(k, 0, 0, first=True)
                rest_weights(1, 2)
                top(0, 0)
                top(1, 1)
                pair(0, True, False)
                with dve.Fori(1, PAIRS - 1) as i:
                    pair(i, False, False)
                pair(PAIRS - 1, False, True)
                add(PAIRS * GROUPS - 2, GROUPS - 2)
                invert(PAIRS * UNITS, GROUPS - 1)
                add(PAIRS * GROUPS - 1, GROUPS - 1)


def cross_attention_0(nc, sems, norm_sems, x_res, xn_t, ident, ones, ctx_t, ctx_tok, ctx_loaded, ctx_tok_loaded, ins):
    CHUNKS = -(-S // BANK)
    TAIL = S - (CHUNKS - 1) * BANK
    TAIL_TILES = -(-TAIL // P)
    PROB_RING = 3
    assert (CHUNKS - 1) % PROB_RING == 0
    with Phase(nc, sems, "ca0") as ph:
        w_gate = ph.sb("w_gate", [P, D])
        b_gate = ph.sb("b_gate", [P, 1])
        w_out = ph.sb("w_out", [P, D])
        b_out = ph.sb("b_out", [1, D])
        gate_hi = ph.sb("gate_hi", [P, S], F32R)
        gate_lo = ph.sb("gate_lo", [P, S], F32R)
        xn_hi = ph.sb("xn_hi", [P, T], F32R)
        xn_lo = ph.sb("xn_lo", [P, T], F32R)
        q_hi = ph.sb("q_hi", [P, P], F32R)
        q_lo = ph.sb("q_lo", [P, P], F32R)
        scores = ph.sb("scores", [P, S])
        probs = [ph.sb(f"probs{b}", [P, BANK]) for b in range(PROB_RING)]
        probs_tail = ph.sb("probs_tail", [P, TAIL_TILES * P])
        probs_t = [ph.sb(f"probs_t{b}", [P, BANK]) for b in range(2)]
        chunk_max = ph.sb("chunk_max", [P, CHUNKS])
        chunk_den = ph.sb("chunk_den", [P, CHUNKS])
        neg_max = ph.sb("neg_max", [P, 1])
        den = ph.sb("den", [P, 1])
        inv_den = ph.sb("inv_den", [P, 1])
        attended = ph.sb("attended", [P, TT, D])
        attended_t = ph.sb("attended_t", [P, T])
        ps_scores = [ph.ps(f"ps_scores{b}", [P, BANK]) for b in range(2)]
        ps_turn = [ph.ps(f"ps_turn{b}", [P, BANK]) for b in range(2)]
        ps_out = ph.ps("ps_out", [P, D])
        ps_proj = [ph.ps(f"ps_proj{b}", [P, BANK]) for b in range(2)]
        ps_gate = ps_scores + ps_proj
        GATES = len(ps_gate)
        assert CHUNKS % GATES == 1
        norm = LayerNorm(ph, norm_sems, 1, x_res, ident, xn_t, [bank[:, :] for bank in ps_turn])
        loaded = ph.sem("loaded")
        gate_ready = ph.sem("gate_ready")
        gate_rounded = ph.sem("gate_rounded")
        gate_done = ph.sem("gate_done")
        split_hi = ph.sem("split_hi")
        split_done = ph.sem("split_done")
        tail_cleared = ph.sem("tail_cleared")
        q_ready = ph.sem("q_ready")
        scores_ready = ph.sem("scores_ready")
        scores_kept = ph.sem("scores_kept")
        chunk_max_ready = ph.sem("chunk_max_ready")
        max_ready = ph.sem("max_ready")
        exp_done = ph.sem("exp_done")
        turned = ph.sem("turned")
        probs_t_ready = ph.sem("probs_t_ready")
        pv_done = ph.sem("pv_done")
        den_ready = ph.sem("den_ready")
        inv_ready = ph.sem("inv_ready")
        attended_ready = ph.sem("attended_ready")
        out_turned = ph.sem("out_turned")
        attended_t_ready = [ph.sem(f"attended_t_ready{b}") for b in range(2)]
        projected = ph.sem("projected")

        def width(c):
            return BANK if c < CHUNKS - 1 else TAIL

        def prob_tile(c):
            return probs[c % PROB_RING] if c < CHUNKS - 1 else probs_tail

        def tiles(c):
            return 4 if c < CHUNKS - 1 else TAIL_TILES

        with ph.block() as block:

            @block.sync
            def _(sp):
                sp.dma_start(w_gate[:, :], ins["w_gate"]).then_inc(loaded, 16)
                sp.dma_start(b_gate[:, :], ins["b_gate"]).then_inc(loaded, 16)
                sp.dma_start(w_out[:, :], ins["w_ca0_out"]).then_inc(loaded, 16)
                sp.dma_start(b_out[:, :], ins["b_ca0_out"]).then_inc(loaded, 16)

            @block.tensor
            def _(pe):
                def gate(n, b, at, w):
                    nc.tensor.matmul(ps_gate[b][:, 0:w], w_gate[:, :], ctx_t[:, at], start=True, stop=True)\
                        .then_inc(gate_ready, 1)

                def score(t, c, first=False):
                    if c == 0:
                        pe.wait_ge(q_ready, t + 1)
                    if c != 1 and not (first and c < 2):
                        pe.wait_ge(scores_kept, t * CHUNKS + (c - 1 if c else 0))
                    w, at = width(c), slice(c * BANK, c * BANK + width(c))
                    for m, (q, g) in enumerate(((q_hi, gate_hi), (q_hi, gate_lo), (q_lo, gate_hi))):
                        last = nc.tensor.matmul(ps_scores[c % 2][:, 0:w], q[:, :], g[:, at],
                                                start=(m == 0), stop=(m == 2))
                    last.then_inc(scores_ready, 1)

                def turn(t, c):
                    pe.wait_ge(exp_done, t * CHUNKS + c + 1)
                    if c != 1:
                        pe.wait_ge(probs_t_ready, t * CHUNKS + (c if c else 1))
                    for j in range(tiles(c)):
                        last = nc.tensor.transpose(ps_turn[c % 2][:, j * P:(j + 1) * P],
                                                   prob_tile(c)[:, j * P:(j + 1) * P], ident[:, :])
                    last.then_inc(turned, 1)

                def times_context(t, c):
                    pe.wait_ge(probs_t_ready, t * CHUNKS + c + 2)
                    if c == 0:
                        pe.wait_ge(attended_ready, t + 1)
                    for j in range(tiles(c)):
                        last = nc.tensor.matmul(ps_out[:, :], probs_t[c % 2][:, j * P:(j + 1) * P],
                                                ctx_tok[:, c * 4 + j, :], start=(c == 0 and j == 0),
                                                stop=(c == CHUNKS - 1 and j == TAIL_TILES - 1))
                    if c == CHUNKS - 1:
                        last.then_inc(pv_done, 1)

                pe.wait_ge(loaded, 64)
                pe.wait_ge(ctx_loaded, 16)
                pe.wait_ge(ctx_tok_loaded, 32)
                for b in range(GATES):
                    gate(b, b, slice(b * BANK, (b + 1) * BANK), BANK)
                norm.tensor(pe)
                with pe.Fori(1, CHUNKS // GATES) as i:
                    for b in range(GATES):
                        pe.wait_ge(gate_done, i * GATES + (b + 1 - GATES))
                        gate(i * GATES + b, b, bass.ds(i * (GATES * BANK) + b * BANK, BANK), BANK)
                pe.wait_ge(gate_done, CHUNKS - GATES)
                gate(CHUNKS - 1, 0, slice((CHUNKS - 1) * BANK, S), TAIL)
                pe.wait_ge(gate_done, CHUNKS)
                norm.wait_turned(pe)
                for c in range(CHUNKS):
                    score(0, c, first=True)
                with pe.Fori(0, TT - 1) as t:
                    for c in range(CHUNKS):
                        turn(t, c)
                        if c == 0:
                            score(t + 1, 0)
                        if c + 1 < CHUNKS:
                            score(t + 1, c + 1)
                        if c:
                            times_context(t, c - 1)
                    times_context(t, CHUNKS - 1)
                for c in range(CHUNKS):
                    turn(TT - 1, c)
                    if c:
                        times_context(TT - 1, c - 1)
                times_context(TT - 1, CHUNKS - 1)
                pe.wait_ge(attended_ready, TT + 1)
                for i in range(TT):
                    last = nc.tensor.transpose(ps_turn[i // 4][:, i % 4 * P:(i % 4 + 1) * P],
                                               attended[:, i, :], ident[:, :])
                    if i % 4 == 3:
                        last.then_inc(out_turned, 1)
                for half in range(2):
                    pe.wait_ge(attended_t_ready[half], 1)
                    for j in range(4):
                        i = half * 4 + j
                        nc.tensor.matmul(ps_proj[half][:, j * P:(j + 1) * P], attended_t[:, i * P:(i + 1) * P],
                                         w_out[:, :], start=True, stop=False)
                        last = nc.tensor.matmul(ps_proj[half][:, j * P:(j + 1) * P], ones[0:1, :],
                                                b_out[:, :], start=False, stop=True)
                    last.then_inc(projected, 1)

            @block.scalar
            def _(act):
                def round_gate(n, b, at, w):
                    act.wait_ge(gate_ready, n + 1)
                    nc.scalar.activation(gate_hi[:, at], ps_gate[b][:, 0:w], ACT.Identity, bias=b_gate[:, :])\
                        .then_inc(gate_rounded, 1)

                def keep(t, c, first=False):
                    act.wait_ge(scores_ready, t * CHUNKS + c + 1)
                    if not first:
                        act.wait_ge(exp_done, t * CHUNKS + (c + 1 - CHUNKS))
                    w, at = width(c), slice(c * BANK, c * BANK + width(c))
                    nc.scalar.activation(scores[:, at], ps_scores[c % 2][:, 0:w], ACT.Copy).then_inc(scores_kept, 1)

                def exp(t, c, first=False):
                    if c == 0:
                        act.wait_ge(max_ready, t + 1)
                    if c == CHUNKS - 1:
                        if not first:
                            act.wait_ge(turned, t * CHUNKS)
                    elif c >= PROB_RING:
                        act.wait_ge(turned, t * CHUNKS + (c - PROB_RING + 1))
                    elif not first:
                        act.wait_ge(turned, t * CHUNKS + (c - PROB_RING))
                    w, at = width(c), slice(c * BANK, c * BANK + width(c))
                    nc.scalar.activation(prob_tile(c)[:, 0:w], scores[:, at], ACT.Exp, bias=neg_max[:, :],
                                         accum_out=chunk_den[:, c:c + 1]).then_inc(exp_done, 1)

                norm.scalar_root(act)
                norm.scalar_keep(act)
                norm.wait_turned(act)
                nc.scalar.activation(xn_hi[:, :], xn_t[:, :], ACT.Copy).then_inc(split_hi, 1)
                act.wait_ge(loaded, 64)
                with act.Fori(0, CHUNKS // GATES) as i:
                    for b in range(GATES):
                        round_gate(i * GATES + b, b, bass.ds(i * (GATES * BANK) + b * BANK, BANK), BANK)
                round_gate(CHUNKS - 1, 0, slice((CHUNKS - 1) * BANK, S), TAIL)
                act.wait_ge(tail_cleared, 1)
                for c in range(CHUNKS):
                    keep(0, c, first=True)

                def tile(t, first):
                    exp(t, 0, first)
                    exp(t, 1, first)
                    for c in range(CHUNKS):
                        if c == 0:
                            keep(t + 1, 0)
                        if c + 2 < CHUNKS:
                            exp(t, c + 2, first)
                        if c + 1 < CHUNKS:
                            keep(t + 1, c + 1)

                tile(0, True)
                with act.Fori(1, TT - 1) as t:
                    tile(t, False)
                for c in range(CHUNKS):
                    exp(TT - 1, c)
                act.wait_ge(out_turned, 2)
                nc.scalar.activation(attended_t[:, BANK:T], ps_turn[1][:, :], ACT.Copy).then_inc(attended_t_ready[1], 1)

            @block.vector
            def _(dve):
                dve.sem_inc(probs_t_ready, 1)
                dve.sem_inc(attended_ready, 1)

                def rest_gate(n, b, at, w):
                    dve.wait_ge(gate_rounded, n + 1)
                    nc.vector.scalar_tensor_tensor(gate_lo[:, at], ps_gate[b][:, 0:w], b_gate[:, :],
                                                   gate_hi[:, at].bitcast(F32), ALU.add, ALU.subtract)\
                        .then_inc(gate_done, 1)

                def top(t, c):
                    w, at = width(c), slice(c * BANK, c * BANK + width(c))
                    dve.wait_ge(scores_kept, t * CHUNKS + c + 1)
                    nc.vector.tensor_reduce(chunk_max[:, c:c + 1], scores[:, at], AX, ALU.max)\
                        .then_inc(chunk_max_ready, 1)

                def top_of_all(t):
                    dve.wait_ge(chunk_max_ready, t * CHUNKS + CHUNKS)
                    nc.vector.tensor_reduce(neg_max[:, :], chunk_max[:, :], AX, ALU.max, negate=True)\
                        .then_inc(max_ready, 1)

                def query(t, first=False):
                    if not first:
                        dve.wait_ge(scores_ready, t * CHUNKS)
                    at = slice(0, P) if first else bass.ds(t * P, P)
                    nc.vector.tensor_copy(q_hi[:, :], xn_hi[:, at].bitcast(F32))
                    nc.vector.tensor_copy(q_lo[:, :], xn_lo[:, at].bitcast(F32)).then_inc(q_ready, 1)

                def copy_turned(t, c):
                    dve.wait_ge(turned, t * CHUNKS + c + 1)
                    w = tiles(c) * P
                    nc.vector.tensor_copy(probs_t[c % 2][:, 0:w], ps_turn[c % 2][:, 0:w]).then_inc(probs_t_ready, 1)

                def invert(t):
                    dve.wait_ge(exp_done, t * CHUNKS + CHUNKS)
                    nc.vector.tensor_reduce(den[:, :], chunk_den[:, :], AX, ALU.add).then_inc(den_ready, 1)
                    dve.wait_ge(den_ready, t + 1)
                    nc.vector.reciprocal(inv_den[:, :], den[:, :]).then_inc(inv_ready, 1)

                def normalise(t, at):
                    dve.wait_ge(pv_done, t + 1)
                    dve.wait_ge(inv_ready, t + 1)
                    nc.vector.tensor_scalar(attended[:, at, :], ps_out[:, :].unsqueeze(1), inv_den[:, :], None,
                                            ALU.mult)\
                        .then_inc(attended_ready, 1)

                norm.vector(dve)
                norm.wait_turned(dve)
                dve.wait_ge(split_hi, 1)
                nc.vector.tensor_tensor(xn_lo[:, :], xn_t[:, :], xn_hi[:, :].bitcast(F32), ALU.subtract)\
                    .then_inc(split_done, 1)
                nc.vector.memset(probs_tail[:, :], 0.0).then_inc(tail_cleared, 1)
                dve.wait_ge(loaded, 64)
                with dve.Fori(0, CHUNKS // GATES) as i:
                    for b in range(GATES):
                        rest_gate(i * GATES + b, b, bass.ds(i * (GATES * BANK) + b * BANK, BANK), BANK)
                rest_gate(CHUNKS - 1, 0, slice((CHUNKS - 1) * BANK, S), TAIL)
                dve.wait_ge(split_done, 1)
                query(0, first=True)
                for c in range(CHUNKS):
                    top(0, c)
                top_of_all(0)
                query(1)

                def tile(t, at):
                    for c in range(CHUNKS):
                        copy_turned(t, c)
                        if c == 0:
                            top(t + 1, 0)
                        if c + 1 < CHUNKS:
                            top(t + 1, c + 1)
                    invert(t)
                    top_of_all(t + 1)
                    normalise(t, at)

                with dve.Fori(0, TT - 2) as t:
                    tile(t, bass.ds(t, 1))
                    query(t + 2)
                tile(TT - 2, slice(TT - 2, TT - 1))
                for c in range(CHUNKS):
                    copy_turned(TT - 1, c)
                invert(TT - 1)
                normalise(TT - 1, slice(TT - 1, TT))
                dve.wait_ge(out_turned, 1)
                nc.vector.tensor_copy(attended_t[:, 0:BANK], ps_turn[0][:, :]).then_inc(attended_t_ready[0], 1)
                for half in range(2):
                    dve.wait_ge(projected, half + 1)
                    cut = slice(half * 4, half * 4 + 4)
                    nc.vector.tensor_tensor(x_res[:, cut, :], x_res[:, cut, :],
                                            ps_proj[half][:, :].rearrange("p (a d) -> p a d", a=4), ALU.add)


def experts(nc, sems, norm_sems, x_res, xn_t, consts, ins):
    E, F = 8, 352
    FT = [(0, P), (P, P), (2 * P, F - 2 * P)]
    UNITS = 2 * len(FT)
    with Phase(nc, sems, "moe") as ph:
        router = ph.sb("router", [P, E])
        w_in = [ph.sb(f"w_in{b}", [P, 2 * F]) for b in range(2)]
        w_hi = [ph.sb(f"w_hi{b}", [P, 2 * F], F32R) for b in range(2)]
        w_lo = [ph.sb(f"w_lo{b}", [P, 2 * F], F32R) for b in range(2)]
        xn_hi = ph.sb("xn_hi", [P, T], F32R)
        xn_lo = ph.sb("xn_lo", [P, T], F32R)
        w_down = [ph.sb(f"w_down{b}", [P, len(FT), D]) for b in range(2)]
        logit_max = ph.sb("logit_max", [P, TT])
        shifted = ph.sb("shifted", [P, TT, E])
        expd = ph.sb("expd", [P, TT, E])
        den = ph.sb("den", [P, TT])
        inv_den = ph.sb("inv_den", [P, TT])
        probs = ph.sb("probs", [P, TT, E])
        best = ph.sb("best", [P, TT, 8])
        best_at = ph.sb("best_at", [P, TT, 8], U32)
        best_at_f = ph.sb("best_at_f", [P, TT, 8])
        pair_sum = ph.sb("pair_sum", [P, TT])
        pair_inv = ph.sb("pair_inv", [P, TT])
        chosen_w = ph.sb("chosen_w", [P, TT, 2])
        hit = [ph.sb(f"hit{k}", [P, TT, E]) for k in range(2)]
        hit_w = [ph.sb(f"hit_w{k}", [P, TT, E]) for k in range(2)]
        expert_w = ph.sb("expert_w", [P, TT, E])
        silu = [ph.sb(f"silu{n}", [P, BANK]) for n in range(2)]
        acts = [[ph.sb(f"acts{b}_{f}", [P, T]) for f in range(len(FT))] for b in range(2)]
        ps_gate = [ph.ps(f"ps_gate{n}", [P, BANK]) for n in range(2)]
        ps_up = [ph.ps(f"ps_up{n}", [P, BANK]) for n in range(2)]
        ps_down = [ph.ps(f"ps_down{n}", [P, BANK]) for n in range(2)]
        ps_router = ph.ps("ps_router", [P, TT * E])
        norm = LayerNorm(ph, norm_sems, 2, x_res, consts["ident"], xn_t, [bank[:, :] for bank in ps_down])
        chain_sem = ph.sem("chain")
        router_loaded = ph.sem("router_loaded")
        in_loaded = [ph.sem(f"in_loaded{b}") for b in range(2)]
        down_loaded = [ph.sem(f"down_loaded{b}") for b in range(2)]
        xn_rounded = ph.sem("xn_rounded")
        xn_split = ph.sem("xn_split")
        w_rounded = ph.sem("w_rounded")
        w_split = ph.sem("w_split")
        logits_ready = ph.sem("logits_ready")
        shifted_ready = ph.sem("shifted_ready")
        exp_done = ph.sem("exp_done")
        gate_ready = ph.sem("gate_ready")
        up_ready = ph.sem("up_ready")
        silu_done = ph.sem("silu_done")
        acts_done = ph.sem("acts_done")
        down_ready = ph.sem("down_ready")
        down_added = ph.sem("down_added")

        def wide(stat, n):
            return stat.unsqueeze(2).to_broadcast([P, TT, n])

        with ph.block() as block:

            @block.sync
            def _(sp):
                sp.dma_start(router[:, :], ins["router"]).then_inc(router_loaded, 16)

                def load(e, b):
                    at = slice(e, e + 1) if isinstance(e, int) else bass.ds(e, 1)
                    sp.dma_start(w_in[b][:, :], ins["w_moe_in"][at].rearrange("a d f -> (a d) f"))\
                        .then_inc(in_loaded[b], 16)

                def load_down(e, b):
                    at = slice(e, e + 1) if isinstance(e, int) else bass.ds(e, 1)
                    sp.dma_start(w_down[b][:, :, :], ins["w_moe_down"][at].rearrange("a f k d -> (a f) k d"))\
                        .then_inc(down_loaded[b], 16)

                for e in range(2):
                    load(e, e)
                    load_down(e, e)

                def load_next(e, b):
                    sp.wait_ge(w_split, e - 1)
                    load(e, b)

                def load_next_down(e, b):
                    sp.wait_ge(down_ready, e * 2 - 2)
                    load_down(e, b)

                load_next(2, 0)
                load_next(3, 1)
                load_next_down(2, 0)
                with sp.Fori(2, E // 2) as i:
                    load_next(i * 2, 0)
                    load_next_down(i * 2 - 1, 1)
                    load_next(i * 2 + 1, 1)
                    load_next_down(i * 2, 0)
                load_next_down(E - 1, 1)

            @block.tensor
            def _(pe):
                def expert_in(e, b):
                    for f, (start, rows) in enumerate(FT):
                        for n in range(2):
                            count = e * UNITS + 2 * f + n
                            first = isinstance(e, int) and count < 2
                            cols = slice(n * BANK, (n + 1) * BANK)

                            def product(out, at):
                                for k, (w, x) in enumerate(((w_hi, xn_hi), (w_hi, xn_lo), (w_lo, xn_hi))):
                                    last = nc.tensor.matmul(out[0:rows, :], w[b][:, at:at + rows], x[:, cols],
                                                            start=(k == 0), stop=(k == 2))
                                return last

                            if not first:
                                pe.wait_ge(silu_done, count - 1)
                            product(ps_gate[n], start).then_inc(gate_ready, 1)
                            if not first:
                                pe.wait_ge(acts_done, count - 1)
                            product(ps_up[n], F + start).then_inc(up_ready, 1)

                def expert_out(e, b):
                    pe.wait_ge(acts_done, e * UNITS + UNITS)
                    for half in range(2):
                        if not (isinstance(e, int) and e == 0):
                            pe.wait_ge(down_added, e * 2 + half - 1)
                        for j in range(4):
                            i = half * 4 + j
                            for f, (_, rows) in enumerate(FT):
                                last = nc.tensor.matmul(ps_down[half][:, j * P:(j + 1) * P],
                                                        acts[b][f][0:rows, i * P:(i + 1) * P],
                                                        w_down[b][0:rows, f, :], start=(f == 0), stop=(f == 2))
                        last.then_inc(down_ready, 1)

                norm.tensor(pe)
                norm.wait_turned(pe)
                pe.wait_ge(router_loaded, 16)
                for i in range(TT):
                    last = nc.tensor.matmul(ps_router[:, i * E:(i + 1) * E], xn_t[:, i * P:(i + 1) * P],
                                            router[:, :], start=True, stop=True)
                last.then_inc(logits_ready, 1)
                pe.wait_ge(xn_split, 1)
                pe.wait_ge(w_split, 1)
                expert_in(0, 0)
                pe.wait_ge(w_split, 2)
                expert_in(1, 1)
                pe.wait_ge(down_loaded[0], 16)
                expert_out(0, 0)
                with pe.Fori(1, E // 2) as i:
                    for b in range(2):
                        pe.wait_ge(w_split, i * 2 + (b + 1))
                        expert_in(i * 2 + b, b)
                        pe.wait_ge(down_loaded[1 - b], i * 16 + 16 * b)
                        expert_out(i * 2 + (b - 1), 1 - b)
                pe.wait_ge(down_loaded[1], E // 2 * 16)
                expert_out(E - 1, 1)

            @block.scalar
            def _(act):
                def round_weights(e, b):
                    count = e // 2 * 16 + 16 if isinstance(e, int) else e
                    act.wait_ge(in_loaded[b], count)
                    nc.scalar.activation(w_hi[b][:, :], w_in[b][:, :], ACT.Copy).then_inc(w_rounded, 1)

                norm.scalar_root(act)
                for e in range(2):
                    round_weights(e, e)
                norm.scalar_keep(act)
                norm.wait_turned(act)
                nc.scalar.activation(xn_hi[:, :], xn_t[:, :], ACT.Copy).then_inc(xn_rounded, 1)
                act.wait_ge(shifted_ready, 1)
                nc.scalar.activation(expd[:, :, :], shifted[:, :, :], ACT.Exp).then_inc(exp_done, 1)

                def gates(e):
                    for f, (_, rows) in enumerate(FT):
                        for n in range(2):
                            count = e * UNITS + 2 * f + n
                            act.wait_ge(gate_ready, count + 1)
                            if not (isinstance(e, int) and count < 2):
                                act.wait_ge(acts_done, count - 1)
                            nc.scalar.activation(silu[n][0:rows, :], ps_gate[n][0:rows, :], ACT.Silu)\
                                .then_inc(silu_done, 1)

                def gates_and_next(e, b, loads):
                    act.wait_ge(up_ready, e * UNITS)
                    round_weights(loads, b)
                    gates(e)

                gates(0)
                gates_and_next(1, 0, 2)
                with act.Fori(1, E // 2 - 1) as i:
                    gates_and_next(i * 2, 1, i * 16 + 16)
                    gates_and_next(i * 2 + 1, 0, i * 16 + 32)
                gates_and_next(E - 2, 1, E - 1)
                gates(E - 1)

            @block.vector
            def _(dve):
                def rest_weights(e, b):
                    dve.wait_ge(w_rounded, e + 1)
                    nc.vector.tensor_tensor(w_lo[b][:, :], w_in[b][:, :], w_hi[b][:, :].bitcast(F32), ALU.subtract)\
                        .then_inc(w_split, 1)

                norm.vector(dve)
                norm.wait_turned(dve)
                dve.wait_ge(xn_rounded, 1)
                nc.vector.tensor_tensor(xn_lo[:, :], xn_t[:, :], xn_hi[:, :].bitcast(F32), ALU.subtract)\
                    .then_inc(xn_split, 1)
                for e in range(2):
                    rest_weights(e, e)
                step = Chain(dve, chain_sem)
                logits = ps_router[:, :].rearrange("p (i e) -> p i e", e=E)
                dve.wait_ge(logits_ready, 1)
                step(nc.vector.tensor_reduce(logit_max[:, :], logits, AX, ALU.max))
                nc.vector.tensor_tensor(shifted[:, :, :], logits, wide(logit_max[:, :], E), ALU.subtract)\
                    .then_inc(shifted_ready, 1)
                dve.wait_ge(exp_done, 1)
                step(nc.vector.tensor_reduce(den[:, :], expd[:, :, :], AX, ALU.add))
                step(nc.vector.reciprocal(inv_den[:, :], den[:, :]))
                step(nc.vector.tensor_tensor(probs[:, :, :], expd[:, :, :], wide(inv_den[:, :], E), ALU.mult))
                for i in range(TT):
                    last = nc.vector.max(best[:, i, :], probs[:, i, :])
                step(last)
                for i in range(TT):
                    last = nc.vector.max_index(best_at[:, i, :], best[:, i, :], probs[:, i, :])
                step(last)
                step(nc.vector.tensor_copy(best_at_f[:, :, :], best_at[:, :, :]))
                step(nc.vector.tensor_tensor(pair_sum[:, :], best[:, :, 0], best[:, :, 1], ALU.add))
                step(nc.vector.reciprocal(pair_inv[:, :], pair_sum[:, :]))
                step(nc.vector.tensor_tensor(chosen_w[:, :, :], best[:, :, 0:2], wide(pair_inv[:, :], 2), ALU.mult))
                places = consts["places"][:, :].unsqueeze(1).to_broadcast([P, TT, E])
                for k in range(2):
                    step(nc.vector.tensor_tensor(hit[k][:, :, :], places, wide(best_at_f[:, :, k], E), ALU.is_equal))
                    step(nc.vector.tensor_tensor(hit_w[k][:, :, :], hit[k][:, :, :], wide(chosen_w[:, :, k], E),
                                                 ALU.mult))
                step(nc.vector.tensor_tensor(expert_w[:, :, :], hit_w[0][:, :, :], hit_w[1][:, :, :], ALU.add))

                def products(e, b):
                    for f, (_, rows) in enumerate(FT):
                        for n in range(2):
                            count = e * UNITS + 2 * f + n
                            dve.wait_ge(up_ready, count + 1)
                            dve.wait_ge(silu_done, count + 1)
                            nc.vector.tensor_tensor(acts[b][f][0:rows, n * BANK:(n + 1) * BANK], ps_up[n][0:rows, :],
                                                    silu[n][0:rows, :], ALU.mult).then_inc(acts_done, 1)

                def add(e):
                    for half in range(2):
                        dve.wait_ge(down_ready, e * 2 + half + 1)
                        for j in range(4):
                            i = half * 4 + j
                            at = slice(e, e + 1) if isinstance(e, int) else bass.ds(e, 1)
                            last = nc.vector.scalar_tensor_tensor(
                                x_res[:, i, :], ps_down[half][:, j * P:(j + 1) * P], expert_w[:, i, at],
                                x_res[:, i, :], ALU.mult, ALU.add)
                        last.then_inc(down_added, 1)

                products(0, 0)
                rest_weights(2, 0)
                products(1, 1)
                with dve.Fori(1, E // 2 - 1) as i:
                    for b in range(2):
                        add(i * 2 + (b - 2))
                        rest_weights(i * 2 + (b + 1), 1 - b)
                        products(i * 2 + b, b)
                add(E - 4)
                rest_weights(E - 1, 1)
                products(E - 2, 0)
                add(E - 3)
                products(E - 1, 1)
                add(E - 2)
                add(E - 1)


def linear_attention(nc, sems, norm_sems, x_res, xn_t, xn_tok, consts, ins):
    R = 64
    W = HEADS * D
    TWOS = HEADS // 2
    scale = float(R) ** -0.5
    with Phase(nc, sems, "la") as ph:
        w_v = ph.sb("w_v", [R, HEADS, D])
        w_o = ph.sb("w_o", [R, HEADS, D])
        w_q = ph.sb("w_q", [P, TWOS, D])
        w_k = ph.sb("w_k", [P, HEADS * R])
        b_v = ph.sb("b_v", [R, HEADS])
        b_q = ph.sb("b_q", [P, TWOS])
        b_k = ph.sb("b_k", [P, TWOS])
        b_o = ph.sb("b_o", [P, D])
        gram = ph.sb("gram", [P, D])
        s_col = ph.sb("s_col", [P, 1])
        c_all = ph.sb("c_all", [P, W])
        vw = ph.sb("vw", [P, W])
        z = ph.sb("z", [P, W])
        z0 = ph.sb("z0", [P, TWOS, D])
        n_all = ph.sb("n_all", [P, TWOS, D])
        m_mat = ph.sb("m_mat", [P, D])
        b_all = ph.sb("b_all", [P, D])
        ps_w = ph.ps("ps_w", [P, W])
        ps_r = ph.ps("ps_r", [P, W])
        norm = LayerNorm(ph, norm_sems, 3, x_res, consts["ident"], xn_t,
                         [ps_r[:, b * BANK:(b + 1) * BANK] for b in range(2)], xn_tok)
        loaded = ph.sem("loaded")
        gram_ready = ph.sem("gram_ready")
        gram_kept = ph.sem("gram_kept")
        c_ready = ph.sem("c_ready")
        c_kept = ph.sem("c_kept")
        vw_ready = ph.sem("vw_ready")
        vw_kept = ph.sem("vw_kept")
        z_ready = ph.sem("z_ready")
        z_kept = ph.sem("z_kept")
        z0_ready = ph.sem("z0_ready")
        z0_kept = ph.sem("z0_kept")
        n_ready = ph.sem("n_ready")
        n_kept = ph.sem("n_kept")
        m_ready = ph.sem("m_ready")
        m_kept = ph.sem("m_kept")
        b_ready = ph.sem("b_ready")
        bias_step = ph.sem("bias_step")
        out_ready = ph.sem("out_ready")
        CUTS = W // BANK

        with ph.block() as block:

            @block.sync
            def _(sp):
                for name, tile in (("w_la_v", w_v), ("w_la_o", w_o), ("w_la_q", w_q)):
                    sp.dma_start(tile[:, :, :], ins[name]).then_inc(loaded, 16)
                for name, tile in (("w_la_k", w_k), ("b_la_v", b_v), ("b_la_q", b_q), ("b_la_k", b_k)):
                    sp.dma_start(tile[:, :], ins[name]).then_inc(loaded, 16)
                sp.dma_start(b_o[:, :], ins["b_la_o"].to_broadcast([P, D])).then_inc(loaded, 16)

            @block.tensor
            def _(pe):
                ones = consts["ones"]
                pe.wait_ge(loaded, 8 * 16)
                for h in range(HEADS):
                    last = nc.tensor.matmul(ps_r[:, h * D:(h + 1) * D], b_v[:, h:h + 1].to_broadcast([R, P]),
                                            w_o[:, h, :], start=True, stop=True)
                last.then_inc(c_ready, 1)
                for h in range(HEADS):
                    last = nc.tensor.matmul(ps_w[:, h * D:(h + 1) * D], w_v[:, h, :], w_o[:, h, :],
                                            start=True, stop=True)
                last.then_inc(vw_ready, 1)
                pe.wait_ge(c_kept, 1)
                norm.tensor(pe)
                for i in range(TT):
                    nc.tensor.matmul(ps_r[:, 2 * BANK:2 * BANK + D], xn_tok[:, i, :], xn_tok[:, i, :],
                                     start=(i == 0), stop=(i == TT - 1))
                for i in range(TT):
                    last = nc.tensor.matmul(ps_r[:, 3 * BANK:3 * BANK + 1], xn_tok[:, i, :], ones[:, 0:1],
                                            start=(i == 0), stop=(i == TT - 1))
                last.then_inc(gram_ready, 1)
                pe.wait_ge(gram_kept, 1)
                pe.wait_ge(vw_kept, 1)
                norm.wait_turned(pe)
                for c in range(CUTS):
                    cut = slice(c * BANK, (c + 1) * BANK)
                    nc.tensor.matmul(ps_w[:, cut], gram[:, :], vw[:, cut], start=True, stop=True).then_inc(z_ready, 1)
                for c in range(CUTS):
                    cut = slice(c * BANK, (c + 1) * BANK)
                    last = nc.tensor.matmul(ps_r[:, cut], s_col[:, :].to_broadcast([P, P]), vw[:, cut],
                                            start=True, stop=True)
                last.then_inc(z0_ready, 1)
                for h in range(HEADS):
                    if h == 0:
                        pe.wait_ge(z_kept, CUTS)
                    rows = slice(h % 2 * R, h % 2 * R + R)
                    last = nc.tensor.matmul(ps_w[rows, h // 2 * D:(h // 2 + 1) * D], w_k[:, h * R:(h + 1) * R],
                                            z[:, h * D:(h + 1) * D], start=True, stop=True)
                    if h % 2:
                        last.then_inc(n_ready, 1)
                pe.wait_ge(z0_kept, 2)
                for k in range(TWOS):
                    pe.wait_ge(n_kept, k + 1)
                    last = nc.tensor.matmul(ps_r[:, 0:D], w_q[:, k, :], n_all[:, k, :],
                                            start=(k == 0), stop=(k == TWOS - 1))
                last.then_inc(m_ready, 1)
                for k in range(TWOS):
                    last = nc.tensor.matmul(ps_r[:, BANK:BANK + D], b_q[:, k:k + 1].to_broadcast([P, P]),
                                            n_all[:, k, :], start=(k == 0), stop=(k == TWOS - 1))
                last.then_inc(b_ready, 1)
                pe.wait_ge(m_kept, 1)
                for i in range(TT):
                    last = nc.tensor.matmul(ps_w[:, i * D:(i + 1) * D], xn_t[:, i * P:(i + 1) * P], m_mat[:, :],
                                            start=True, stop=True)
                last.then_inc(out_ready, 1)

            @block.scalar
            def _(act):
                norm.scalar_root(act)
                act.wait_ge(c_ready, 1)
                nc.scalar.activation(c_all[:, :], ps_r[:, :], ACT.Copy).then_inc(c_kept, 1)
                act.wait_ge(vw_ready, 1)
                nc.scalar.activation(vw[:, :], ps_w[:, :], ACT.Copy).then_inc(vw_kept, 1)
                norm.scalar_keep(act)
                act.wait_ge(m_ready, 1)
                nc.scalar.activation(m_mat[:, :], ps_r[:, 0:D], ACT.Copy, scale=scale).then_inc(m_kept, 1)

            @block.vector
            def _(dve):
                norm.vector(dve)
                dve.wait_ge(gram_ready, 1)
                nc.vector.tensor_copy(gram[:, :], ps_r[:, 2 * BANK:2 * BANK + D])
                nc.vector.tensor_copy(s_col[:, :], ps_r[:, 3 * BANK:3 * BANK + 1]).then_inc(gram_kept, 1)
                dve.wait_ge(c_kept, 1)
                dve.wait_ge(gram_kept, 1)
                for c in range(CUTS):
                    cut = slice(c * BANK, (c + 1) * BANK)
                    dve.wait_ge(z_ready, c + 1)
                    nc.vector.scalar_tensor_tensor(z[:, cut], c_all[:, cut], s_col[:, :], ps_w[:, cut],
                                                   ALU.mult, ALU.add).then_inc(z_kept, 1)
                dve.wait_ge(z0_ready, 1)
                for half in range(2):
                    rows = slice(half * R, half * R + R)
                    own = lambda tile: tile[rows, :].rearrange("p (k h d) -> p k h d", h=2, d=D)[:, :, half, :]
                    nc.vector.scalar_tensor_tensor(z0[rows, :, :], own(c_all), float(T), own(ps_r),
                                                   ALU.mult, ALU.add).then_inc(z0_kept, 1)
                dve.wait_ge(z0_kept, 2)
                for k in range(TWOS):
                    dve.wait_ge(n_ready, (k // 4 + 1) * 4)
                    nc.vector.scalar_tensor_tensor(n_all[:, k, :], z0[:, k, :], b_k[:, k:k + 1],
                                                   ps_w[:, k * D:(k + 1) * D], ALU.mult, ALU.add).then_inc(n_kept, 1)
                dve.wait_ge(b_ready, 1)
                nc.vector.scalar_tensor_tensor(b_all[:, :], ps_r[:, BANK:BANK + D], scale, b_o[:, :],
                                               ALU.mult, ALU.add).then_inc(bias_step, 1)
                dve.wait_ge(bias_step, 1)
                nc.vector.tensor_tensor(x_res[:, :, :], x_res[:, :, :],
                                        b_all[:, :].unsqueeze(1).to_broadcast([P, TT, D]), ALU.add)\
                    .then_inc(bias_step, 1)
                dve.wait_ge(bias_step, 2)
                dve.wait_ge(out_ready, 1)
                nc.vector.tensor_tensor(x_res[:, :, :], x_res[:, :, :],
                                        ps_w[:, 0:TT * D].rearrange("p (i d) -> p i d", d=D), ALU.add)


def cross_attention_1(nc, sems, norm_sems, x_res, xn_t, consts, ins):
    G, GH, HD, ROWS = 4, 4, 8, 32
    VC = HD + 1
    UNROLL = 3
    ROUNDS = KT // UNROLL
    LAG = 2
    PAIRS = 2 * G
    assert KT % UNROLL == 0
    CHUNKS = ROUNDS
    CH = UNROLL * P
    LAST = S - (KT - 1) * P
    scale = float(D) ** -0.5
    E_RING, M_RING, P_RING, Q_RING = 3, 2, 6, 3
    with Phase(nc, sems, "ca1") as outer:
        q_heads = [outer.sb(f"q_heads{g}", [P, T], F32R) for g in range(G)]
        w_o = outer.sb("w_o", [P, D])
        w_o_loaded = outer.sem("w_o_loaded")
        with Phase(nc, sems, "ca1s") as ph:
            keys = ph.sb("keys", [P, G, KT * P], F32R)
            values = ph.sb("values", [P, KT * HEADS * VC])
            values4 = values[:, :].rearrange("p (k h c) -> p k h c", h=HEADS, c=VC)

            q_diag = [ph.sb(f"q_diag{b}", [P, GH, BANK], F32R) for b in range(Q_RING)]
            neg_max = ph.sb("neg_max", [P, P])
            cleared = ph.sem("cleared")
            q_placed = ph.sem("q_placed")

            def put_on_diagonal(pool, p):
                for j in range(GH):
                    rows = slice(j * ROWS, (j + 1) * ROWS)
                    pool.dma_start(q_diag[p % Q_RING][rows, j, :].bitcast(F32),
                                   q_heads[p // 2][rows, p % 2 * BANK:(p % 2 + 1) * BANK].bitcast(F32))\
                        .then_inc(q_placed, 16)

            with Phase(nc, sems, "ca1k") as kp:
                w_q = kp.sb("w_q", [P, G, P])
                w_k = kp.sb("w_k", [P, G, P])
                w_v = kp.sb("w_v", [P, D])
                ctx = [kp.sb(f"ctx{b}", [P, CH]) for b in range(2)]
                rounded = [kp.sb(f"rounded{g}", [P, BANK], F32R) for g in range(G)]
                ps_k = [kp.ps(f"ps_k{g}", [P, BANK]) for g in range(G)]
                ps_v = [kp.ps(f"ps_v{b}", [P, UNROLL * P]) for b in range(2)]
                ps_turn = [kp.ps(f"ps_turn{b}", [P, BANK]) for b in range(2)]
                norm = LayerNorm(kp, norm_sems, 4, x_res, consts["ident"], xn_t, [bank[:, :] for bank in ps_turn])
                w_loaded = kp.sem("w_loaded")
                ctx_loaded = [kp.sem(f"ctx_loaded{b}") for b in range(2)]
                values_set = kp.sem("values_set")
                k_ready = kp.sem("k_ready")
                k_rounded = kp.sem("k_rounded")
                k_done = kp.sem("k_done")
                v_ready = kp.sem("v_ready")
                v_done = kp.sem("v_done")
                with ph.block() as block:

                    @block.sync
                    def _(sp):
                        sp.dma_start(w_q[:, :, :], ins["w_ca1_q"]).then_inc(w_loaded, 16)
                        sp.dma_start(w_k[:, :, :], ins["w_ca1_k"]).then_inc(w_loaded, 16)
                        sp.dma_start(w_v[:, :], ins["w_ca1_v"]).then_inc(w_loaded, 16)
                        sp.dma_start(w_o[:, :], ins["w_ca1_o"]).then_inc(w_o_loaded, 16)

                        def load(b, at):
                            sp.dma_start(ctx[b][:, :], ins["ctx_t"][:, at]).then_inc(ctx_loaded[b], 16)

                        for b in range(2):
                            load(b, slice(b * CH, (b + 1) * CH))
                        with sp.Fori(1, CHUNKS // 2) as i:
                            for b in range(2):
                                sp.wait_ge(v_ready, i * 2 + (b - 1))
                                load(b, bass.ds(i * (2 * CH) + b * CH, CH))
                        sp.wait_ge(v_ready, CHUNKS - 2)
                        load(0, slice((CHUNKS - 1) * CH, CHUNKS * CH))

                    @block.gpsimd
                    def _(pool):
                        nc.gpsimd.memset(values4[:, KT - 1, :, :], 0.0).then_inc(values_set, 1)
                        nc.gpsimd.memset(values4[:, 0:KT - 1, :, HD], 1.0).then_inc(values_set, 1)
                        pool.wait_ge(values_set, 2)
                        nc.gpsimd.memset(values4[0:LAST, KT - 1, :, HD], 1.0).then_inc(values_set, 1)
                        for b in range(Q_RING):
                            nc.gpsimd.memset(q_diag[b][:, :, :].bitcast(F32), 0.0)
                        nc.gpsimd.memset(neg_max[:, :], 0.0).then_inc(cleared, 1)
                        pool.wait_ge(cleared, 1)
                        for p in range(2):
                            pool.wait_ge(k_done, p + 1)
                            put_on_diagonal(pool, p)

                    @block.tensor
                    def _(pe):
                        def chunk(c, b, first=False):
                            for g in range(G):
                                pe.wait_ge(k_done, c * G + (PAIRS + g - (G - 1)))
                                nc.tensor.matmul(ps_k[g][:, 0:CH], w_k[:, g, :], ctx[b][:, :], start=True, stop=True)\
                                    .then_inc(k_ready, 1)
                            if not first:
                                pe.wait_ge(v_done, c - 1)
                            for j in range(UNROLL):
                                last = nc.tensor.matmul(ps_v[b][:, j * P:(j + 1) * P], ctx[b][:, j * P:(j + 1) * P],
                                                        w_v[:, :], start=True, stop=True)
                            last.then_inc(v_ready, 1)

                        norm.tensor(pe)
                        norm.wait_turned(pe)
                        pe.wait_ge(w_loaded, 48)
                        for p in range(PAIRS):
                            if p >= G:
                                pe.wait_ge(k_done, p - G + 1)
                            nc.tensor.matmul(ps_k[p % G][:, :], w_q[:, p // 2, :],
                                             xn_t[:, p % 2 * BANK:(p % 2 + 1) * BANK], start=True, stop=True)\
                                .then_inc(k_ready, 1)
                        for b in range(2):
                            pe.wait_ge(ctx_loaded[b], 16)
                            chunk(b, b, first=True)
                        with pe.Fori(1, CHUNKS // 2) as i:
                            for b in range(2):
                                pe.wait_ge(ctx_loaded[b], i * 16 + 16)
                                chunk(i * 2 + b, b)
                        pe.wait_ge(ctx_loaded[0], (CHUNKS // 2 + 1) * 16)
                        chunk(CHUNKS - 1, 0)

                    @block.scalar
                    def _(act):
                        norm.scalar_root(act)
                        norm.scalar_keep(act)
                        for p in range(PAIRS):
                            act.wait_ge(k_ready, p + 1)
                            if p >= G:
                                act.wait_ge(k_done, p - G + 1)
                            nc.scalar.activation(rounded[p % G][:, :], ps_k[p % G][:, :], ACT.Copy)\
                                .then_inc(k_rounded, 1)
                        with act.Fori(0, CHUNKS) as c:
                            for g in range(G):
                                act.wait_ge(k_ready, c * G + (PAIRS + g + 1))
                                nc.scalar.activation(rounded[g][:, 0:CH], ps_k[g][:, 0:CH], ACT.Identity,
                                                     bias=consts["masks"][:, 3:4]).then_inc(k_rounded, 1)

                    @block.vector
                    def _(dve):
                        def chunk(c, b, tail=False):
                            at = bass.ds(c * CH, CH) if not isinstance(c, int) else slice(c * CH, (c + 1) * CH)
                            for g in range(G):
                                dve.wait_ge(k_rounded, c * G + (PAIRS + g + 1))
                                nc.vector.scalar_tensor_tensor(
                                    keys[:, g, at], rounded[g][:, 0:CH].bitcast(F32), consts["masks"][:, 2:3],
                                    ps_k[g][:, 0:CH], ALU.mult, ALU.add).then_inc(k_done, 1)
                            dve.wait_ge(v_ready, c + 1)
                            split = ps_v[b][:, :].rearrange("p (k h c) -> p k h c", k=UNROLL, c=HD)
                            if tail:
                                nc.vector.tensor_copy(values4[:, KT - UNROLL:KT - 1, :, 0:HD], split[:, 0:UNROLL - 1])
                                nc.vector.tensor_copy(values4[0:LAST, KT - 1, :, 0:HD], split[0:LAST, UNROLL - 1])
                            else:
                                wide = values[:, bass.ds(c * (UNROLL * HEADS * VC), UNROLL * HEADS * VC)]
                                nc.vector.tensor_copy(
                                    wide.rearrange("p (k h c) -> p k h c", h=HEADS, c=VC)[:, :, :, 0:HD], split)\
                                    .then_inc(v_done, 1)

                        norm.vector(dve)
                        for p in range(PAIRS):
                            dve.wait_ge(k_rounded, p + 1)
                            nc.vector.scalar_tensor_tensor(
                                q_heads[p // 2][:, p % 2 * BANK:(p % 2 + 1) * BANK],
                                rounded[p % G][:, :].bitcast(F32), consts["masks"][:, 1:2], ps_k[p % G][:, :],
                                ALU.mult, ALU.add).then_inc(k_done, 1)
                        with dve.Fori(0, CHUNKS // 2) as i:
                            for b in range(2):
                                chunk(i * 2 + b, b)
                        dve.wait_ge(values_set, 3)
                        chunk(CHUNKS - 1, 0, tail=True)

            run_max = ph.sb("run_max", [P, GH, BANK])
            key_tile = [ph.sb(f"key_tile{s}", [P, P], F32R) for s in range(UNROLL)]
            max_key_tile = [ph.sb(f"max_key_tile{s}", [P, P], F32R) for s in range(UNROLL)]
            value_tile = [ph.sb(f"value_tile{s}", [P, GH * VC]) for s in range(UNROLL)]
            probs = [ph.sb(f"probs{r}", [P, BANK]) for r in range(P_RING)]
            max_hi = ph.sb("max_hi", [GH * 4, P], F32R)
            max_lo = ph.sb("max_lo", [GH * 4, P], F32R)
            banks = ph.ps("banks", [P, 8, BANK])
            ps_m = [banks[:, 2 * r:2 * r + 2, :] for r in range(M_RING)]
            ps_e = [banks[:, 2 * M_RING + r, :] for r in range(E_RING)]
            ps_o = banks[:, 7, :]
            sums_cleared = ph.sem("sums_cleared")
            key_loaded = [ph.sem(f"key_loaded{s}") for s in range(UNROLL)]
            max_key_loaded = [ph.sem(f"max_key_loaded{s}") for s in range(UNROLL)]
            value_loaded = [ph.sem(f"value_loaded{s}") for s in range(UNROLL)]
            e_ready = ph.sem("e_ready")
            m_ready = ph.sem("m_ready")
            exp_done = ph.sem("exp_done")
            max_done = ph.sem("max_done")
            pv_done = ph.sem("pv_done")
            run_turned = ph.sem("run_turned")
            max_found = ph.sem("max_found")
            max_turned = ph.sem("max_turned")
            hi_ready = ph.sem("hi_ready")
            max_split = ph.sem("max_split")
            max_placed = ph.sem("max_placed")
            heads_kept = ph.sem("heads_kept")

            def wait(engine, sem, count):
                if not isinstance(count, int) or count > 0:
                    engine.wait_ge(sem, count)

            def max_slot(m, s, half):
                n = (2 * s + half) % (M_RING + 1 if m == 0 else M_RING)
                return banks[:, 2 * n:2 * n + 2, :]

            WIDE_E, WIDE_P = 6, 12

            def score_bank(e, s, j):
                n = (GH * s + j) % (WIDE_E if e == PAIRS - 1 else E_RING)
                return ps_e[n] if n < E_RING else ps_m[(n - E_RING) // 2][:, (n - E_RING) % 2, :]

            def prob_slot(e, s, j):
                n = (GH * s + j) % (WIDE_P if e == PAIRS - 1 else P_RING)
                if n < P_RING:
                    return probs[n][:, :]
                if n < P_RING + GH:
                    return run_max[:, n - P_RING, :]
                return xn_t[:, (n - P_RING - GH) * BANK:(n - P_RING - GH + 1) * BANK]

            def ring(e, r, n, narrow, wide):
                return wide if e == PAIRS - 1 and not (isinstance(r, int) and r == 0 and n < narrow) else narrow

            def parts(w):
                head = (w - 2 if w >= 2 else None, ROUNDS - LAG, range(0, LAG))
                body = (w - 1 if 1 <= w <= PAIRS else None, 0, range(LAG, ROUNDS))
                return head, body

            def rounds(engine, w, part, step):
                e, e_start, span = part
                m = w if w < PAIRS else None
                if e is None and m is None:
                    return
                step(e, e_start, m, span[0])
                with engine.Fori(1, len(span)) as i:
                    step(e, i + e_start, m, i + span[0])

            with ph.block() as block:

                @block.sync
                def _(sp):
                    def step(e, er, m, mr):
                        for s in range(UNROLL):
                            def tiles(r):
                                at = r * (UNROLL * P) + s * P
                                return slice(at, at + P) if isinstance(at, int) else bass.ds(at, P)

                            if m is not None:
                                wait(sp, m_ready, mr * (UNROLL * 2) + (m * (KT * 2) + 2 * (s + 1 - UNROLL)))
                                sp.dma_start(max_key_tile[s][:, :].bitcast(F32),
                                             keys[:, m // 2, tiles(mr)].bitcast(F32))\
                                    .then_inc(max_key_loaded[s], 16)
                            if e is not None:
                                wait(sp, e_ready, er * (UNROLL * GH) + (e * (KT * GH) + GH * (s + 1 - UNROLL)))
                                sp.dma_start(key_tile[s][:, :].bitcast(F32), keys[:, e // 2, tiles(er)].bitcast(F32))\
                                    .then_inc(key_loaded[s], 16)
                                wait(sp, pv_done, er * UNROLL + (e * KT + (s + 1 - UNROLL)))
                                at = er * (UNROLL * HEADS * VC) + (e // 2 * (GH * VC) + s * HEADS * VC)
                                at = slice(at, at + GH * VC) if isinstance(at, int) else bass.ds(at, GH * VC)
                                sp.dma_start(value_tile[s][:, :], values[:, at]).then_inc(value_loaded[s], 16)

                    for w in range(PAIRS + 2):
                        for part in parts(w):
                            rounds(sp, w, part, step)

                @block.gpsimd
                def _(pool):
                    def place_queries(p):
                        wait(pool, e_ready, (p - Q_RING + 1) * (KT * GH))
                        put_on_diagonal(pool, p)

                    def place_maxima(p):
                        pool.wait_ge(max_split, p + 1)
                        for j in range(GH):
                            for r, part in enumerate((max_hi, max_lo)):
                                row = j * ROWS + 3 * HD + r
                                pool.dma_start(
                                    q_diag[p % Q_RING][row:row + 1, j, :].bitcast(F32)
                                    .rearrange("p (a q) -> p a q", q=P),
                                    part[j * 4:(j + 1) * 4, :].bitcast(F32)).then_inc(max_placed, 16)

                    for w in range(1, PAIRS + 1):
                        place_maxima(w - 1)
                        if w + 1 < PAIRS:
                            place_queries(w + 1)

                @block.tensor
                def _(pe):
                    def weigh(e, a, s, loads, start, stop):
                        pe.wait_ge(exp_done, a * GH + GH)
                        pe.wait_ge(value_loaded[s], loads * 16)
                        for j in range(GH):
                            last = nc.tensor.matmul(ps_o[j * ROWS:j * ROWS + VC, :],
                                                    value_tile[s][:, j * VC:(j + 1) * VC],
                                                    prob_slot(e, s, j), start=start, stop=stop,
                                                    skip_group_check=True)
                        last.then_inc(pv_done, 1)

                    def weigh_before(e, er, s):
                        a = er * UNROLL + (e * KT + s - 1)
                        r = er + e * ROUNDS + (1 if s else 0)
                        if not isinstance(a, int):
                            weigh(e, a, (s - 1) % UNROLL, r, False, False)
                        elif a >= 0:
                            if a % KT == 0 and a:
                                pe.wait_ge(heads_kept, a // KT)
                            weigh(a // KT, a, (s - 1) % UNROLL, r, a % KT == 0, a % KT == KT - 1)

                    def exp_scores(e, er, s, j):
                        back = ring(e, er, GH * s + j, E_RING, WIDE_E)
                        wait(pe, exp_done, er * (UNROLL * GH) + (e * (KT * GH) + s * GH + j + 1 - back))
                        nc.tensor.matmul(score_bank(e, s, j), key_tile[s][:, :],
                                         q_diag[e % Q_RING][:, j, :], start=True, stop=True).then_inc(e_ready, 1)

                    def max_scores(m, mr, s, j):
                        if j % 2 == 0:
                            back = M_RING + 1 if m == 0 else M_RING
                            wait(pe, max_done, mr * (UNROLL * 2) + (m * (KT * 2) + 2 * s + j // 2 + 1 - back))
                        last = nc.tensor.matmul(max_slot(m, s, j // 2)[:, j % 2, :], max_key_tile[s][:, :],
                                                q_diag[m % Q_RING][:, j, :], start=True, stop=True)
                        if j % 2:
                            last.then_inc(m_ready, 1)

                    def turn_maxima(p, half):
                        pe.wait_ge(max_done, (p + 1) * (KT * 2) - 1 + half)
                        for j in range(2):
                            for i in range(4):
                                last = nc.tensor.transpose(ps_m[half][:, j, i * P:(i + 1) * P],
                                                           run_max[:, half * 2 + j, i * P:(i + 1) * P],
                                                           consts["ident"][:, :])
                        last.then_inc(run_turned, 1)

                    def step(e, er, m, mr):
                        for s in range(UNROLL):
                            if e is not None:
                                pe.wait_ge(key_loaded[s], er * 16 + (e * ROUNDS + 1) * 16)
                            if m is not None:
                                pe.wait_ge(max_key_loaded[s], mr * 16 + (m * ROUNDS + 1) * 16)
                            turning = s == 0 and isinstance(mr, int) and mr == 0 and 0 < window <= PAIRS
                            if turning:
                                if e is not None:
                                    exp_scores(e, er, s, 0)
                                turn_maxima(window - 1, 0)
                                if e is not None:
                                    exp_scores(e, er, s, 1)
                                turn_maxima(window - 1, 1)
                                if e is not None:
                                    weigh_before(e, er, s)
                                    exp_scores(e, er, s, 2)
                                    exp_scores(e, er, s, 3)
                                pe.wait_ge(max_found, window)
                                nc.tensor.transpose(ps_m[1][:, 0, 0:P], neg_max[:, :], consts["ident"][:, :])\
                                    .then_inc(max_turned, 1)
                                if m is not None:
                                    pe.wait_ge(max_split, window)
                                    for j in range(GH):
                                        max_scores(m, mr, s, j)
                                continue
                            for j in range(GH):
                                if e is not None:
                                    exp_scores(e, er, s, j)
                                if m is not None:
                                    max_scores(m, mr, s, j)
                                if e is not None and j == (3 if e == PAIRS - 1 else 1):
                                    weigh_before(e, er, s)

                    pe.wait_ge(sums_cleared, 1)
                    for window in range(PAIRS + 2):
                        if window < PAIRS:
                            pe.wait_ge(q_placed, (window + 1) * 64 if window else 128)
                        head, body = parts(window)
                        rounds(pe, window, head, step)
                        if body[0] is not None:
                            pe.wait_ge(max_placed, (body[0] + 1) * 128)
                        rounds(pe, window, body, step)
                    weigh(PAIRS - 1, PAIRS * KT - 1, UNROLL - 1, PAIRS * ROUNDS, False, True)

                @block.scalar
                def _(act):
                    def step(e, er):
                        for s in range(UNROLL):
                            for j in range(GH):
                                a = er * UNROLL + (e * KT + s)
                                act.wait_ge(e_ready, er * (UNROLL * GH) + (e * (KT * GH) + s * GH + j + 1))
                                back = ring(e, er, GH * s + j, P_RING, WIDE_P)
                                wait(act, pv_done, a + ((j - back) // GH + 1))
                                nc.scalar.activation(prob_slot(e, s, j), score_bank(e, s, j), ACT.Exp, scale=scale)\
                                    .then_inc(exp_done, 1)

                    step(0, 0)
                    with act.Fori(1, (PAIRS - 1) * ROUNDS) as r:
                        step(0, r)
                    act.wait_ge(max_split, PAIRS)
                    step(PAIRS - 1, 0)
                    with act.Fori(1, ROUNDS) as r:
                        step(PAIRS - 1, r)

                @block.vector
                def _(dve):
                    def find_maxima(p):
                        for half in range(2):
                            dve.wait_ge(run_turned, p * 2 + half + 1)
                            last = nc.vector.tensor_reduce(
                                neg_max[:, half * 8:half * 8 + 8],
                                ps_m[half][:, :, :].rearrange("p j (i k) -> p (j i) k", k=P), AX, ALU.max, negate=True)
                        last.then_inc(max_found, 1)
                        dve.wait_ge(max_turned, p + 1)
                        if p:
                            dve.wait_ge(max_placed, p * 128)
                        nc.vector.tensor_copy(max_hi[:, :], ps_m[1][0:GH * 4, 0, 0:P]).then_inc(hi_ready, 1)
                        dve.wait_ge(hi_ready, p + 1)
                        nc.vector.tensor_tensor(max_lo[:, :], ps_m[1][0:GH * 4, 0, 0:P], max_hi[:, :].bitcast(F32),
                                                ALU.subtract).then_inc(max_split, 1)

                    def keep_heads(p):
                        dve.wait_ge(pv_done, p * KT + KT)
                        dve.wait_ge(q_placed, (p + 1) * 64 if p else 128)
                        nc.vector.tensor_copy(q_heads[p // 2][:, p % 2 * BANK:(p % 2 + 1) * BANK].bitcast(F32),
                                              ps_o).then_inc(heads_kept, 1)

                    def step(e, er, m, mr):
                        for s in range(UNROLL):
                            for half in range(2):
                                if m is not None:
                                    b = mr * (UNROLL * 2) + (m * (KT * 2) + 2 * s + half)
                                    dve.wait_ge(m_ready, b + 1)
                                    run = run_max[:, half * 2:half * 2 + 2, :]
                                    if s == 0 and isinstance(mr, int) and mr == 0:
                                        nc.vector.tensor_copy(run, max_slot(m, s, half)).then_inc(max_done, 1)
                                    else:
                                        dve.wait_ge(max_done, b - 1)
                                        nc.vector.tensor_tensor(run, max_slot(m, s, half), run, ALU.max)\
                                            .then_inc(max_done, 1)
                                if s == 0 and half == 0 and isinstance(er, int) and er == 0 and e:
                                    keep_heads(e - 1)

                    dve.wait_ge(cleared, 1)
                    nc.vector.memset(ps_o, 0.0).then_inc(sums_cleared, 1)
                    for w in range(PAIRS + 2):
                        head, body = parts(w)
                        if 1 <= w <= PAIRS:
                            find_maxima(w - 1)
                        if w < PAIRS:
                            rounds(dve, w, head, step)
                            rounds(dve, w, body, step)
                        elif body[0]:
                            keep_heads(body[0] - 1)
                    keep_heads(PAIRS - 1)
        attend_out(nc, sems, x_res, [heads[:, :].bitcast(F32) for heads in q_heads], consts, w_o, w_o_loaded,
                   G, HD, ROWS)


def attend_out(nc, sems, x_res, heads, consts, w_o, w_o_loaded, G, HD, ROWS):
    with Phase(nc, sems, "ao") as ph:
        inv = [ph.sb(f"inv{b}", [P, HEADS]) for b in range(2)]
        normed = [ph.sb(f"normed{b}", [P, HEADS, HD]) for b in range(2)]
        normed_t = [ph.sb(f"normed_t{b}", [P, P]) for b in range(2)]
        ps_turn = [ph.ps(f"ps_turn{b}", [P, BANK]) for b in range(2)]
        ps_back = [ph.ps(f"ps_back{b}", [P, P]) for b in range(2)]
        ps_out = [ph.ps(f"ps_out{b}", [P, D]) for b in range(2)]
        turned = ph.sem("turned")
        inv_ready = ph.sem("inv_ready")
        normed_ready = ph.sem("normed_ready")
        back_ready = ph.sem("back_ready")
        back_kept = ph.sem("back_kept")
        out_ready = ph.sem("out_ready")
        out_added = ph.sem("out_added")
        with ph.block() as block:

            @block.tensor
            def _(pe):
                def turn(i):
                    if i >= 2:
                        pe.wait_ge(normed_ready, i - 1)
                    for g in range(G):
                        last = nc.tensor.transpose(ps_turn[i % 2][:, g * P:(g + 1) * P],
                                                   heads[g][:, i * P:(i + 1) * P], consts["ident"][:, :])
                    last.then_inc(turned, 1)

                pe.wait_ge(w_o_loaded, 16)
                def back(i):
                    pe.wait_ge(normed_ready, i + 1)
                    if i >= 2:
                        pe.wait_ge(back_kept, i - 1)
                    nc.tensor.transpose(ps_back[i % 2][:, :], normed[i % 2][:, :, :].rearrange("p h c -> p (h c)"),
                                        consts["ident"][:, :]).then_inc(back_ready, 1)

                turn(0)
                turn(1)
                back(0)
                for i in range(TT):
                    if i + 2 < TT:
                        turn(i + 2)
                    if i + 1 < TT:
                        back(i + 1)
                    pe.wait_ge(back_kept, i + 1)
                    if i >= 2:
                        pe.wait_ge(out_added, i - 1)
                    nc.tensor.matmul(ps_out[i % 2][:, :], normed_t[i % 2][:, :], w_o[:, :], start=True, stop=True)\
                        .then_inc(out_ready, 1)

            @block.scalar
            def _(act):
                for i in range(TT):
                    act.wait_ge(back_ready, i + 1)
                    if i >= 2:
                        act.wait_ge(out_ready, i - 1)
                    nc.scalar.activation(normed_t[i % 2][:, :], ps_back[i % 2][:, :], ACT.Copy).then_inc(back_kept, 1)

            @block.vector
            def _(dve):
                for i in range(TT + 1):
                    if i < TT:
                        dve.wait_ge(turned, i + 1)
                        by_head = ps_turn[i % 2][:, :].rearrange("p (h r) -> p h r", r=ROWS)
                        nc.vector.reciprocal(inv[i % 2][:, :], by_head[:, :, HD]).then_inc(inv_ready, 1)
                        dve.wait_ge(inv_ready, i + 1)
                        if i >= 2:
                            dve.wait_ge(back_ready, i - 1)
                        nc.vector.tensor_tensor(normed[i % 2][:, :, :], by_head[:, :, 0:HD],
                                                inv[i % 2][:, :].unsqueeze(2).to_broadcast([P, HEADS, HD]), ALU.mult)\
                            .then_inc(normed_ready, 1)
                    if i:
                        dve.wait_ge(out_ready, i)
                        nc.vector.tensor_tensor(x_res[:, i - 1, :], x_res[:, i - 1, :], ps_out[(i - 1) % 2][:, :],
                                                ALU.add).then_inc(out_added, 1)


def bit_linear_ffn(nc, sems, norm_sems, x_res, xn_tok, consts, ins):
    H = 512
    HC = H // P
    ROUND = WHOLE
    with Phase(nc, sems, "bl") as ph:
        w1 = ph.sb("w1", [P, H])
        w2 = ph.sb("w2", [P, HC, D])
        b1 = ph.sb("b1", [P, H])
        b2 = ph.sb("b2", [P, D])
        w1_t = ph.sb("w1_t", [P, H], BF16)
        w2_t = ph.sb("w2_t", [P, HC * D], BF16)
        w_scaled = ph.sb("w_scaled", [P, H])
        w_scaled2 = ph.sb("w_scaled2", [P, HC * D])
        w_whole = ph.sb("w_whole", [P, H])
        w_whole2 = ph.sb("w_whole2", [P, HC * D])
        w_sums = ph.sb("w_sums", [P, 2])
        w_mean = ph.sb("w_mean", [P, 2])
        w_inv = ph.sb("w_inv", [P, 2])
        ident_b = ph.sb("ident_b", [P, P], BF16)
        norm_sq = ph.sb("norm_sq", [P, TT])
        x_scaled = ph.sb("x_scaled", [P, TT, D])
        x_shifted = ph.sb("x_shifted", [P, TT, D])
        x_whole = ph.sb("x_whole", [P, TT, D], BF16)
        x_turned = ph.sb("x_turned", [P, T], BF16)
        hidden_in = [ph.sb(f"hidden_in{b}", [P, H]) for b in range(2)]
        hidden = ph.sb("hidden", [P, TT, H])
        h_squares = ph.sb("h_squares", [P, H])
        h_scaled = [ph.sb(f"h_scaled{b}", [P, H]) for b in range(2)]
        h_shifted = [ph.sb(f"h_shifted{b}", [P, H]) for b in range(2)]
        h_whole = [ph.sb(f"h_whole{b}", [P, H], BF16) for b in range(2)]
        h_turned = [ph.sb(f"h_turned{b}", [P, H], BF16) for b in range(2)]
        summed = [ph.sb(f"summed{b}", [P, D]) for b in range(2)]
        ps_turn = [ph.ps(f"ps_turn{b}", [P, BANK]) for b in range(2)]
        ps_h = [ph.ps(f"ps_h{b}", [P, H]) for b in range(2)]
        ps_out = [ph.ps(f"ps_out{b}", [P, D]) for b in range(2)]
        ps_mean = ph.ps("ps_mean", [P, 2])

        norm = LayerNorm(ph, norm_sems, 5, x_res, consts["ident"], xn_tok=xn_tok)
        loaded = ph.sem("loaded")
        chain_sem = ph.sem("chain")
        w_summed = ph.sem("w_summed")
        means_ready = ph.sem("means_ready")
        var_ready = ph.sem("var_ready")
        std_ready = ph.sem("std_ready")
        w_ready = ph.sem("w_ready")
        x_ready = ph.sem("x_ready")
        turn_ready = ph.sem("turn_ready")
        x_kept = ph.sem("x_kept")
        h_ready = ph.sem("h_ready")
        in_ready = ph.sem("in_ready")
        hidden_ready = ph.sem("hidden_ready")
        squared = ph.sem("squared")
        peaks_ready = ph.sem("peaks_ready")
        gains_ready = ph.sem("gains_ready")
        h_scaled_ready = ph.sem("h_scaled_ready")
        h_whole_ready = ph.sem("h_whole_ready")
        h_kept = ph.sem("h_kept")
        out_ready = ph.sem("out_ready")
        out_added = ph.sem("out_added")

        def stats(name):
            return {k: ph.sb(f"{name}_{k}", [P, TT]) for k in
                    ("sum_sq", "var", "std", "rstd", "sq", "vsq", "corr", "norm", "peak", "top", "clipped", "inv",
                     "step", "gain", "back")}

        x_stats, h_stats = stats("x"), stats("h")

        def wide(stat, width):
            return stat[:, :].unsqueeze(2).to_broadcast([P, TT, width])

        with ph.block() as block:

            @block.sync
            def _(sp):
                sp.dma_start(w1[:, :], ins["w_bl1"]).then_inc(loaded, 16)
                sp.dma_start(w2[:, :, :], ins["w_bl2"]).then_inc(loaded, 16)
                sp.dma_start(b1[:, :], ins["b_bl1"].to_broadcast([P, H])).then_inc(loaded, 16)
                sp.dma_start(b2[:, :], ins["b_bl2"].to_broadcast([P, D])).then_inc(loaded, 16)

            @block.tensor
            def _(pe):
                pe.wait_ge(w_summed, 1)
                nc.tensor.matmul(ps_mean[:, :], consts["ones"][:, :], w_sums[:, :], start=True, stop=True)\
                    .then_inc(means_ready, 1)
                pe.wait_ge(x_ready, 1)
                for i in range(TT):
                    last = nc.tensor.matmul(ps_turn[i // 4][:, i % 4 * P:(i % 4 + 1) * P], x_whole[:, i, :],
                                            ident_b[:, :], start=True, stop=True)
                    if i % 4 == 3:
                        last.then_inc(turn_ready, 1)
                pe.wait_ge(w_ready, 1)
                pe.wait_ge(x_kept, 2)
                for i in range(TT):
                    if i >= 2:
                        pe.wait_ge(in_ready, i - 1)
                    nc.tensor.matmul(ps_h[i % 2][:, :], x_turned[:, i * P:(i + 1) * P], w1_t[:, :],
                                     start=True, stop=True).then_inc(h_ready, 1)

                def turn(i):
                    pe.wait_ge(h_whole_ready, i + 1)
                    if i >= 2:
                        pe.wait_ge(h_kept, i - 1)
                    for c in range(HC):
                        last = nc.tensor.matmul(ps_turn[i % 2][:, c * P:(c + 1) * P],
                                                h_whole[i % 2][:, c * P:(c + 1) * P], ident_b[:, :],
                                                start=True, stop=True)
                    last.then_inc(turn_ready, 1)

                turn(0)
                for i in range(TT):
                    if i + 1 < TT:
                        turn(i + 1)
                    pe.wait_ge(h_kept, i + 1)
                    if i >= 2:
                        pe.wait_ge(out_added, i - 1)
                    for c in range(HC):
                        last = nc.tensor.matmul(ps_out[i % 2][:, :], h_turned[i % 2][:, c * P:(c + 1) * P],
                                                w2_t[:, c * D:(c + 1) * D], start=c == 0, stop=c == HC - 1)
                    last.then_inc(out_ready, 1)

            @block.scalar
            def _(act):
                norm.scalar_root(act)
                act.wait_ge(var_ready, 1)
                nc.scalar.activation(x_stats["std"][:, :], x_stats["var"][:, :], ACT.Sqrt).then_inc(std_ready, 1)
                for b in range(2):
                    act.wait_ge(turn_ready, b + 1)
                    nc.scalar.activation(x_turned[:, b * BANK:(b + 1) * BANK], ps_turn[b][:, :], ACT.Copy)\
                        .then_inc(x_kept, 1)
                for i in range(TT):
                    act.wait_ge(in_ready, i + 1)
                    nc.scalar.activation(hidden[:, i, :], hidden_in[i % 2][:, :], ACT.Gelu).then_inc(hidden_ready, 1)
                    act.wait_ge(hidden_ready, i + 1)
                    if i:
                        act.wait_ge(squared, i)
                    nc.scalar.activation(h_squares[:, :], hidden[:, i, :], ACT.Square,
                                         accum_out=h_stats["sum_sq"][:, i:i + 1]).then_inc(squared, 1)
                act.wait_ge(var_ready, 2)
                nc.scalar.activation(h_stats["std"][:, :], h_stats["var"][:, :], ACT.Sqrt).then_inc(std_ready, 1)

                def scale(i):
                    if i >= 2:
                        act.wait_ge(h_whole_ready, i - 1)
                    nc.scalar.activation(h_scaled[i % 2][:, :], hidden[:, i, :], ACT.Identity,
                                         bias=consts["masks"][:, 4:5], scale=h_stats["gain"][:, i:i + 1])\
                        .then_inc(h_scaled_ready, 1)

                act.wait_ge(gains_ready, 2)
                scale(0)
                scale(1)
                for i in range(TT):
                    act.wait_ge(turn_ready, i + 3)
                    if i >= 2:
                        act.wait_ge(out_ready, i - 1)
                    nc.scalar.activation(h_turned[i % 2][:, :], ps_turn[i % 2][:, :], ACT.Copy).then_inc(h_kept, 1)
                    if i + 2 < TT:
                        scale(i + 2)

            @block.vector
            def _(dve):
                step = Chain(dve, chain_sem)

                def norm_scales(s, width, turn, mean):
                    step(nc.vector.tensor_scalar(s["var"][:, :], s["sum_sq"][:, :], 1.0 / width, 1e-6,
                                                 ALU.mult, ALU.add))
                    nc.vector.tensor_copy(s["corr"][:, :], s["var"][:, :]).then_inc(var_ready, 1)
                    dve.wait_ge(std_ready, turn)
                    dve.wait_ge(var_ready, turn)
                    step(nc.vector.reciprocal(s["rstd"][:, :], s["std"][:, :]))
                    step(nc.vector.tensor_tensor(s["sq"][:, :], s["rstd"][:, :], s["rstd"][:, :], ALU.mult))
                    step(nc.vector.tensor_tensor(s["vsq"][:, :], s["sq"][:, :], s["var"][:, :], ALU.mult))
                    step(nc.vector.tensor_scalar(s["corr"][:, :], s["vsq"][:, :], -0.5, 1.5, ALU.mult, ALU.add))
                    step(nc.vector.tensor_tensor(s["norm"][:, :], s["rstd"][:, :], s["corr"][:, :], ALU.mult))
                    step(nc.vector.tensor_tensor(s["top"][:, :], s["peak"][:, :], s["norm"][:, :], ALU.mult))
                    step(nc.vector.tensor_scalar(s["clipped"][:, :], s["top"][:, :], 1e-5, 1.0 / 127.0,
                                                 ALU.max, ALU.mult))
                    step(nc.vector.reciprocal(s["inv"][:, :], s["clipped"][:, :]))
                    step(nc.vector.tensor_tensor(s["gain"][:, :], s["inv"][:, :], s["norm"][:, :], ALU.mult))
                    nc.vector.tensor_scalar(s["back"][:, :], s["clipped"][:, :], mean, None, ALU.mult)\
                        .then_inc(gains_ready, 1)
                    dve.wait_ge(gains_ready, turn)

                norm.vector(dve)
                norm.wait_normed(dve)
                dve.wait_ge(loaded, 64)
                w2_flat = w2[:, :, :].rearrange("p c d -> p (c d)")
                nc.vector.tensor_reduce(w_sums[:, 0:1], w1[:, :], AX, ALU.add, apply_absolute_value=True)
                nc.vector.tensor_reduce(w_sums[:, 1:2], w2_flat, AX, ALU.add, apply_absolute_value=True)\
                    .then_inc(w_summed, 1)
                nc.vector.tensor_copy(ident_b[:, :], consts["ident"][:, :])
                nc.vector.tensor_reduce(x_stats["peak"][:, :], xn_tok[:, :, :], AX, ALU.max, apply_absolute_value=True)
                step(nc.vector.tensor_tensor(norm_sq[:, :], norm.rstd2[:, :], norm.rstd2[:, :], ALU.mult))
                step(nc.vector.scalar_tensor_tensor(x_stats["sum_sq"][:, :], norm_sq[:, :], float(D),
                                                    norm.moments[:, :, 1], ALU.mult, ALU.mult))
                dve.wait_ge(means_ready, 1)
                step(nc.vector.tensor_scalar(w_mean[:, :], ps_mean[:, :], 1.0 / (H * D), 1e-5, ALU.mult, ALU.max))
                norm_scales(x_stats, D, 1, w_mean[:, 0:1])
                step(nc.vector.tensor_tensor(x_scaled[:, :, :], xn_tok[:, :, :], wide(x_stats["gain"], D), ALU.mult))
                step(nc.vector.tensor_scalar(x_shifted[:, :, :], x_scaled[:, :, :], ROUND, ROUND + 127.0,
                                             ALU.add, ALU.min))
                nc.vector.tensor_scalar(x_whole[:, :, :], x_shifted[:, :, :], ROUND, -128.0,
                                        ALU.subtract, ALU.max).then_inc(x_ready, 1)
                step(nc.vector.reciprocal(w_inv[:, :], w_mean[:, :]))
                nc.vector.tensor_scalar(w_scaled[:, :], w1[:, :], w_inv[:, 0:1], ROUND, ALU.mult, ALU.add)
                step(nc.vector.tensor_scalar(w_scaled2[:, :], w2_flat, w_inv[:, 1:2], ROUND, ALU.mult, ALU.add))
                nc.vector.tensor_scalar(w_whole[:, :], w_scaled[:, :], ROUND, -1.0, ALU.subtract, ALU.max)
                step(nc.vector.tensor_scalar(w_whole2[:, :], w_scaled2[:, :], ROUND, -1.0, ALU.subtract, ALU.max))
                nc.vector.tensor_scalar(w1_t[:, :], w_whole[:, :], 1.0, None, ALU.min)
                nc.vector.tensor_scalar(w2_t[:, :], w_whole2[:, :], 1.0, None, ALU.min).then_inc(w_ready, 1)
                for i in range(TT + 1):
                    if i < TT:
                        dve.wait_ge(h_ready, i + 1)
                        if i >= 2:
                            dve.wait_ge(hidden_ready, i - 1)
                        nc.vector.scalar_tensor_tensor(hidden_in[i % 2][:, :], ps_h[i % 2][:, :],
                                                       x_stats["back"][:, i:i + 1], b1[:, :], ALU.mult, ALU.add)\
                            .then_inc(in_ready, 1)
                    if i:
                        dve.wait_ge(hidden_ready, i)
                        nc.vector.tensor_reduce(h_stats["peak"][:, i - 1:i], hidden[:, i - 1, :], AX, ALU.max,
                                                apply_absolute_value=True).then_inc(peaks_ready, 1)
                dve.wait_ge(squared, TT)
                dve.wait_ge(peaks_ready, TT)
                norm_scales(h_stats, H, 2, w_mean[:, 1:2])

                def add_out(i):
                    dve.wait_ge(out_ready, i + 1)
                    nc.vector.scalar_tensor_tensor(summed[i % 2][:, :], ps_out[i % 2][:, :],
                                                   h_stats["back"][:, i:i + 1], b2[:, :], ALU.mult, ALU.add)\
                        .then_inc(out_added, 1)
                    dve.wait_ge(out_added, i + 1)
                    nc.vector.tensor_tensor(x_res[:, i, :], x_res[:, i, :], summed[i % 2][:, :], ALU.add)

                for i in range(TT):
                    b = i % 2
                    dve.wait_ge(h_scaled_ready, i + 1)
                    step(nc.vector.tensor_scalar(h_shifted[b][:, :], h_scaled[b][:, :], ROUND, -128.0,
                                                 ALU.subtract, ALU.max))
                    if i >= 2:
                        dve.wait_ge(turn_ready, i + 1)
                    nc.vector.tensor_scalar(h_whole[b][:, :], h_shifted[b][:, :], 127.0, None, ALU.min)\
                        .then_inc(h_whole_ready, 1)
                    if i >= 2:
                        add_out(i - 2)
                add_out(TT - 2)
                add_out(TT - 1)


def program(nc, ins, out):
    with ExitStack() as sems, Phase(nc, sems, "main") as ph:
        x_res = ph.sb("x_res", [P, TT, D])
        xn_t = ph.sb("xn_t", [P, T])
        ident = ph.sb("ident", [P, P])
        masks = ph.sb("masks", [P, 8])
        ones = ph.sb("ones", [P, P])
        places = ph.sb("places", [P, 8])
        consts = {"ones": ones, "places": places, "masks": masks, "ident": ident}
        norm_sems = [ph.sem(f"norm_{name}") for name in NORM_SEMS]
        loaded = ph.sem("loaded")
        stored = ph.sem("stored")
        ctx_loaded = ph.sem("ctx_loaded")
        ctx_tok_loaded = ph.sem("ctx_tok_loaded")
        tail_cleared = ph.sem("tail_cleared")
        with Phase(nc, sems, "early") as early:
            ctx_t = early.sb("ctx_t", [P, S])
            ctx_tok = early.sb("ctx_tok", [P, KT, D])

            def load_context(sp):
                sp.dma_start(ctx_t[:, :], ins["ctx_t"][:, 0:S]).then_inc(ctx_loaded, 16)
                sp.dma_start(ctx_tok[:, 0:KT - 1, :],
                             ins["ctx"][0, 0:(KT - 1) * P, :].rearrange("(k p) d -> p k d", p=P))\
                    .then_inc(ctx_tok_loaded, 16)
                sp.wait_ge(tail_cleared, 1)
                sp.dma_start(ctx_tok[0:S - (KT - 1) * P, KT - 1, :], ins["ctx"][0, (KT - 1) * P:S, :])\
                    .then_inc(ctx_tok_loaded, 16)

            with ph.block() as block:

                @block.sync
                def _(sp):
                    sp.dma_start(x_res[:, :, :], ins["x"].rearrange("a (i p) d -> p (a i) d", p=P)).then_inc(loaded, 16)
                    sp.dma_start(ident[:, :], ins["ident"]).then_inc(loaded, 16)
                    sp.dma_start(masks[:, :], ins["masks"]).then_inc(loaded, 16)
                    sp.dma_start(ones[:, :], ins["ones"]).then_inc(loaded, 16)
                    sp.dma_start(places[:, :], ins["places"]).then_inc(loaded, 16)
                    sp.wait_ge(loaded, 80)

                @block.gpsimd
                def _(pool):
                    nc.gpsimd.memset(ctx_tok[:, KT - 1, :], 0.0).then_inc(tail_cleared, 1)

            self_attention_0(nc, sems, norm_sems, x_res, xn_t, ident, masks, ins["w_heads"], load_context)
            cross_attention_0(nc, sems, norm_sems, x_res, xn_t, ident, ones, ctx_t, ctx_tok, ctx_loaded,
                              ctx_tok_loaded, ins)

        experts(nc, sems, norm_sems, x_res, xn_t, consts, ins)
        with Phase(nc, sems, "la_in") as la:
            xn_tok = la.sb("xn_tok", [P, TT, D])
            linear_attention(nc, sems, norm_sems, x_res, xn_t, xn_tok, consts, ins)

        cross_attention_1(nc, sems, norm_sems, x_res, xn_t, consts, ins)
        with Phase(nc, sems, "bl_in") as bl:
            xn_tok = bl.sb("xn_tok", [P, TT, D])
            bit_linear_ffn(nc, sems, norm_sems, x_res, xn_tok, consts, ins)

        with ph.block() as block:

            @block.sync
            def _(sp):
                sp.dma_start(out.rearrange("a (i p) d -> p (a i) d", p=P), x_res[:, :, :]).then_inc(stored, 16)
                sp.wait_ge(stored, 16)


def layouts(np, given):
    a = {"x": given["x"]}
    turn = lambda w: np.transpose(w, (0, 2, 1))
    q, k = turn(given["L0_attn_Q"]), turn(given["L0_attn_K"])
    a["w_heads"] = np.concatenate([q, q, k, k, given["L0_attn_VO"]], axis=2)
    a["ident"] = np.eye(P, dtype=np.float32)
    masks = np.zeros((P, 8), np.float32)
    masks[64:, 0] = -1.0
    for head in range(0, P, 32):
        masks[head + 16:head + 24, 1] = -1.0
        masks[head + 8:head + 16, 2] = -1.0
        masks[head + 24:head + 26, 2] = 1.0
        masks[head + 24:head + 26, 3] = 1.0
    masks[:, 4] = WHOLE
    a["masks"] = masks
    a["ones"] = np.ones((P, P), np.float32)
    a["places"] = np.tile(np.arange(8, dtype=np.float32), (P, 1))
    a["ctx"] = given["ctx_1024"]
    ctx = given["ctx_1024"][0]
    a["ctx_t"] = np.concatenate([ctx, ctx[:KT * P - S]]).T
    a["w_gate"] = given["L0_xattn_Wg"]
    a["b_gate"] = given["L0_xattn_bg"].reshape(D, 1)
    a["w_ca0_out"] = given["L0_xattn_Wo"]
    a["b_ca0_out"] = given["L0_xattn_bo"].reshape(1, D)
    a["router"] = given["L0_ffn_router_w"]
    a["w_moe_in"] = np.concatenate([given["L0_ffn_gate_proj"], given["L0_ffn_up_proj"]], axis=2)
    down = given["L0_ffn_down_proj"]
    padded = np.zeros((down.shape[0], 3 * P, D), np.float32)
    padded[:, :down.shape[1]] = down
    a["w_moe_down"] = padded.reshape(-1, 3, P, D).transpose(0, 2, 1, 3)
    by_head = lambda w: w.reshape(D, HEADS, -1).transpose(2, 1, 0)
    a["w_la_v"] = by_head(given["L1_attn_Wv"])
    twos = lambda w: w.reshape(w.shape[0], HEADS // 2, P).transpose(2, 1, 0)
    a["w_la_q"] = twos(given["L1_attn_Wq"])
    a["w_la_o"] = given["L1_attn_Wo"].reshape(HEADS, -1, D).transpose(1, 0, 2)
    a["w_la_k"] = given["L1_attn_Wk"]
    a["b_la_v"] = given["L1_attn_bv"].reshape(HEADS, -1).T
    a["b_la_q"] = given["L1_attn_bq"].reshape(HEADS // 2, P).T
    a["b_la_k"] = given["L1_attn_bk"].reshape(HEADS // 2, P).T
    a["b_la_o"] = given["L1_attn_bo"].reshape(1, -1)

    def in_rows(w):
        by = w.T.reshape(D, 4, 4, 1, 8)
        return np.concatenate([by, by, by, np.zeros_like(by)], axis=3).reshape(D, 4, P)

    a["w_ca1_q"] = in_rows(given["L1_xattn_Wq"])
    a["w_ca1_k"] = in_rows(given["L1_xattn_Wk"])
    a["w_ca1_v"] = given["L1_xattn_Wv"].T
    a["w_ca1_o"] = given["L1_xattn_Wo"].T
    a["w_bl1"] = given["L1_ffn_w1"].T
    a["w_bl2"] = given["L1_ffn_w2"].T.reshape(-1, P, D).transpose(1, 0, 2)
    a["b_bl1"] = given["L1_ffn_b1"].reshape(1, -1)
    a["b_bl2"] = given["L1_ffn_b2"].reshape(1, -1)
    a["w_bl1"] = given["L1_ffn_w1"].T
    a["w_bl2"] = given["L1_ffn_w2"].T.reshape(-1, P, D).transpose(1, 0, 2)
    a["b_bl1"] = given["L1_ffn_b1"].reshape(1, -1)
    a["b_bl2"] = given["L1_ffn_b2"].reshape(1, -1)
    a["w_bl1"] = given["L1_ffn_w1"].T
    a["w_bl2"] = given["L1_ffn_w2"].T.reshape(-1, P, D).transpose(1, 0, 2)
    a["b_bl1"] = given["L1_ffn_b1"].reshape(1, -1)
    a["b_bl2"] = given["L1_ffn_b2"].reshape(1, -1)
    a["w_bl1"] = given["L1_ffn_w1"].T
    a["w_bl2"] = given["L1_ffn_w2"].T.reshape(-1, P, D).transpose(1, 0, 2)
    a["b_bl1"] = given["L1_ffn_b1"].reshape(1, -1)
    a["b_bl2"] = given["L1_ffn_b2"].reshape(1, -1)
    a["w_bl1"] = given["L1_ffn_w1"].T
    a["w_bl2"] = given["L1_ffn_w2"].T.reshape(-1, P, D).transpose(1, 0, 2)
    a["b_bl1"] = given["L1_ffn_b1"].reshape(1, -1)
    a["b_bl2"] = given["L1_ffn_b2"].reshape(1, -1)
    a["w_bl1"] = given["L1_ffn_w1"].T
    a["w_bl2"] = given["L1_ffn_w2"].T.reshape(-1, P, D).transpose(1, 0, 2)
    a["b_bl1"] = given["L1_ffn_b1"].reshape(1, -1)
    a["b_bl2"] = given["L1_ffn_b2"].reshape(1, -1)
    a["w_bl1"] = given["L1_ffn_w1"].T
    a["w_bl2"] = given["L1_ffn_w2"].T.reshape(-1, P, D).transpose(1, 0, 2)
    a["b_bl1"] = given["L1_ffn_b1"].reshape(1, -1)
    a["b_bl2"] = given["L1_ffn_b2"].reshape(1, -1)
    return a


def kernel(**inputs):
    import numpy as np
    import concourse.bacc as bacc
    from concourse.bass_utils import run_bass_kernel_spmd

    given = {k: np.asarray(v) for k, v in inputs.items()}
    arrays = {f"in_{k}": np.ascontiguousarray(v) for k, v in layouts(np, given).items()}
    nc = bacc.Bacc("TRN2", target_bir_lowering=False, num_devices=1)
    ins = {k[3:]: nc.dram_tensor(k, v.shape, mybir.dt.from_np(v.dtype), kind="ExternalInput").ap()
           for k, v in arrays.items()}
    out = nc.dram_tensor("out_x", (1, T, D), F32, kind="ExternalOutput").ap()
    program(nc, ins, out)
    result = run_bass_kernel_spmd(nc, [arrays], core_ids=[0])
    return result.results[0]["out_x"]
```
